# Optimizing a Trainium2 kernel written in Bass

```python
import numpy as np
import jax
import jax.numpy as jnp

def _softmax(x, axis=-1):
    return jax.nn.softmax(x, axis=axis)

def _gelu(x):
    return jax.nn.gelu(x, approximate=True)

def _silu(x):
    return jax.nn.silu(x)

def _sigmoid(x):
    return jax.nn.sigmoid(x)

def _layernorm(x, axis=-1, eps=1e-05):
    m = jnp.mean(x, axis=axis, keepdims=True)
    v = jnp.var(x, axis=axis, keepdims=True)
    return (x - m) / jnp.sqrt(v + eps)

def _scatter_add(tgt, idx, src, axis=0):
    return tgt.at[idx].add(src)

def _segment_sum(src, seg, n):
    return jax.ops.segment_sum(src, seg, n)
kernel_name = 'mk_gps_d1_gnn_r16_56a22f'

def setup_inputs(seed: int=0):
    np.random.seed(seed)
    _w = jnp.asarray

    def _rec_inputs():
        import jax
        import jax.numpy as jnp
        _gk = jax.random.key(seed)
        x = 7.22e-05 + 1 * jax.random.normal(jax.random.fold_in(_gk, 1), (3125, 256), jnp.float32)
        _s = jax.random.randint(jax.random.fold_in(_gk, 2), (50000,), 0, 3125, jnp.int32)
        _d = jax.random.randint(jax.random.fold_in(_gk, 3), (50000,), 0, 3125, jnp.int32)
        _loop = jnp.arange(3125, dtype=jnp.int32)
        src = jnp.concatenate([_s, _d, _loop])
        dst = jnp.concatenate([_d, _s, _loop])
        _o = jnp.argsort(dst, stable=True)
        src = src[_o]
        dst = dst[_o]
        edge_attr_5 = jax.random.uniform(jax.random.fold_in(_gk, 11), (103125, 5), jnp.float32, 0.0, 99.9996)
        node_type_19 = jax.random.randint(jax.random.fold_in(_gk, 13), (3125,), 0, 19, jnp.int32)
        return (x, src, dst, edge_attr_5, node_type_19)
    x, src, dst, edge_attr_5, node_type_19 = _rec_inputs()

    def _L0_gnn_setup():
        import jax, jax.numpy as jnp
        import numpy as np
        N = 2048
        E = 8192
        IN = 256
        OUT = 256
        TD = 32
        H = 4
        T = 19
        PROJ = OUT - 2 * TD
        DK = (OUT - TD) // H
        SQRT_DK = float(np.sqrt(DK))
        LN_EPS = 1e-05

        def time_emb(t, w, b):
            return jnp.cos(jnp.log(t + 1.0)[:, None] * w[None, :] + b[None, :])

        def typed_linear(x, W, b, node_type):
            out = jnp.zeros((x.shape[0], W.shape[2]), x.dtype)
            for t in range(W.shape[0]):
                out = jnp.where((node_type == t)[:, None], x @ W[t] + b[t], out)
            return out

        def seg_softmax(att, idx, n):
            m = jax.ops.segment_max(att, idx, num_segments=n)
            e = jnp.exp(att - m[idx])
            s = jax.ops.segment_sum(e, idx, num_segments=n)
            return e / (s[idx] + 1e-16)
        key = jax.random.key(seed)
        ks = jax.random.split(key, 8)
        x = jax.random.normal(ks[0], (N, IN), jnp.float32)
        node_type = jax.random.randint(ks[1], (N,), 0, T, jnp.int32)
        edge_index = jax.random.randint(ks[2], (2, E), 0, N, jnp.int32)
        times = jax.random.uniform(ks[3], (E, 3), jnp.float32, 0.0, 100.0)
        edge_attr = jnp.concatenate([times, node_type[edge_index[0]][:, None].astype(jnp.float32), node_type[edge_index[1]][:, None].astype(jnp.float32)], axis=1)
        s = 0.02
        Wk = jax.random.normal(ks[4], (T, IN, PROJ), jnp.float32) * s
        Wq = jax.random.normal(ks[5], (T, IN, PROJ), jnp.float32) * s
        Wv = jax.random.normal(ks[6], (T, IN, PROJ), jnp.float32) * s
        bk = jnp.zeros((T, PROJ), jnp.float32)
        bq = jnp.zeros((T, PROJ), jnp.float32)
        bv = jnp.zeros((T, PROJ), jnp.float32)
        Wa = jax.random.normal(ks[7], (T, 2 * OUT, IN), jnp.float32) * s
        ba = jnp.zeros((T, IN), jnp.float32)
        gamma = jnp.ones((T, IN), jnp.float32)
        beta = jnp.zeros((T, IN), jnp.float32)
        w_time = jnp.asarray(1.0 / 10 ** np.linspace(0, 1.5, TD), jnp.float32)
        b_time = jnp.zeros((TD,), jnp.float32)
        return dict(x=x, node_type=node_type, edge_index=edge_index, edge_attr=edge_attr, Wk=Wk, bk=bk, Wq=Wq, bq=bq, Wv=Wv, bv=bv, Wa=Wa, ba=ba, gamma=gamma, beta=beta, w_time=w_time, b_time=b_time)
    _L0_gnn_all = _L0_gnn_setup()
    _L0_gnn_in = {k: v for k, v in _L0_gnn_all.items() if k in ('Wk', 'bk', 'Wq', 'bq', 'Wv', 'bv', 'Wa', 'ba', 'gamma', 'beta', 'w_time', 'b_time')}
    del _L0_gnn_all

    def _L0_mix_setup():
        import jax, jax.numpy as jnp
        import numpy as np
        D_MODEL = 256
        NUM_HEADS = 8
        DEPTH = D_MODEL // NUM_HEADS
        B, L = (32, 256)

        def _feature_map(x):
            return jax.nn.elu(x) + 1.0
        key = jax.random.key(seed)
        ks = jax.random.split(key, 9)
        sc = 1.0 / np.sqrt(D_MODEL)
        return {'x': jax.random.normal(ks[0], (B, L, D_MODEL), dtype=jnp.float32), 'wq': jax.random.normal(ks[1], (D_MODEL, D_MODEL), dtype=jnp.float32) * sc, 'bq': jnp.zeros((D_MODEL,), dtype=jnp.float32), 'wk': jax.random.normal(ks[2], (D_MODEL, D_MODEL), dtype=jnp.float32) * sc, 'bk': jnp.zeros((D_MODEL,), dtype=jnp.float32), 'wv': jax.random.normal(ks[3], (D_MODEL, D_MODEL), dtype=jnp.float32) * sc, 'bv': jnp.zeros((D_MODEL,), dtype=jnp.float32), 'wo': jax.random.normal(ks[4], (D_MODEL, D_MODEL), dtype=jnp.float32) * sc, 'bo': jnp.zeros((D_MODEL,), dtype=jnp.float32)}
    _L0_mix_all = _L0_mix_setup()
    _L0_mix_in = {k: v for k, v in _L0_mix_all.items() if k in ('wq', 'bq', 'wk', 'bk', 'wv', 'bv', 'wo', 'bo')}
    del _L0_mix_all

    def _L0_ffn_setup():
        import jax, jax.numpy as jnp
        import numpy as np
        B, S, H, F, E, K = (8, 256, 256, 512, 16, 2)
        EPS = 1e-05
        key = jax.random.key(seed)
        ks = jax.random.split(key, 9)
        sc = 0.02
        return {'x': jax.random.normal(ks[0], (B, S, H), dtype=jnp.float32), 'gate_w': jax.random.normal(ks[1], (H, E), dtype=jnp.float32) * sc, 'gate_b': jnp.zeros((E,), dtype=jnp.float32), 'w1': jax.random.normal(ks[2], (E, H, F), dtype=jnp.float32) * sc, 'b1': jnp.zeros((E, F), dtype=jnp.float32), 'w2': jax.random.normal(ks[3], (E, F, H), dtype=jnp.float32) * sc, 'b2': jnp.zeros((E, H), dtype=jnp.float32), 'gamma': jnp.ones((H,), dtype=jnp.float32), 'beta': jnp.zeros((H,), dtype=jnp.float32)}
    _L0_ffn_all = _L0_ffn_setup()
    _L0_ffn_in = {k: v for k, v in _L0_ffn_all.items() if k in ('gate_w', 'gate_b', 'w1', 'b1', 'w2', 'b2', 'gamma', 'beta')}
    del _L0_ffn_all
    return {'x': x, 'src': src, 'dst': dst, 'edge_attr_5': edge_attr_5, 'node_type_19': node_type_19, 'L0_gnn_Wk': _L0_gnn_in['Wk'], 'L0_gnn_bk': _L0_gnn_in['bk'], 'L0_gnn_Wq': _L0_gnn_in['Wq'], 'L0_gnn_bq': _L0_gnn_in['bq'], 'L0_gnn_Wv': _L0_gnn_in['Wv'], 'L0_gnn_bv': _L0_gnn_in['bv'], 'L0_gnn_Wa': _L0_gnn_in['Wa'], 'L0_gnn_ba': _L0_gnn_in['ba'], 'L0_gnn_gamma': _L0_gnn_in['gamma'], 'L0_gnn_beta': _L0_gnn_in['beta'], 'L0_gnn_w_time': _L0_gnn_in['w_time'], 'L0_gnn_b_time': _L0_gnn_in['b_time'], 'L0_mix_wq': _L0_mix_in['wq'], 'L0_mix_bq': _L0_mix_in['bq'], 'L0_mix_wk': _L0_mix_in['wk'], 'L0_mix_bk': _L0_mix_in['bk'], 'L0_mix_wv': _L0_mix_in['wv'], 'L0_mix_bv': _L0_mix_in['bv'], 'L0_mix_wo': _L0_mix_in['wo'], 'L0_mix_bo': _L0_mix_in['bo'], 'L0_ffn_gate_w': _L0_ffn_in['gate_w'], 'L0_ffn_gate_b': _L0_ffn_in['gate_b'], 'L0_ffn_w1': _L0_ffn_in['w1'], 'L0_ffn_b1': _L0_ffn_in['b1'], 'L0_ffn_w2': _L0_ffn_in['w2'], 'L0_ffn_b2': _L0_ffn_in['b2'], 'L0_ffn_gamma': _L0_ffn_in['gamma'], 'L0_ffn_beta': _L0_ffn_in['beta']}

def reference(x, src, dst, edge_attr_5, node_type_19, L0_gnn_Wk, L0_gnn_bk, L0_gnn_Wq, L0_gnn_bq, L0_gnn_Wv, L0_gnn_bv, L0_gnn_Wa, L0_gnn_ba, L0_gnn_gamma, L0_gnn_beta, L0_gnn_w_time, L0_gnn_b_time, L0_mix_wq, L0_mix_bq, L0_mix_wk, L0_mix_bk, L0_mix_wv, L0_mix_bv, L0_mix_wo, L0_mix_bo, L0_ffn_gate_w, L0_ffn_gate_b, L0_ffn_w1, L0_ffn_b1, L0_ffn_w2, L0_ffn_b2, L0_ffn_gamma, L0_ffn_beta):
    import jax
    import jax.numpy as jnp

    def _L0_gnn_ref(x, node_type, edge_index, edge_attr, Wk, bk, Wq, bq, Wv, bv, Wa, ba, gamma, beta, w_time, b_time):
        import jax, jax.numpy as jnp
        import numpy as np
        N = 2048
        E = 8192
        IN = 256
        OUT = 256
        TD = 32
        H = 4
        T = 19
        PROJ = OUT - 2 * TD
        DK = (OUT - TD) // H
        SQRT_DK = float(np.sqrt(DK))
        LN_EPS = 1e-05

        def time_emb(t, w, b):
            return jnp.cos(jnp.log(t + 1.0)[:, None] * w[None, :] + b[None, :])

        def typed_linear(x, W, b, node_type):
            out = jnp.zeros((x.shape[0], W.shape[2]), x.dtype)
            for t in range(W.shape[0]):
                out = jnp.where((node_type == t)[:, None], x @ W[t] + b[t], out)
            return out

        def seg_softmax(att, idx, n):
            m = jax.ops.segment_max(att, idx, num_segments=n)
            e = jnp.exp(att - m[idx])
            s = jax.ops.segment_sum(e, idx, num_segments=n)
            return e / (s[idx] + 1e-16)
        row, col = (edge_index[0], edge_index[1])
        n = x.shape[0]
        K = typed_linear(x, Wk, bk, node_type)
        Q = typed_linear(x, Wq, bq, node_type)
        V = typed_linear(x, Wv, bv, node_type)
        e0 = time_emb(edge_attr[:, 0], w_time, b_time)
        e1 = time_emb(edge_attr[:, 1], w_time, b_time)
        e2 = time_emb(edge_attr[:, 2], w_time, b_time)

        def edge_msgs(Kn, Qn, Vn, ek, eq):
            k = jnp.concatenate([Kn, ek], axis=1).reshape(-1, H, DK)
            q = jnp.concatenate([Qn, eq], axis=1).reshape(-1, H, DK)
            att = jnp.einsum('ehd,ed->eh', k, q.sum(axis=1)) / SQRT_DK
            v = jnp.concatenate([Vn, ek], axis=1).reshape(-1, H, DK)
            return (att, v)
        att, v = edge_msgs(K[row], Q[col], V[row], e1, e2)
        att_i, v_i = edge_msgs(K[col], Q[row], V[col], e2, e1)
        att = seg_softmax(att, col, n)
        att_i = seg_softmax(att_i, row, n)
        res = (v * att[:, :, None]).reshape(-1, H * DK)
        res = jnp.concatenate([res, e0], axis=1)
        res_i = (v_i * att_i[:, :, None]).reshape(-1, H * DK)
        res_i = jnp.concatenate([res_i, e0], axis=1)
        agg = jax.ops.segment_sum(res, col, num_segments=n) + jax.ops.segment_sum(res_i, row, num_segments=n)
        h = jnp.concatenate([agg, agg], axis=1)
        o = typed_linear(h, Wa, ba, node_type)
        y = o + x
        mu = y.mean(axis=-1, keepdims=True)
        var = y.var(axis=-1, keepdims=True)
        yn = (y - mu) / jnp.sqrt(var + LN_EPS)
        return yn * gamma[node_type] + beta[node_type]

    def _L0_mix_ref(x, wq, bq, wk, bk, wv, bv, wo, bo):
        import jax, jax.numpy as jnp
        import numpy as np
        D_MODEL = 256
        NUM_HEADS = 8
        DEPTH = D_MODEL // NUM_HEADS
        B, L = (32, 256)

        def _feature_map(x):
            return jax.nn.elu(x) + 1.0
        b, l, _ = x.shape
        q = (x @ wq + bq).reshape(b, l, NUM_HEADS, DEPTH)
        k = (x @ wk + bk).reshape(b, l, NUM_HEADS, DEPTH)
        v = (x @ wv + bv).reshape(b, l, NUM_HEADS, DEPTH)
        q = _feature_map(q)
        k = _feature_map(k)
        kv = jnp.einsum('blhd,blhe->bhde', k, v)
        k_sum = jnp.sum(k, axis=1)
        qkv = jnp.einsum('blhd,bhde->blhe', q, kv)
        normalizer = jnp.einsum('blhd,bhd->blh', q, k_sum) + 1e-06
        out = qkv / normalizer[..., None]
        out = out.reshape(b, l, D_MODEL)
        return out @ wo + bo

    def _L0_ffn_ref(x, gate_w, gate_b, w1, b1, w2, b2, gamma, beta):
        import jax, jax.numpy as jnp
        import numpy as np
        B, S, H, F, E, K = (8, 256, 256, 512, 16, 2)
        EPS = 1e-05
        gate_logits = x @ gate_w + gate_b
        topk_vals, topk_idx = jax.lax.top_k(gate_logits, K)
        topk_w = jax.nn.softmax(topk_vals, axis=-1)
        h = jax.nn.relu(jnp.einsum('bsh,ehf->bsef', x, w1) + b1)
        expert_out = jnp.einsum('bsef,efh->bseh', h, w2) + b2
        sel = jnp.take_along_axis(expert_out, topk_idx[:, :, :, None], axis=2)
        moe = jnp.sum(topk_w[..., None] * sel, axis=2)
        y = x + moe
        mu = jnp.mean(y, axis=-1, keepdims=True)
        var = jnp.var(y, axis=-1, keepdims=True)
        return (y - mu) / jnp.sqrt(var + EPS) * gamma + beta
    edge_index = jnp.stack([src, dst])
    xn = _layernorm(x, axis=-1)
    x = x + _L0_gnn_ref(xn, node_type_19, edge_index, edge_attr_5, L0_gnn_Wk, L0_gnn_bk, L0_gnn_Wq, L0_gnn_bq, L0_gnn_Wv, L0_gnn_bv, L0_gnn_Wa, L0_gnn_ba, L0_gnn_gamma, L0_gnn_beta, L0_gnn_w_time, L0_gnn_b_time) + _L0_mix_ref(xn[None], L0_mix_wq, L0_mix_bq, L0_mix_wk, L0_mix_bk, L0_mix_wv, L0_mix_bv, L0_mix_wo, L0_mix_bo)[0]
    x = x + _L0_ffn_ref(_layernorm(x, axis=-1)[None], L0_ffn_gate_w, L0_ffn_gate_b, L0_ffn_w1, L0_ffn_b1, L0_ffn_w2, L0_ffn_b2, L0_ffn_gamma, L0_ffn_beta)[0]
    return x

_drawn_inputs = setup_inputs


def setup_inputs(seed=0):
    import zlib

    import numpy as np

    out = dict(_drawn_inputs(seed))
    spreads = {'L0_gnn_bk': (0.0, 0.8),
     'L0_gnn_bq': (0.0, 0.8),
     'L0_gnn_bv': (0.0, 0.8),
     'L0_gnn_ba': (0.0, 0.8),
     'L0_gnn_gamma': (1.0, 0.2),
     'L0_gnn_beta': (0.0, 0.1),
     'L0_gnn_b_time': (0.0, 0.1),
     'L0_mix_bq': (0.0, 0.8),
     'L0_mix_bk': (0.0, 0.8),
     'L0_mix_bv': (0.0, 0.1),
     'L0_mix_bo': (0.0, 0.1),
     'L0_ffn_gate_b': (0.0, 0.292),
     'L0_ffn_b1': (0.0, 0.8),
     'L0_ffn_b2': (0.0, 0.275),
     'L0_ffn_gamma': (1.0, 0.2),
     'L0_ffn_beta': (0.0, 0.1)}
    factors = {'L0_gnn_Wk': 8.0,
     'L0_gnn_Wq': 8.0,
     'L0_gnn_Wv': 8.0,
     'L0_mix_wq': 8.0,
     'L0_mix_wk': 8.0,
     'L0_mix_wv': 4.082}
    for name, (base, spread) in spreads.items():
        noise = np.random.default_rng([zlib.crc32(name.encode()), seed]).standard_normal(out[name].shape)
        drawn = base * np.exp(spread * noise) if base else spread * noise
        out[name] = jnp.asarray(drawn.astype(out[name].dtype))
    for name, factor in factors.items():
        out[name] = (out[name] * factor).astype(out[name].dtype)
    return out
```

```python
from contextlib import ExitStack, contextmanager

import numpy as np

import concourse.bass as bass
from concourse import mybir

F32 = mybir.dt.float32
BF16 = mybir.dt.bfloat16
I32 = mybir.dt.int32
ALU = mybir.AluOpType
ACT = mybir.ActivationFunctionType
AX = mybir.AxisListType

P = 128
N = 3125
D = 256
NB = (N + P - 1) // P
NP = NB * P
LAST = N - (NB - 1) * P
E = 103125
ET = (E + P - 1) // P
EP = ET * P
ELAST = E - (P - 1) * ET
TYPES = 19
TD = 32
PROJ = 192
HEADS = 4
DK = 56
VW = HEADS * DK
QKV = 2 * PROJ + DK
S = 4
ITEM = S * P
GUARD = ITEM
DIR_ROWS = EP + GUARD
DIRS = 2
REC = 5
NI = E // ITEM * DIRS + NB * DIRS
NI += (2 - NI) % 3
SLOTS = NB * DIRS
PAYW = HEADS * (DK + 1)
ACCW = PAYW + TD
TABLE_ROWS = NP + P
BIG = 2.0 ** 100
MAGIC = 12582912.0
SCALE = 1.0 / float(np.sqrt(DK))
EPS = 1e-5
CHUNK = 13
EXPERTS = 16
FF = 512
MH = 8
MD = D // MH


class Chain:

    def __init__(self, eng, sem):
        self.eng, self.sem, self.n, self.term = eng, sem, 0, 0

    def __call__(self, ins):
        ins.then_inc(self.sem, 1)
        self.n += 1
        self.eng.wait_ge(self.sem, self.term + self.n)

    @contextmanager
    def loop(self, count, per):
        start = self.n
        with self.eng.Fori(0, count) as i:
            self.term = i * per
            yield i
            assert self.n - start == per, (self.n - start, per)
        self.n, self.term = start + per * count, 0


class Tick:

    def __init__(self, eng, sem, step, first, name):
        self.eng, self.sem, self.step = eng, sem, step
        self.reg = eng.alloc_register(name)
        eng.reg_mov(self.reg, first)

    def __call__(self, value=None):
        self.eng.wait_ge(self.sem, self.reg if value is None else value)
        self.eng.reg_add(self.reg, self.reg, self.step)


def bc(ap, axis, count):
    shape = list(ap.shape)
    shape.insert(axis, count)
    return ap.unsqueeze(axis).broadcast_to(shape)


def layer_norm(nc, link, act, src, sq, out, mean, var, std, s_var, s_std, turn):
    link(nc.vector.tensor_reduce(mean, src, AX.X, ALU.add))
    link(nc.vector.tensor_scalar(mean, mean, -1.0 / D, None, ALU.mult))
    link(nc.vector.tensor_tensor(out, src, bc(mean, 2, D), ALU.add))
    link(nc.vector.tensor_tensor(sq, out, out, ALU.mult))
    nc.vector.tensor_reduce(var, sq, AX.X, ALU.add).then_inc(s_var, 1)
    link.eng.wait_ge(s_std, turn)
    link(nc.vector.reciprocal(std, std))
    link(nc.vector.tensor_tensor(out, out, bc(std, 2, D), ALU.mult))


def build(nc, a, out):
    with ExitStack() as whole:
        def keep(name, shape, dt=F32):
            return whole.enter_context(nc.sbuf_tensor(name, shape, dt))

        rec_d = nc.dram_tensor("records", [DIRS * DIR_ROWS, REC], F32, kind="Internal").ap()
        kv_d = nc.dram_tensor("kv_table", [TABLE_ROWS, 2 * PROJ], F32, kind="Internal").ap()
        mix_d = nc.dram_tensor("mix_rows", [NP, D], F32, kind="Internal").ap()
        agg_d = nc.dram_tensor("agg_rows", [NP, D], F32, kind="Internal").ap()

        consts = keep("consts", [P, 4])
        ident = keep("ident", [P, P])
        identb = keep("identb", [P, P], BF16)
        iota = keep("iota", [P, P])
        types = keep("types", [P, NP])
        xn = keep("xn", [P, NB, D])
        with ExitStack() as edges:
            def hold(name, shape, dt=F32):
                return edges.enter_context(nc.sbuf_tensor(name, shape, dt))

            qtab = hold("qtab", [P, NB, DK])
            item_blk = hold("item_blk", [P, NI], I32)
            item_qblk = hold("item_qblk", [P, NI], I32)
            item_row = hold("item_row", [P, NI], I32)
            item_base = hold("item_base", [P, NI])
            prepare(nc, a, rec_d, kv_d, mix_d, consts, ident, identb, iota, qtab,
                    item_blk, item_qblk, item_row, item_base, types, xn)
            messages(nc, a, rec_d, kv_d, agg_d, consts, ident, identb, iota, qtab,
                     item_blk, item_qblk, item_row, item_base)
        finish(nc, a, agg_d, mix_d, consts, ident, types, xn, out)


def prepare(nc, a, rec_d, kv_d, mix_d, consts, ident, identb, iota, qtab,
            item_blk, item_qblk, item_row, item_base, types, xn):
    with ExitStack() as ctx:
        def sb(name, shape, dt=F32):
            return ctx.enter_context(nc.sbuf_tensor(name, shape, dt))

        def ps(name, shape, dt=F32):
            return ctx.enter_context(nc.psum_tensor(name, shape, dt))

        def sem(name):
            return ctx.enter_context(nc.semaphore(name))

        work = sb("work", [P, 2, ET])
        ends_i = work[:, :, :].bitcast(I32)
        ends = sb("ends", [P, 2, ET])
        logs = sb("logs", [P, 3, ET])
        key = sb("key", [P, ET])
        mask = sb("mask", [P, ET], I32)
        scan, rank = work[:, 0, :], work[:, 1, :]
        pos = sb("pos", [P, 2, ET], I32)
        KB = NB + 1
        tot = sb("tot", [P, DIRS, KB])
        base = sb("base", [P, KB])
        sums = sb("sums", [P, DIRS, KB])
        small = sb("small", [P, 8, SLOTS])
        small_i = sb("small_i", [P, SLOTS], I32)
        items = work[:, :, :].rearrange("p a t -> p (a t)")[:, 0:3 * NI].rearrange("p (a n) -> p a n", a=3)
        item_n = sb("item_n", [P, NI])
        item_ni = sb("item_ni", [P, NI], I32)
        before = sb("before", [P, P])
        ones = sb("ones", [P, P])
        stage = [sb(f"stage{i}", [P, CHUNK, REC]) for i in range(2)]
        spos = [sb(f"spos{i}", [P, CHUNK], I32) for i in range(2)]
        guard = sb("guard", [P, S, REC])

        stat = sb("stat", [P, 3, NB])
        xnT = sb("xnT", [P, 2, NP])
        xs = sb("xs", [P, D])
        WK = sb("WK", [P, 2, TYPES, QKV])
        wq_raw = sb("wq_raw", [P, TYPES, PROJ])
        types_i = xnT[:, 0, :].bitcast(I32)
        attr = wq_raw[:, :, :].rearrange("p a b -> p (a b)")
        bias = sb("bias", [TYPES, QKV])
        bq_raw = sb("bq_raw", [TYPES, PROJ])
        one_t = sb("one_t", [TYPES, P])
        pidx = sb("pidx", [P, 1])
        pidx_i = sb("pidx_i", [P, 1], I32)
        iota_i = sb("iota_i", [P, P], I32)
        xm = [sb(f"xm{i}", [P, 2, P]) for i in range(3)]
        kv_row = sb("kv_row", [P, 2 * PROJ])
        place = [0]

        def carve(shape, rows=P):
            size = int(np.prod(shape))
            lo, place[0] = place[0], place[0] + size
            v = WK[:, :, :, :].rearrange("p a b c -> p (a b c)")[0:rows, lo:lo + size]
            names = "abc"[:len(shape)]
            return v.rearrange(f"p ({' '.join(names)}) -> p {' '.join(names)}", **dict(zip(names, shape)))

        mw = carve([4, 2, D])
        mb = carve([2])
        mbr = carve([3, D], 1)
        fk = carve([2, 2 * D])
        kf = carve([D])
        vf = carve([D + 1])
        kvm = carve([2, P + 4])
        qT = carve([2, P])
        mo = carve([D])
        moT = carve([2, P])
        mrow = carve([D])
        rn = sb("rn", [P, MH])

        psT = ps("psT", [P, 4, P])[:, 0:2, :]
        psK = ps("psK", [P, 512])
        psC = ps("psC", [P, 2, 256])
        psM = ps("psM", [P, 2, D])
        psV = [ps(f"psV{i}", [P, 512]) for i in range(2)]
        psQ = ps("psQ", [P, 4, P])[:, 0:2, :]
        psO = ps("psO", [P, 2, 256])

        kv_zero = kv_row[:, :]

        s_clear = sem("s_clear")
        s_zero = sem("s_zero")
        s_x = sem("s_x")
        s_ends = sem("s_ends")
        s_attr = sem("s_attr")
        s_types = sem("s_types")
        s_w = sem("s_w")
        s_mw = sem("s_mw")
        s_wq = [sem(f"s_wq{i}") for i in range(2)]
        s_wqfree = sem("s_wqfree")
        s_iota = sem("s_iota")
        s_pool = sem("s_pool")
        s_dve = sem("s_dve")
        s_var = sem("s_var")
        s_std = sem("s_std")
        s_log = sem("s_log")
        s_tot = sem("s_tot")
        s_psC = sem("s_psC")
        s_pos = sem("s_pos")
        s_guard = sem("s_guard")
        s_gout = sem("s_gout")
        s_copied = sem("s_copied")
        s_scat = [sem(f"s_scat{i}") for i in range(2)]
        s_xs = sem("s_xs")
        s_psT = sem("s_psT")
        s_xT = sem("s_xT")
        s_tf = sem("s_tf")
        s_mask = sem("s_mask")
        s_mm = sem("s_mm")
        s_kvrow = sem("s_kvrow")
        s_kvout = sem("s_kvout")
        s_wsum = sem("s_wsum")
        s_kz = sem("s_kz")
        s_kzps = sem("s_kzps")
        s_kexp = sem("s_kexp")
        s_kf = sem("s_kf")
        s_vf = sem("s_vf")
        s_kvm = sem("s_kvm")
        s_qps = sem("s_qps")
        s_qz = sem("s_qz")
        s_qexp = sem("s_qexp")
        s_qT = sem("s_qT")
        s_ops = sem("s_ops")
        s_mo = sem("s_mo")
        s_moT = sem("s_moT")
        s_moTs = sem("s_moTs")
        s_mrow = sem("s_mrow")
        s_mout = sem("s_mout")
        s_mops = sem("s_mops")
        s_zt = sem("s_zt")

        block = ctx.enter_context(nc.Block())

        @block.sync
        def _(sp):
            sp.wait_ge(s_clear, 4)
            for n, end in enumerate(("src", "dst")):
                v = a[end]
                sp.dma_start(ends_i[0:P - 1, n, :], v[0:(P - 1) * ET].rearrange("(p t) -> p t", t=ET)).then_inc(s_ends, 16)
                sp.dma_start(ends_i[P - 1:P, n, 0:ELAST], v[(P - 1) * ET:E].rearrange("(o t) -> o t", o=1)).then_inc(s_ends, 16)
            sp.dma_start(xn[:, 0:NB - 1, :], a["x"][0:(NB - 1) * P, :].rearrange("(b p) d -> p b d", p=P)).then_inc(s_x, 16)
            sp.dma_start(xn[0:LAST, NB - 1, :], a["x"][(NB - 1) * P:N, :]).then_inc(s_x, 16)
            attr_d = a["edge_attr_5"]
            at = WK[:, :, :, :].rearrange("p a b c -> p (a b c)")[:, 0:ET * 5]
            sp.dma_start(at[0:P - 1, :], attr_d[0:(P - 1) * ET, :].rearrange("(p t) c -> p (t c)", t=ET)).then_inc(s_attr, 16)
            sp.dma_start(at[P - 1:P, 0:ELAST * 5], attr_d[(P - 1) * ET:E, :].rearrange("(o t) c -> o (t c)", o=1)).then_inc(s_attr, 16)
            sp.dma_start(types_i[:, 0:N], a["node_type_19"].rearrange("(o n) -> o n", o=1).broadcast_to([P, N])).then_inc(s_types, 16)
            sp.wait_ge(s_log, 1)
            for kc in range(2):
                sp.dma_start(WK[:, kc, :, 0:PROJ], a["L0_gnn_Wk"][:, kc * P:kc * P + P, :].rearrange("t i o -> i t o")).then_inc(s_w, 16)
                sp.dma_start(WK[:, kc, :, PROJ:2 * PROJ], a["L0_gnn_Wv"][:, kc * P:kc * P + P, :].rearrange("t i o -> i t o")).then_inc(s_w, 16)
            sp.dma_start(bias[:, 0:PROJ], a["L0_gnn_bk"]).then_inc(s_w, 16)
            sp.dma_start(bias[:, PROJ:2 * PROJ], a["L0_gnn_bv"]).then_inc(s_w, 16)
            sp.dma_start(bq_raw[:, :], a["L0_gnn_bq"]).then_inc(s_w, 16)
            for kc in range(2):
                if kc:
                    sp.wait_ge(s_wqfree, 1)
                sp.dma_start(wq_raw[:, :, :], a["L0_gnn_Wq"][:, kc * P:kc * P + P, :].rearrange("t i o -> i t o")).then_inc(s_wq[kc], 16)
            sp.wait_ge(s_guard, 2)
            sp.wait_ge(s_zero, 1)
            for d in range(DIRS):
                sp.dma_start(rec_d[d * DIR_ROWS + EP:(d + 1) * DIR_ROWS, :].rearrange("(p s) c -> p (s c)", p=P),
                             guard[:, :, :].rearrange("p s c -> p (s c)")).then_inc(s_gout, 16)
            sp.dma_start(kv_d[NP:TABLE_ROWS, :], kv_zero).then_inc(s_gout, 16)
            sp.wait_ge(s_gout, 48)
            sp.wait_ge(s_mm, NB * TYPES)
            for n, w in enumerate(("wq", "wk", "wv", "wo")):
                sp.dma_start(mw[:, n, :, :], a["L0_mix_" + w].rearrange("(c p) o -> p c o", p=P)).then_inc(s_mw, 16)
            sp.dma_start(mb[:, :], a["L0_mix_bq"].rearrange("(c p) -> p c", p=P), allow_slow_non_contiguous=True).then_inc(s_mw, 16)
            for n, w in enumerate(("bk", "bv", "bo")):
                sp.dma_start(mbr[:, n, :], a["L0_mix_" + w].rearrange("(o d) -> o d", o=1)).then_inc(s_mw, 16)

        @block.gpsimd
        def _(pool):
            nc.gpsimd.memset(ident[:, :], 0.0).then_inc(s_iota, 1)
            nc.gpsimd.memset(before[:, :], 1.0).then_inc(s_iota, 1)
            pool.wait_ge(s_iota, 2)
            nc.gpsimd.affine_select(out=ident[:, :], in_=ident[:, :], compare_op=ALU.not_equal, fill=1.0, base=0,
                                    pattern=[[-1, P]], channel_multiplier=1).then_inc(s_iota, 1)
            nc.gpsimd.affine_select(out=before[:, :], in_=before[:, :], compare_op=ALU.is_ge, fill=0.0, base=-1,
                                    pattern=[[1, P]], channel_multiplier=-1).then_inc(s_iota, 1)
            nc.gpsimd.iota(iota_i[:, :], pattern=[[1, P]], base=0, channel_multiplier=0).then_inc(s_iota, 1)
            nc.gpsimd.iota(pidx_i[:, :], pattern=[[0, 1]], base=0, channel_multiplier=1).then_inc(s_iota, 1)
            nc.gpsimd.iota(item_ni[:, :], pattern=[[1, NI]], base=0, channel_multiplier=0).then_inc(s_iota, 1)
            nc.gpsimd.memset(guard[:, :, :], 0.0).then_inc(s_guard, 1)
            pool.wait_ge(s_guard, 1)
            nc.gpsimd.memset(guard[:, :, 0:1], float(NP)).then_inc(s_guard, 1)
            chunks = ET // CHUNK
            pool.wait_ge(s_log, 1)
            ncopy = Tick(pool, s_copied, 6, 6, "copied")
            nscat = [Tick(pool, s_scat[u], 16 * CHUNK, 16 * CHUNK, f"scattered{u}") for u in range(2)]
            for d in range(DIRS):
                pool.wait_ge(s_pos, d + 1)
                centre, other = (1, 0) if d == 0 else (0, 1)
                cols = [(0, ends[:, centre, :]), (1, ends[:, other, :]), (2, logs[:, 1 + d, :]),
                        (3, logs[:, 2 - d, :]), (4, logs[:, 0, :])]

                def fill(u, c, first):
                    if not first:
                        nscat[u]()
                    for n, v in cols:
                        nc.gpsimd.tensor_copy(stage[u][:, :, n], v[:, bass.ds(c * CHUNK, CHUNK)]).then_inc(s_copied, 1)
                    nc.gpsimd.tensor_copy(spos[u][:, :], pos[:, d, bass.ds(c * CHUNK, CHUNK)]).then_inc(s_copied, 1)
                    ncopy()
                    for t in range(CHUNK):
                        pool.indirect_dma_start(
                            out=rec_d, out_offset=bass.IndirectOffsetOnAxis(ap=spos[u][:, t:t + 1], axis=0),
                            in_=stage[u][:, t, :], in_offset=None).then_inc(s_scat[u], 16)

                if d == 0:
                    fill(0, 0, True)
                    fill(1, 1, True)
                with pool.Fori(1 if d == 0 else 0, chunks // 2) as i:
                    for u in range(2):
                        fill(u, i * 2 + u, False)
            for u in range(2):
                nscat[u]()

        @block.scalar
        def _(act):
            act.wait_ge(s_attr, 32)
            at = WK[:, :, :, :].rearrange("p a b c -> p (a b c)")[:, 0:ET * 5].rearrange("p (t c) -> p c t", c=5)
            act.wait_ge(s_clear, 5)
            nc.scalar.activation(logs[:, :, :], at[:, 0:3, :], ACT.Ln, bias=1.0).then_inc(s_log, 1)
            act.wait_ge(s_var, 1)
            nc.scalar.activation(stat[:, 2, :], stat[:, 1, :], ACT.Sqrt, bias=consts[:, 0:1], scale=1.0 / D).then_inc(s_std, 1)
            turned = Tick(act, s_psT, 1, 1, "turned")
            with act.Fori(0, NB) as b:
                turned()
                nc.scalar.copy(xnT[:, :, bass.ds(b * P, P)], psT).then_inc(s_xT, 1)
            act.wait_ge(s_gout, 48)
            with act.Fori(0, NB) as b:
                act.wait_ge(s_mm, b * TYPES + TYPES)
                act.wait_ge(s_kvout, b * 16)
                lo = DK - TD
                nc.scalar.copy(kv_row[:, 0:lo], psK[:, 3 * DK:PROJ])
                kk = kv_row[:, lo:PROJ].rearrange("p (h d) -> p h d", h=3)
                kp = psK[:, 0:3 * DK].rearrange("p (h d) -> p h d", h=3)
                nc.scalar.copy(kk[:, :, 0:TD], kp[:, :, lo:DK])
                nc.scalar.copy(kk[:, :, TD:DK], kp[:, :, 0:lo])
                nc.scalar.copy(kv_row[:, PROJ:2 * PROJ], psK[:, PROJ:2 * PROJ])
                nc.scalar.copy(qtab[:, bass.ds(b, 1), 0:TD], psK[:, 2 * PROJ + lo:QKV].unsqueeze(1))
                nc.scalar.copy(qtab[:, bass.ds(b, 1), TD:DK], psK[:, 2 * PROJ:2 * PROJ + lo].unsqueeze(1)).then_inc(s_kvrow, 1)
                act.wait_ge(s_kvrow, b + 1)
                act.dma_start(kv_d[bass.ds(b * P, P), :], kv_row[:, :]).then_inc(s_kvout, 16)
            act.wait_ge(s_kvout, NB * 16)
            with act.Fori(0, NB) as b:
                act.wait_ge(s_kz, b + 1)
                nc.scalar.activation(fk[:, 1, 0:D], fk[:, 0, 0:D], ACT.Exp).then_inc(s_kexp, 1)
            with act.Fori(0, NB) as b:
                act.wait_ge(s_qz, b + 1)
                nc.scalar.activation(fk[:, 1, 0:D], fk[:, 0, 0:D], ACT.Exp).then_inc(s_qexp, 1)
                act.wait_ge(s_moT, b + 1)
                nc.scalar.copy(moT[:, :, :], psT).then_inc(s_moTs, 1)
                act.wait_ge(s_mops, b + 1)
                act.wait_ge(s_mout, b * 16)
                nc.scalar.copy(mrow[:, :], psO[:, 1, 0:D]).then_inc(s_mrow, 1)
                act.wait_ge(s_mrow, b + 1)
                act.dma_start(mix_d[bass.ds(b * P, P), :], mrow[:, :]).then_inc(s_mout, 16)
            act.wait_ge(s_mout, NB * 16)

        @block.vector
        def _(dve):
            link = Chain(dve, s_dve)
            at = WK[:, :, :, :].rearrange("p a b c -> p (a b c)")[:, 0:ET * 5]
            nc.vector.memset(at, 0.0).then_inc(s_clear, 1)
            nc.vector.memset(xn[:, NB - 1, :], 0.0).then_inc(s_clear, 1)
            nc.vector.memset(ends_i, NP).then_inc(s_clear, 1)
            nc.vector.memset(xnT[:, 0, :].bitcast(I32), -1).then_inc(s_clear, 1)
            for n, v in enumerate((EPS, MAGIC, -BIG, 1.0)):
                nc.vector.memset(consts[:, n:n + 1], v)
            nc.vector.memset(kv_zero, 0.0).then_inc(s_zero, 1)
            link(nc.vector.memset(ones[:, :], 1.0))
            nc.vector.memset(consts[:, 3:4], 1.0).then_inc(s_clear, 1)
            dve.wait_ge(s_iota, 7)
            nc.vector.tensor_copy(iota[:, :], iota_i[:, :])
            nc.vector.tensor_copy(pidx[:, :], pidx_i[:, :])
            nc.vector.tensor_copy(item_n[:, :], item_ni[:, :])
            link(nc.vector.tensor_copy(identb[:, :], ident[:, :]))
            dve.wait_ge(s_ends, 64)
            link(nc.vector.tensor_copy(ends[:, :, :], ends_i))

            for d in range(DIRS):
                centre = 1 - d
                link(nc.vector.tensor_copy(mask[:, :], ends[:, centre, :]))
                link(nc.vector.tensor_scalar(mask[:, :], mask[:, :], 7, None, ALU.arith_shift_right))
                link(nc.vector.tensor_copy(key[:, :], mask[:, :]))
                for k in range(KB):
                    link(nc.vector.tensor_scalar(mask[:, :], key[:, :], float(k), None, ALU.is_equal))
                    link(nc.vector.tensor_tensor_scan(scan, mask[:, :], mask[:, :], 0.0, ALU.add, ALU.max))
                    last = nc.vector.tensor_copy(tot[:, d, k:k + 1], scan[:, ET - 1:ET])
                    if k == KB - 1:
                        last.then_inc(s_tot, 1)
                    link(nc.vector.copy_predicated(rank, mask[:, :], scan) if k else
                         nc.vector.tensor_copy(rank, scan))
                dve.wait_ge(s_psC, d + 1)
                link(nc.vector.tensor_copy(sums[:, d, :], psC[:, 1, 0:KB]))
                first = small[:, 0, 0:KB]
                link(nc.vector.memset(first[:, 0:1], float(d * DIR_ROWS - 1)))
                for k in range(1, KB):
                    link(nc.vector.tensor_tensor(first[:, k:k + 1], first[:, k - 1:k], sums[:, d, k - 1:k], ALU.add))
                link(nc.vector.tensor_scalar(small[:, 1, d * NB:d * NB + NB], first[:, 0:NB], 1.0, None, ALU.add))
                link(nc.vector.tensor_tensor(base[:, :], first, psC[:, 0, 0:KB], ALU.add))
                for k in range(KB):
                    link(nc.vector.tensor_scalar(scan, key[:, :], float(k), base[:, k:k + 1], ALU.is_equal, ALU.mult))
                    link(nc.vector.tensor_tensor(rank, rank, scan, ALU.add))
                nc.vector.tensor_copy(pos[:, d, :], rank).then_inc(s_pos, 1)

            start = small[:, 1, :]
            link(nc.vector.tensor_copy(small[:, 2, :].rearrange("p (d k) -> p d k", d=DIRS), sums[:, :, 0:NB]))
            link(nc.vector.tensor_scalar(small[:, 2, :], small[:, 2, :], float(ITEM - 1), None, ALU.add))
            link(nc.vector.tensor_copy(small_i[:, :], small[:, 2, :]))
            link(nc.vector.tensor_scalar(small_i[:, :], small_i[:, :], int(np.log2(ITEM)), None, ALU.arith_shift_right))
            link(nc.vector.tensor_copy(small[:, 3, :], small_i[:, :]))
            link(nc.vector.tensor_tensor_scan(small[:, 4, :], small[:, 3, :], small[:, 3, :], 0.0, ALU.add, ALU.max))
            past = small[:, 4, :]
            link(nc.vector.tensor_tensor(small[:, 5, :], past, small[:, 3, :], ALU.subtract))
            link(nc.vector.tensor_scalar(small[:, 5, :], small[:, 5, :], -float(ITEM), None, ALU.mult))
            link(nc.vector.tensor_tensor(small[:, 5, :], small[:, 5, :], start, ALU.add))
            link(nc.vector.tensor_tensor(small[:, 6, 0:SLOTS - 1], small[:, 5, 1:SLOTS], small[:, 5, 0:SLOTS - 1], ALU.subtract))
            link(nc.vector.tensor_scalar(small[:, 7, 0:1], past[:, SLOTS - 1:SLOTS], -float(ITEM), float(DIRS * DIR_ROWS - GUARD), ALU.mult, ALU.add))
            link(nc.vector.tensor_tensor(small[:, 6, SLOTS - 1:SLOTS], small[:, 7, 0:1], small[:, 5, SLOTS - 1:SLOTS], ALU.subtract))
            link(nc.vector.tensor_scalar(items[:, 0, :], item_n[:, :], float(ITEM), small[:, 5, 0:1], ALU.mult, ALU.add))
            link(nc.vector.memset(items[:, 1, :], 0.0))
            for k in range(SLOTS):
                link(nc.vector.tensor_scalar(items[:, 2, :], item_n[:, :], past[:, k:k + 1], small[:, 6, k:k + 1], ALU.is_ge, ALU.mult))
                nc.vector.tensor_tensor(items[:, 0, :], items[:, 0, :], items[:, 2, :], ALU.add)
                link(nc.vector.scalar_tensor_tensor(items[:, 1, :], item_n[:, :], past[:, k:k + 1], items[:, 1, :], ALU.is_ge, ALU.add))
            link(nc.vector.tensor_scalar(items[:, 0, :], items[:, 0, :], float(DIRS * DIR_ROWS - GUARD), None, ALU.min))
            link(nc.vector.tensor_scalar(items[:, 1, :], items[:, 1, :], float(SLOTS - 1), None, ALU.min))
            link(nc.vector.tensor_scalar(items[:, 2, :], items[:, 1, :], float(NB), -float(NB), ALU.is_ge, ALU.mult))
            link(nc.vector.tensor_tensor(items[:, 2, :], items[:, 2, :], items[:, 1, :], ALU.add))
            nc.vector.tensor_copy(item_row[:, :], items[:, 0, :])
            nc.vector.tensor_copy(item_blk[:, :], items[:, 1, :])
            nc.vector.tensor_copy(item_qblk[:, :], items[:, 2, :])
            link(nc.vector.tensor_scalar(item_base[:, :], items[:, 2, :], float(P), None, ALU.mult))

            dve.wait_ge(s_types, 16)
            link(nc.vector.tensor_copy(types[:, :], types_i))
            dve.wait_ge(s_x, 32)
            layer_norm(nc, link, None, xn[:, :, :], xnT[:, :, :].rearrange("p c n -> p (c n)").rearrange("p (b d) -> p b d", d=D),
                       xn[:, :, :], stat[:, 0, :], stat[:, 1, :], stat[:, 2, :], s_var, s_std, 1)
            with dve.Fori(0, NB) as b:
                dve.wait_ge(s_psT, b)
                nc.vector.tensor_copy(xs[:, :], xn[:, bass.ds(b, 1), :].rearrange("p b d -> p (b d)")).then_inc(s_xs, 1)

            def head_sum(dst, src):
                link(nc.vector.tensor_tensor(dst, src[..., 0:DK], src[..., DK:2 * DK], ALU.add))
                link(nc.vector.tensor_tensor(dst, dst, src[..., 2 * DK:3 * DK], ALU.add))
                link(nc.vector.tensor_tensor(dst[..., 0:PROJ - 3 * DK], dst[..., 0:PROJ - 3 * DK], src[..., 3 * DK:PROJ], ALU.add))
            for kc in range(2):
                dve.wait_ge(s_wq[kc], 16)
                head_sum(WK[:, kc, :, 2 * PROJ:QKV], wq_raw[:, :, :])
                nc.vector.memset(rn[:, :], 0.0).then_inc(s_wqfree, 1)
            dve.wait_ge(s_w, 16 * 7)
            head_sum(bias[:, 2 * PROJ:QKV], bq_raw[:, :])
            nc.vector.memset(rn[:, :], 0.0).then_inc(s_wsum, 1)

            dve.wait_ge(s_xT, NB)
            with dve.Fori(0, NB) as b:
                cols = bass.ds(b * P, P)
                dve.wait_ge(s_mm, b * TYPES)
                nc.vector.tensor_scalar(one_t[:, :], types[0:TYPES, cols], pidx[0:TYPES, :], None, ALU.is_equal).then_inc(s_mask, 1)
                for t in range(TYPES):
                    dve.wait_ge(s_mm, b * TYPES + max(t - 2, 0))
                    nc.vector.scalar_tensor_tensor(xm[t % 3][:, :, :], bc(types[:, cols], 1, 2), float(t), xnT[:, :, cols],
                                                   ALU.is_equal, ALU.mult).then_inc(s_mask, 1)

            dve.wait_ge(s_mm, NB * TYPES)
            dve.wait_ge(s_mw, 16 * 8)
            nc.vector.memset(vf[:, D:D + 1], 1.0)
            link(nc.vector.memset(kvm[:, :, :], 0.0))
            with link.loop(NB, 1) as b:
                dve.wait_ge(s_kzps, b + 1)
                nc.vector.tensor_scalar(fk[:, 0, 0:D], psM[:, 0, :], 0.0, None, ALU.min).then_inc(s_kz, 1)
                dve.wait_ge(s_kf, b)
                nc.vector.tensor_copy(vf[:, 0:D], psM[:, 1, :])
                link(nc.vector.tensor_scalar(kf[:, :], psM[:, 0, :], 0.0, None, ALU.max))
                dve.wait_ge(s_kexp, b + 1)
                nc.vector.tensor_tensor(kf[:, :], kf[:, :], fk[:, 1, 0:D], ALU.add).then_inc(s_vf, 1)
            dve.wait_ge(s_kf, NB)
            for c in range(2):
                for h in range(4):
                    r = slice(h * MD, h * MD + MD)
                    nc.vector.tensor_copy(kvm[r, c, h * MD:h * MD + MD], psV[c][r, c * P + h * MD:c * P + h * MD + MD])
                    last = nc.vector.tensor_copy(kvm[r, c, P + h:P + h + 1], psV[c][r, D:D + 1])
            last.then_inc(s_kvm, 1)
            with link.loop(NB, 4) as b:
                dve.wait_ge(s_qps, b + 1)
                link(nc.vector.tensor_tensor(fk[:, 0, D:2 * D].rearrange("p (c n) -> p c n", c=2), psQ, bc(mb[:, :], 2, P), ALU.add))
                nc.vector.tensor_scalar(fk[:, 0, 0:D], fk[:, 0, D:2 * D], 0.0, None, ALU.min).then_inc(s_qz, 1)
                link(nc.vector.tensor_scalar(fk[:, 1, D:2 * D], fk[:, 0, D:2 * D], 0.0, None, ALU.max))
                dve.wait_ge(s_qexp, b + 1)
                dve.wait_ge(s_ops, b)
                nc.vector.tensor_tensor(qT[:, :, :].rearrange("p c n -> p (c n)"), fk[:, 1, D:2 * D], fk[:, 1, 0:D], ALU.add).then_inc(s_qT, 1)
                dve.wait_ge(s_ops, b + 1)
                link(nc.vector.tensor_scalar(rn[:, :], psM[:, 1, 0:MH], 1e-6, None, ALU.add))
                link(nc.vector.reciprocal(rn[:, :], rn[:, :]))
                dve.wait_ge(s_moT, b)
                nc.vector.tensor_tensor(mo[:, :].rearrange("p (h d) -> p h d", h=MH), psO[:, 0, 0:D].rearrange("p (h d) -> p h d", h=MH),
                                        bc(rn[:, :], 2, MD), ALU.mult).then_inc(s_mo, 1)

        @block.tensor
        def _(pe):
            for d in range(DIRS):
                pe.wait_ge(s_tot, d + 1)
                if d:
                    pe.wait_ge(s_pos, d)
                nc.tensor.matmul(psC[:, 0, 0:KB], before[:, :], tot[:, d, :], start=True, stop=True)
                nc.tensor.matmul(psC[:, 1, 0:KB], ones[:, :], tot[:, d, :], start=True, stop=True).then_inc(s_psC, 1)
            with pe.Fori(0, NB) as b:
                pe.wait_ge(s_xs, b + 1)
                pe.wait_ge(s_xT, b)
                nc.tensor.transpose(psT[:, 0, :], xs[:, 0:P], ident[:, :])
                nc.tensor.transpose(psT[:, 1, :], xs[:, P:D], ident[:, :]).then_inc(s_psT, 1)
            pe.wait_ge(s_wsum, 1)
            pe.wait_ge(s_wqfree, 2)
            with pe.Fori(0, NB) as b:
                pe.wait_ge(s_mask, b * (TYPES + 1) + 1)
                pe.wait_ge(s_kvrow, b)
                nc.tensor.matmul(psK[:, 0:QKV], one_t[:, :], bias[:, :], start=True, stop=False)
                for t in range(TYPES):
                    pe.wait_ge(s_mask, b * (TYPES + 1) + t + 2)
                    nc.tensor.matmul(psK[:, 0:QKV], xm[t % 3][:, 0, :], WK[:, 0, t, :], start=False, stop=False)
                    mm = nc.tensor.matmul(psK[:, 0:QKV], xm[t % 3][:, 1, :], WK[:, 1, t, :], start=False, stop=t == TYPES - 1)
                    mm.then_inc(s_mm, 1)
            pe.wait_ge(s_mw, 16 * 8)
            for b in range(NB):
                rows = P if b < NB - 1 else LAST
                cols = slice(b * P, b * P + P)
                if b:
                    pe.wait_ge(s_vf, b)
                for n in range(2):
                    for c in range(2):
                        nc.tensor.matmul(psM[:, n, :], xnT[:, c, cols], mw[:, 1 + n, c, :], start=c == 0, stop=False)
                    mm = nc.tensor.matmul(psM[:, n, :], ones[0:1, :], mbr[:, n, :], start=False, stop=True)
                mm.then_inc(s_kzps, 1)
                pe.wait_ge(s_vf, b + 1)
                for c in range(2):
                    mm = nc.tensor.matmul(psV[c][:, 0:D + 1], kf[0:rows, c * P:c * P + P], vf[0:rows, :], start=b == 0, stop=b == NB - 1)
                mm.then_inc(s_kf, 1)
            pe.wait_ge(s_kvm, 1)
            with pe.Fori(0, NB) as b:
                cols = bass.ds(b * P, P)
                for m in range(2):
                    for c in range(2):
                        mm = nc.tensor.matmul(psQ[:, m, :], mw[:, 0, c, m * P:m * P + P], xnT[:, c, cols], start=c == 0, stop=c == 1)
                mm.then_inc(s_qps, 1)
                pe.wait_ge(s_qT, b + 1)
                pe.wait_ge(s_mo, b)
                for c in range(2):
                    nc.tensor.matmul(psO[:, 0, c * P:c * P + P], qT[:, c, :], kvm[:, c, 0:P], start=True, stop=True)
                    mm = nc.tensor.matmul(psM[:, 1, c * 4:c * 4 + 4], qT[:, c, :], kvm[:, c, P:P + 4], start=True, stop=True)
                mm.then_inc(s_ops, 1)
                pe.wait_ge(s_mo, b + 1)
                pe.wait_ge(s_moTs, b)
                nc.tensor.transpose(psT[:, 0, :], mo[:, 0:P], ident[:, :])
                nc.tensor.transpose(psT[:, 1, :], mo[:, P:D], ident[:, :]).then_inc(s_moT, 1)
                pe.wait_ge(s_moTs, b + 1)
                pe.wait_ge(s_mrow, b)
                for c in range(2):
                    nc.tensor.matmul(psO[:, 1, 0:D], moT[:, c, :], mw[:, 3, c, :], start=c == 0, stop=False)
                nc.tensor.matmul(psO[:, 1, 0:D], ones[0:1, :], mbr[:, 2, :], start=False, stop=True).then_inc(s_mops, 1)


class Item:

    def __init__(self, c, i=None):
        self.c, self.i = c, i
        self.u = c % 3
        self.n = self.count()
        self.j = c // 3 if i is None else i + c // 3

    def exists(self):
        return self.i is not None or 0 <= self.c < NI

    def count(self, plus=0, times=1, gap=0):
        const = (self.c + plus) * times - gap
        return const if self.i is None else self.i * (3 * times) + const


def each_item(eng, body):
    for n in range(3):
        body(Item(n))
    with eng.Fori(0, NI // 3 - 1) as i:
        for u in range(3):
            body(Item(3 + u, i))
    for n in range(NI // 3 * 3, NI):
        body(Item(n))


def each_step(eng, body, link=None, per=0):
    def step(s):
        body(Item(s - 1), Item(s), Item(s + 1))

    step(-1)
    step(0)
    count = (NI - 2) // 3
    loop = link.loop(count, 3 * per) if link else eng.Fori(0, count)
    with loop as i:
        for k in range(3):
            body(*(Item(k + m, i) for m in range(3)))
    step(NI - 1)
    step(NI)


def wait(eng, sem, value):
    if not isinstance(value, int) or value > 0:
        eng.wait_ge(sem, value)


def messages(nc, a, rec_d, kv_d, agg_d, consts, ident, identb, iota, qtab,
             item_blk, item_qblk, item_row, item_base):
    with ExitStack() as ctx:
        def sb(name, shape, dt=F32):
            return ctx.enter_context(nc.sbuf_tensor(name, shape, dt))

        def ps(name, shape, dt=F32):
            return ctx.enter_context(nc.psum_tensor(name, shape, dt))

        def sem(name):
            return ctx.enter_context(nc.semaphore(name))

        def three(name, shape, dt=F32):
            return [sb(f"{name}{u}", shape, dt) for u in range(3)]

        ROW = TD + 2 * PROJ + TD
        acc = sb("acc", [P, SLOTS, ACCW])
        mstate = sb("mstate", [P, SLOTS, HEADS])
        rec = three("rec", [P, S, REC])
        idx = three("idx", [P, S], I32)
        kv = three("kv", [P, S, ROW])
        ph = three("ph", [P, S, 3, TD])
        fr = three("fr", [P, S, 3, TD])
        oh = three("oh", [P, S, P])
        noh = three("noh", [P, S, P], BF16)
        oht = three("oht", [P, S, P])
        eq = three("eq", [P, S, DK])
        pay = three("pay", [P, S, ACCW])
        att = three("att", [P, S, HEADS])
        mnew = three("mnew", [P, HEADS])
        dm = three("dm", [P, HEADS])
        alpha = three("alpha", [P, HEADS])
        centre = sb("centre", [P, S])
        qs = sb("qs", [P, S, DK])
        prod = sb("prod", [P, S, HEADS, DK])
        red = sb("red", [P, S, HEADS])
        z = sb("z", [P, S, HEADS])
        top = sb("top", [P, HEADS])
        PARTS = 3
        rest = sb("rest", [P, S, HEADS])
        parts = three("parts", [P, S, PARTS * HEADS], BF16)
        attT = sb("attT", [PARTS * HEADS, S, P], BF16)
        selc = sb("selc", [PARTS * HEADS, HEADS])
        sel = sb("sel", [PARTS * HEADS, HEADS, P], BF16)
        wt = sb("wt", [P, 2, TD])
        den = sb("den", [P, SLOTS, HEADS])

        psOT = ps("psOT", [P, 2 * S, P], BF16)[:, 0:S, :]
        psX = ps("psX", [PARTS * HEADS, 2 * S, P], BF16)[:, 0:S, :]
        psB = [ps(f"psB{h}", [P, S, P]) for h in range(HEADS)]
        psG = ps("psG", [P, 512])
        psA = ps("psA", [P, 512])
        qg = psG[:, 0:S * DK].rearrange("p (s d) -> p s d", s=S)
        mg = psG[:, S * DK:S * (DK + HEADS)].rearrange("p (s h) -> p s h", s=S)

        s_wt = sem("s_wt")
        s_set = sem("s_set")
        s_dve = sem("s_dve2")
        s_rec = [sem(f"s_rec{u}") for u in range(3)]
        s_kv = [sem(f"s_kv{u}") for u in range(3)]
        s_idx = sem("s_idx")
        s_ph = sem("s_ph")
        s_whole = sem("s_whole")
        s_fr = sem("s_fr")
        s_sin = sem("s_sin")
        s_oh = sem("s_oh")
        s_noh = sem("s_noh")
        s_ot = sem("s_ot")
        s_oht = sem("s_oht")
        s_qg = sem("s_qg")
        s_att = sem("s_att")
        s_x = sem("s_x2")
        s_attT = sem("s_attT")
        s_b = [sem(f"s_b{h}") for h in range(HEADS)]
        s_m = sem("s_m")
        s_alpha = sem("s_alpha")
        s_mg = sem("s_mg")
        s_z = sem("s_z")
        s_w = sem("s_w2")
        s_pay = sem("s_pay")
        s_agg = sem("s_agg")
        s_acc = sem("s_acc")
        s_sum = sem("s_sum")
        s_out = sem("s_out2")

        block = ctx.enter_context(nc.Block())

        @block.sync
        def _(sp):
            sp.dma_start(wt[:, 0, :], a["L0_gnn_w_time"].rearrange("(o n) -> o n", o=1).broadcast_to([P, TD])).then_inc(s_wt, 16)
            sp.dma_start(wt[:, 1, :], a["L0_gnn_b_time"].rearrange("(o n) -> o n", o=1).broadcast_to([P, TD])).then_inc(s_wt, 16)

            def load(it):
                row = sp.value_load(item_row[0:1, bass.ds(it.n, 1)], min_val=0, max_val=DIRS * DIR_ROWS - ITEM)
                sp.lower_val(row * REC * 4)
                if it.i is not None:
                    sp.lower_val(it.count(-2, 2))
                wait(sp, s_oh, it.count(-2))
                wait(sp, s_ph, it.count(-2, 2))
                sp.dma_start(rec[it.u][:, :, :].rearrange("p s c -> p (s c)"),
                             rec_d[bass.ds(row, ITEM), :].rearrange("(p s) c -> p (s c)", p=P)).then_inc(s_rec[it.u], 16)

            each_item(sp, load)
            sp.wait_ge(s_sum, 2)
            sp.dma_start(agg_d.rearrange("(b p) d -> p b d", p=P), acc[:, 0:NB, 0:D]).then_inc(s_out, 16)
            sp.wait_ge(s_out, 16)

        @block.gpsimd
        def _(pool):
            have_rec = [Tick(pool, s_rec[u], 16, 16, f"have_rec{u}") for u in range(3)]
            have_idx = Tick(pool, s_idx, 1, 1, "have_idx")
            kv_free = Tick(pool, s_pay, 1, 1, "kv_free")

            def gather(it):
                u = it.u
                if it.i is not None or it.c >= 3:
                    kv_free(it.count(-2) if it.i is None else None)
                have_rec[u](it.j * 16 + 16 if it.i is None else None)
                nc.gpsimd.tensor_copy(idx[u][:, :], rec[u][:, :, 1]).then_inc(s_idx, 1)
                have_idx(it.c + 1 if it.i is None else None)
                for j in range(S):
                    pool.indirect_dma_start(out=kv[u][:, j, TD:TD + 2 * PROJ], out_offset=None, in_=kv_d,
                                            in_offset=bass.IndirectOffsetOnAxis(ap=idx[u][:, j:j + 1], axis=0)).then_inc(s_kv[u], 16)
                if it.i is None and it.c == 0:
                    pool.wait_ge(s_set, 1)
                wait(pool, s_fr, it.count(-2))
                nc.gpsimd.tensor_tensor(ph[u][:, :, :, :], bc(rec[u][:, :, 2:5], 3, TD),
                                        bc(bc(wt[:, 0, :], 1, 3), 1, S), ALU.mult).then_inc(s_ph, 1)
                pool.wait_ge(s_ph, it.count(1, 2, 1))
                nc.gpsimd.tensor_tensor(ph[u][:, :, :, :].rearrange("p s e d -> p (s e) d"), ph[u][:, :, :, :].rearrange("p s e d -> p (s e) d"),
                                        bc(wt[:, 1, :], 1, 3 * S), ALU.add).then_inc(s_ph, 1)

            each_item(pool, gather)

        @block.scalar
        def _(act):
            act.wait_ge(s_set, 1)

            def step(last, it, nxt):
                if last.exists():
                    u = last.u
                    act.wait_ge(s_z, last.n + 1)
                    nc.scalar.activation(pay[u][:, :, 0:PAYW].rearrange("p s (h d) -> p s h d", h=HEADS)[:, :, :, 0],
                                         z[:, :, :], ACT.Exp).then_inc(s_w, 1)
                if it.exists():
                    act.wait_ge(s_x, it.n + 1)
                    wait(act, s_b[HEADS - 1], it.n)
                    nc.scalar.copy(attT[:, :, :], psX).then_inc(s_attT, 1)
                if nxt.exists():
                    u = nxt.u
                    act.wait_ge(s_ph, nxt.n * 2 + 2)
                    nc.scalar.activation(fr[u][:, :, :, :], ph[u][:, :, :, :], ACT.Identity, bias=consts[:, 1:2]).then_inc(s_whole, 1)
                    act.wait_ge(s_oh, nxt.n + 1)
                    wait(act, s_b[HEADS - 1], nxt.count(-2))
                    nc.scalar.activation(noh[u][:, :, :], oh[u][:, :, :], ACT.Identity, bias=consts[:, 2:3], scale=BIG).then_inc(s_noh, 1)
                    act.wait_ge(s_ot, nxt.n + 1)
                    wait(act, s_mg, nxt.count(-2))
                    nc.scalar.activation(oht[u][:, :, :], psOT, ACT.Identity, bias=1.0, scale=1.0 / BIG).then_inc(s_oht, 1)
                    act.wait_ge(s_fr, nxt.n + 1)
                    wait(act, s_pay, nxt.count(-2))
                    wait(act, s_agg, nxt.count(-2))
                    turn = -6.283185
                    kv_ends = kv[u][:, :, :]
                    nc.scalar.activation(kv_ends[:, :, 0:TD], fr[u][:, :, 0, :], ACT.Sin, scale=turn).then_inc(s_sin, 1)
                    nc.scalar.activation(kv_ends[:, :, ROW - TD:ROW], fr[u][:, :, 0, :], ACT.Sin, scale=turn).then_inc(s_sin, 1)
                    nc.scalar.activation(eq[u][:, :, 0:TD], fr[u][:, :, 1, :], ACT.Sin, scale=turn).then_inc(s_sin, 1)
                    nc.scalar.activation(pay[u][:, :, PAYW:ACCW], fr[u][:, :, 2, :], ACT.Sin, scale=turn).then_inc(s_sin, 1)
                if it.exists():
                    act.wait_ge(s_m, it.n + 1)
                    nc.scalar.activation(alpha[it.u][:, :], dm[it.u][:, :], ACT.Exp).then_inc(s_alpha, 1)

            each_step(act, step)

        @block.vector
        def _(dve):
            link = Chain(dve, s_dve)
            for u in range(3):
                nc.vector.memset(eq[u][:, :, TD:DK], 0.0)
            nc.vector.memset(mstate[:, :, :], -BIG)
            nc.vector.memset(acc[:, :, :], 0.0)
            link(nc.vector.tensor_reduce(selc[:, :], ident[0:PARTS * HEADS, 0:PARTS * HEADS].rearrange("k (a h) -> k h a", a=PARTS), AX.X, ALU.add))
            nc.vector.tensor_copy(sel[:, :, :], bc(selc[:, :], 2, P))
            dve.wait_ge(s_wt, 32)
            turn = float(1 / (2 * np.pi))
            link(nc.vector.tensor_scalar(wt[:, 0, :], wt[:, 0, :], turn, None, ALU.mult))
            link(nc.vector.tensor_scalar(wt[:, 1, :], wt[:, 1, :], turn, 0.25, ALU.mult, ALU.add))
            nc.vector.memset(top[:, :], 0.0).then_inc(s_set, 1)

            def step(last, it, nxt):
                if last.exists():
                    dve.wait_ge(s_mg, last.n + 1)
                    link(nc.vector.tensor_tensor(z[:, :, :], att[last.u][:, :, :], mg, ALU.subtract))
                    nc.vector.tensor_scalar(z[:, :, :], z[:, :, :], 0.0, None, ALU.min).then_inc(s_z, 1)
                if it.exists():
                    u = it.u
                    dve.wait_ge(s_qg, it.n + 1)
                    dve.wait_ge(s_sin, it.n * 4 + 4)
                    link(nc.vector.tensor_tensor(qs[:, :, :], qg, eq[u][:, :, :], ALU.add))
                    dve.wait_ge(s_kv[u], it.j * 64 + 64)
                    link(nc.vector.tensor_tensor(prod[:, :, :, :], kv[u][:, :, 0:VW].rearrange("p s (h d) -> p s h d", h=HEADS),
                                                 bc(qs[:, :, :], 2, HEADS), ALU.mult))
                    link(nc.vector.tensor_reduce(red[:, :, :], prod[:, :, :, :], AX.X, ALU.add))
                    nc.vector.tensor_scalar(att[u][:, :, 0:3], red[:, :, 1:4], SCALE, None, ALU.mult)
                    link(nc.vector.tensor_scalar(att[u][:, :, 3:4], red[:, :, 0:1], SCALE, None, ALU.mult))
                    hi, mid, lo = (parts[u][:, :, k * HEADS:(k + 1) * HEADS] for k in range(PARTS))
                    link(nc.vector.tensor_copy(hi, att[u][:, :, :]))
                    link(nc.vector.tensor_tensor(rest[:, :, :], att[u][:, :, :], hi, ALU.subtract))
                    link(nc.vector.tensor_copy(mid, rest[:, :, :]))
                    nc.vector.tensor_tensor(lo, rest[:, :, :], mid, ALU.subtract).then_inc(s_att, 1)
                if last.exists():
                    u = last.u
                    dve.wait_ge(s_w, last.n + 1)
                    rows = pay[u][:, :, 0:PAYW].rearrange("p s (h d) -> p s h d", h=HEADS)
                    nc.vector.tensor_tensor(rows[:, :, :, 1:DK + 1], kv[u][:, :, VW:2 * VW].rearrange("p s (h d) -> p s h d", h=HEADS),
                                            rows[:, :, :, 0:1].broadcast_to([P, S, HEADS, DK]), ALU.mult).then_inc(s_pay, 1)
                if nxt.exists():
                    u = nxt.u
                    dve.wait_ge(s_rec[u], nxt.j * 16 + 16)
                    link(nc.vector.tensor_scalar(centre[:, :], rec[u][:, :, 0], item_base[:, bass.ds(nxt.n, 1)], None, ALU.subtract))
                    wait(dve, s_agg, nxt.count(-2))
                    nc.vector.tensor_tensor(oh[u][:, :, :], bc(iota[:, :], 1, S), bc(centre[:, :], 2, P), ALU.is_equal).then_inc(s_oh, 1)
                    dve.wait_ge(s_whole, nxt.n + 1)
                    nc.vector.scalar_tensor_tensor(fr[u][:, :, :, :], fr[u][:, :, :, :], -MAGIC, ph[u][:, :, :, :], ALU.add, ALU.subtract).then_inc(s_fr, 1)
                if it.exists():
                    u = it.u
                    slot = dve.value_load(item_blk[0:1, bass.ds(it.n, 1)], min_val=0, max_val=SLOTS - 1)
                    for h in range(HEADS):
                        dve.wait_ge(s_b[h], it.n + 1)
                        ins = nc.vector.tensor_reduce(top[:, h:h + 1], psB[h][:, :, :].rearrange("p s n -> p (s n)"), AX.X, ALU.max)
                    link(ins)
                    m = mstate[:, bass.ds(slot, 1), :].rearrange("p b h -> p (b h)")
                    link(nc.vector.tensor_tensor(mnew[u][:, :], m, top[:, :], ALU.max))
                    link(nc.vector.tensor_tensor(dm[u][:, :], m, mnew[u][:, :], ALU.subtract))
                    link(nc.vector.tensor_tensor(m, m, top[:, :], ALU.max))
                    nc.vector.tensor_scalar(top[:, :], top[:, :], 0.0, None, ALU.mult).then_inc(s_m, 1)
                if last.exists():
                    u = last.u
                    slot = dve.value_load(item_blk[0:1, bass.ds(last.n, 1)], min_val=0, max_val=SLOTS - 1)
                    dve.wait_ge(s_alpha, last.n + 1)
                    wait(dve, s_acc, last.n)
                    row = acc[:, bass.ds(slot, 1), :].rearrange("p b w -> p (b w)")
                    heads = row[:, 0:PAYW].rearrange("p (h d) -> p h d", h=HEADS)
                    link(nc.vector.tensor_tensor(heads, heads, bc(alpha[u][:, :], 2, DK + 1), ALU.mult))
                    dve.wait_ge(s_agg, last.n + 1)
                    nc.vector.tensor_tensor(row, row, psA[:, 0:ACCW], ALU.add).then_inc(s_acc, 1)

            each_step(dve, step, link, 14)
            dve.wait_ge(s_acc, NI)
            heads = acc[:, :, 0:PAYW].rearrange("p b (h d) -> p b h d", h=HEADS)
            link(nc.vector.tensor_scalar(den[:, :, :], heads[:, :, :, 0], 1e-16, None, ALU.add))
            link(nc.vector.reciprocal(den[:, :, :], den[:, :, :]))
            link(nc.vector.tensor_tensor(heads[:, :, :, 1:DK + 1], heads[:, :, :, 1:DK + 1], bc(den[:, :, :], 3, DK), ALU.mult))
            link(nc.vector.tensor_tensor(heads[:, 0:NB, :, 1:DK + 1], heads[:, 0:NB, :, 1:DK + 1], heads[:, NB:SLOTS, :, 1:DK + 1], ALU.add))
            link(nc.vector.tensor_tensor(acc[:, 0:NB, PAYW:ACCW], acc[:, 0:NB, PAYW:ACCW], acc[:, NB:SLOTS, PAYW:ACCW], ALU.add))
            for h in range(HEADS):
                link(nc.vector.tensor_copy(acc[:, NB:SLOTS, h * DK:h * DK + DK], heads[:, 0:NB, h, 1:DK + 1]))
            link(nc.vector.tensor_copy(acc[:, NB:SLOTS, VW:D], acc[:, 0:NB, PAYW:ACCW]))
            nc.vector.tensor_copy(acc[:, 0:NB, 0:D], acc[:, NB:SLOTS, 0:D]).then_inc(s_sum, 2)

        @block.tensor
        def _(pe):
            def step(last, it, nxt):
                if it.exists():
                    u = it.u
                    pe.wait_ge(s_att, it.n + 1)
                    wait(pe, s_attT, it.n)
                    for j in range(S):
                        mm = nc.tensor.transpose(psX[:, j, :], parts[u][:, j, :], identb[:, :])
                    mm.then_inc(s_x, 1)
                    pe.wait_ge(s_attT, it.n + 1)
                    pe.wait_ge(s_noh, it.n + 1)
                    wait(pe, s_m, it.n)
                    for h in range(HEADS):
                        nc.tensor.matmul(psB[h][:, :, :], sel[:, h, :], attT[:, :, :], start=True, stop=False)
                        for j in range(S):
                            mm = nc.tensor.matmul(psB[h][:, j, :], noh[u][:, j, :], identb[:, :], start=False, stop=j == S - 1)
                        mm.then_inc(s_b[h], 1)
                if last.exists():
                    u = last.u
                    pe.wait_ge(s_pay, last.n + 1)
                    wait(pe, s_acc, last.n)
                    for j in range(S):
                        mm = nc.tensor.matmul(psA[:, 0:ACCW], oh[u][:, j, :], pay[u][:, j, :], start=j == 0, stop=j == S - 1)
                    mm.then_inc(s_agg, 1)
                if nxt.exists():
                    u = nxt.u
                    pe.wait_ge(s_noh, nxt.n + 1)
                    wait(pe, s_oht, nxt.n)
                    for j in range(S):
                        mm = nc.tensor.transpose(psOT[:, j, :], noh[u][:, j, :], identb[:, :])
                    mm.then_inc(s_ot, 1)
                    blk = pe.value_load(item_qblk[0:1, bass.ds(nxt.n, 1)], min_val=0, max_val=NB - 1)
                    pe.wait_ge(s_oht, nxt.n + 1)
                    for j in range(S):
                        mm = nc.tensor.matmul(qg[:, j, :], oht[u][:, j, :], qtab[:, bass.ds(blk, 1), :].rearrange("p b d -> p (b d)"), start=True, stop=True)
                    mm.then_inc(s_qg, 1)
                if it.exists():
                    u = it.u
                    pe.wait_ge(s_m, it.n + 1)
                    for j in range(S):
                        mm = nc.tensor.matmul(mg[:, j, :], oht[u][:, j, :], mnew[u][:, :], start=True, stop=True)
                    mm.then_inc(s_mg, 1)

            pe.wait_ge(s_set, 1)
            each_step(pe, step)


def finish(nc, a, agg_d, mix_d, consts, ident, types, xn, out):
    with ExitStack() as ctx:
        def sb(name, shape, dt=F32):
            return ctx.enter_context(nc.sbuf_tensor(name, shape, dt))

        def ps(name, shape, dt=F32):
            return ctx.enter_context(nc.psum_tensor(name, shape, dt))

        def sem(name):
            return ctx.enter_context(nc.semaphore(name))

        BC = 5
        HALF = BC * P // 2
        CH = NB // BC
        FC = FF // P
        x1 = sb("x1", [P, NB, D])
        mix = sb("mix", [P, NB, D])
        WA = sb("WA", [P, 2, TYPES, D])
        raw = sb("raw", [P, TYPES, D])
        agg = [sb(f"agg{i}", [P, D]) for i in range(2)]
        aggT = sb("aggT", [P, 2, P])
        xm = [sb(f"fm{i}", [P, 2, P]) for i in range(3)]
        rows = sb("rows", [TYPES, 3, D])
        one_t = sb("one_t2", [TYPES, P])
        pidx = sb("pidx2", [P, 1])
        pidx_i = sb("pidx2_i", [P, 1], I32)
        y = sb("y", [P, D])
        bn = sb("bn", [P, 6])
        mv = sb("mv", [P, 2])
        std1 = sb("std1", [P, 1])
        stat = sb("stat3", [P, 3, NB])
        x2T = WA[:, :, :, :].rearrange("p a b c -> p (a b c)")[:, 0:2 * NP].rearrange("p (c n) -> p c n", c=2)
        gw = sb("gw", [P, 2, EXPERTS])
        gb = sb("gb", [1, EXPERTS])
        ones1 = sb("ones1", [1, P])
        lg = sb("lg", [P, NB, EXPERTS])
        l2 = sb("l2", [P, NB, EXPERTS])
        t1 = sb("t1", [P, NB, EXPERTS])
        G = sb("G", [P, NB, EXPERTS])
        ex_i = sb("ex_i", [P, EXPERTS], I32)
        ex = sb("ex", [P, EXPERTS])
        gs = sb("gs", [P, 8, NB])
        b1 = sb("b1", [P, EXPERTS, FC])
        b2 = sb("b2", [EXPERTS, D])
        GT = sb("GT", [EXPERTS, P])
        w1 = [sb(f"w1_{i}", [P, 2, FF]) for i in range(2)]
        w2 = [sb(f"w2_{i}", [P, FC, D]) for i in range(2)]
        h = [sb(f"h{i}", [P, FC, 2, HALF]) for i in range(2)]
        gamma = sb("gamma", [P, D])
        beta = sb("beta", [P, D])

        psT = ps("psT3", [P, 4, P])[:, 0:2, :]
        psY = ps("psY", [P, 512])
        psW = ps("psW", [P, 512])
        psH = [ps(f"psH{i}", [P, 512]) for i in range(3)] + [psW]
        psE = [ps(f"psE{i}", [P, 512]) for i in range(2)]

        names = ("s_x s_mixl s_wa s_rows s_wsum s_iota s_dve3 s_aggT s_aggTs s_mask s_mm s_var s_std s_stage s_blk "
                 "s_tT s_tTs s_lg s_lgs s_g s_gT s_gTs s_gb s_gbs s_small s_h s_hs s_e s_es s_final s_out s_ones s_bn").split()
        q = {n: sem(n + "_f") for n in names}
        s_agg = [sem(f"s_agg_f{i}") for i in range(2)]
        s_ww = [sem(f"s_ww_f{i}") for i in range(2)]
        s_raw = [sem(f"s_raw_f{i}") for i in range(2)]
        block = ctx.enter_context(nc.Block())

        @block.sync
        def _(sp):
            wa = a["L0_gnn_Wa"]
            for kc in range(2):
                sp.dma_start(WA[:, kc, :, :], wa[:, kc * P:kc * P + P, :].rearrange("t i o -> i t o")).then_inc(q["s_wa"], 16)
            sp.dma_start(raw[:, :, :], wa[:, D:D + P, :].rearrange("t i o -> i t o")).then_inc(s_raw[0], 16)
            for n, w in enumerate(("ba", "gamma", "beta")):
                sp.dma_start(rows[:, n, :], a["L0_gnn_" + w]).then_inc(q["s_rows"], 16)
            sp.wait_ge(q["s_ones"], 1)
            sp.dma_start(x1[:, 0:NB - 1, :], a["x"][0:(NB - 1) * P, :].rearrange("(b p) d -> p b d", p=P)).then_inc(q["s_x"], 16)
            sp.dma_start(x1[0:LAST, NB - 1, :], a["x"][(NB - 1) * P:N, :]).then_inc(q["s_x"], 16)
            sp.dma_start(mix[:, :, :], mix_d.rearrange("(b p) d -> p b d", p=P)).then_inc(q["s_mixl"], 16)
            sp.dma_start(gw[:, :, :], a["L0_ffn_gate_w"].rearrange("(c p) e -> p c e", p=P)).then_inc(q["s_small"], 16)
            sp.dma_start(gb[:, :], a["L0_ffn_gate_b"].rearrange("(o e) -> o e", o=1)).then_inc(q["s_small"], 16)
            sp.dma_start(b1[:, :, :], a["L0_ffn_b1"].rearrange("e (c p) -> p e c", p=P), allow_slow_non_contiguous=True).then_inc(q["s_small"], 16)
            sp.dma_start(b2[:, :], a["L0_ffn_b2"]).then_inc(q["s_small"], 16)
            sp.dma_start(gamma[:, :], a["L0_ffn_gamma"].rearrange("(o e) -> o e", o=1).broadcast_to([P, D])).then_inc(q["s_small"], 16)
            sp.dma_start(beta[:, :], a["L0_ffn_beta"].rearrange("(o e) -> o e", o=1).broadcast_to([P, D])).then_inc(q["s_small"], 16)
            sp.wait_ge(q["s_wsum"], 1)
            sp.dma_start(raw[:, :, :], wa[:, D + P:2 * D, :].rearrange("t i o -> i t o")).then_inc(s_raw[1], 16)

            def load_agg(i, b, used):
                sp.lower_val(b * P * D * 4)
                wait(sp, q["s_aggT"], used)
                sp.dma_start(agg[i][:, :], agg_d[bass.ds(b * P, P), :]).then_inc(s_agg[i], 16)
            load_agg(0, 0, 0)
            with sp.Fori(0, NB // 2) as b:
                load_agg(1, b * 2 + 1, b * 2)
                load_agg(0, b * 2 + 2, b * 2 + 1)

            def load_expert(i, e):
                sp.dma_start(w1[i][:, :, :], a["L0_ffn_w1"][bass.ds(e, 1), :, :].rearrange("o (c p) f -> p (o c) f", p=P)).then_inc(s_ww[i], 16)
                sp.dma_start(w2[i][:, :, :], a["L0_ffn_w2"][bass.ds(e, 1), :, :].rearrange("o (c p) f -> p (o c) f", p=P)).then_inc(s_ww[i], 16)
            load_expert(0, 0)
            load_expert(1, 1)
            with sp.Fori(0, EXPERTS // 2 - 1) as g:
                for i in range(2):
                    e = g * 2 + (2 + i)
                    sp.lower_val(e * D * FF * 4)
                    sp.wait_ge(q["s_e"], g * (2 * NB) + (1 + i) * NB)
                    load_expert(i, e)
            sp.wait_ge(q["s_final"], 1)
            sp.dma_start(out[0:(NB - 1) * P, :].rearrange("(b p) d -> p b d", p=P), x1[:, 0:NB - 1, :]).then_inc(q["s_out"], 16)
            sp.dma_start(out[(NB - 1) * P:N, :], x1[0:LAST, NB - 1, :]).then_inc(q["s_out"], 16)
            sp.wait_ge(q["s_out"], 32)

        @block.gpsimd
        def _(pool):
            nc.gpsimd.iota(pidx_i[:, :], pattern=[[0, 1]], base=0, channel_multiplier=1).then_inc(q["s_iota"], 1)
            nc.gpsimd.iota(ex_i[:, :], pattern=[[1, EXPERTS]], base=0, channel_multiplier=0).then_inc(q["s_iota"], 1)

        @block.scalar
        def _(act):
            with act.Fori(0, NB) as b:
                act.wait_ge(q["s_aggT"], b + 1)
                act.wait_ge(q["s_mask"], b * (TYPES + 1))
                nc.scalar.copy(aggT[:, :, :], psT).then_inc(q["s_aggTs"], 1)
                act.wait_ge(q["s_var"], b + 1)
                nc.scalar.activation(std1[:, :], mv[:, 1:2], ACT.Sqrt, bias=consts[:, 0:1]).then_inc(q["s_std"], 1)
            act.wait_ge(q["s_var"], NB + 1)
            nc.scalar.activation(stat[:, 2, :], stat[:, 1, :], ACT.Sqrt, bias=consts[:, 0:1], scale=1.0 / D).then_inc(q["s_std"], 1)
            turned = Tick(act, q["s_tT"], 1, 1, "turned2")
            with act.Fori(0, NB) as b:
                turned()
                nc.scalar.copy(x2T[:, :, bass.ds(b * P, P)], psT).then_inc(q["s_tTs"], 1)
            act.wait_ge(q["s_g"], 1)
            nc.scalar.activation(gs[:, 3, :], gs[:, 2, :], ACT.Exp).then_inc(q["s_g"], 1)
            with act.Fori(0, NB) as b:
                act.wait_ge(q["s_gT"], b + 1)
                nc.scalar.copy(GT[:, :], psY[0:EXPERTS, 0:P]).then_inc(q["s_gTs"], 1)
            hidden = Tick(act, q["s_h"], 1, 1, "hidden")
            with act.Fori(0, EXPERTS // 2) as g:
                for k in range(2 * CH):
                    n = g * (2 * CH) + k
                    for m in range(FC * 2):
                        hidden()
                        nc.scalar.activation(h[k % 2][:, m // 2, m % 2, :], psH[m % 4][:, 0:HALF], ACT.Relu,
                                             bias=b1[:, bass.ds(g * 2 + k // CH, 1), m // 2]).then_inc(q["s_hs"], 1)
            act.wait_ge(q["s_var"], NB + 2)
            nc.scalar.activation(stat[:, 2, :], stat[:, 1, :], ACT.Sqrt, bias=consts[:, 0:1], scale=1.0 / D).then_inc(q["s_std"], 1)

        @block.vector
        def _(dve):
            link = Chain(dve, q["s_dve3"])
            link(nc.vector.memset(ones1[:, :], 1.0))
            nc.vector.memset(x1[:, NB - 1, :], 0.0).then_inc(q["s_ones"], 1)
            dve.wait_ge(q["s_iota"], 2)
            nc.vector.tensor_copy(pidx[:, :], pidx_i[:, :])
            nc.vector.tensor_copy(ex[:, :], ex_i[:, :])
            dve.wait_ge(q["s_wa"], 32)
            for kc in range(2):
                dve.wait_ge(s_raw[kc], 16)
                nc.vector.tensor_tensor(WA[:, kc, :, :], WA[:, kc, :, :], raw[:, :, :], ALU.add).then_inc(q["s_wsum"], 1)
            dve.wait_ge(q["s_x"], 32)
            dve.wait_ge(q["s_mixl"], 16)
            link(nc.vector.tensor_tensor(x1[:, :, :], x1[:, :, :], mix[:, :, :], ALU.add))
            have_bn = Tick(dve, q["s_bn"], 1, 1, "have_bn")
            with link.loop(NB, 5) as b:
                cols = bass.ds(b * P, P)
                dve.wait_ge(q["s_mm"], b * TYPES)
                nc.vector.tensor_scalar(one_t[:, :], types[0:TYPES, cols], pidx[0:TYPES, :], None, ALU.is_equal).then_inc(q["s_mask"], 1)
                dve.wait_ge(q["s_aggTs"], b + 1)
                for t in range(TYPES):
                    dve.wait_ge(q["s_mm"], b * TYPES + max(t - 2, 0))
                    nc.vector.scalar_tensor_tensor(xm[t % 3][:, :, :], bc(types[:, cols], 1, 2), float(t), aggT[:, :, :],
                                                   ALU.is_equal, ALU.mult).then_inc(q["s_mask"], 1)
                dve.wait_ge(q["s_mm"], b * TYPES + TYPES)
                link(nc.vector.tensor_tensor(y[:, :], psY[:, 0:D], xn[:, bass.ds(b, 1), :].rearrange("p b d -> p (b d)"), ALU.add))
                nc.vector.bn_stats(bn[:, :], y[:, :]).then_inc(q["s_bn"], 1)
                have_bn()
                nc.vector.bn_aggr(mv[:, :], bn[:, :]).then_inc(q["s_var"], 1)
                dve.wait_ge(q["s_std"], b + 1)
                link(nc.vector.reciprocal(std1[:, :], std1[:, :]))
                link(nc.vector.tensor_scalar(y[:, :], y[:, :], mv[:, 0:1], std1[:, :], ALU.subtract, ALU.mult))
                link(nc.vector.tensor_tensor(y[:, :], y[:, :], psW[:, 0:D], ALU.mult))
                link(nc.vector.tensor_tensor(y[:, :], y[:, :], psW[:, D:2 * D], ALU.add))
                row = x1[:, bass.ds(b, 1), :].rearrange("p b d -> p (b d)")
                nc.vector.tensor_tensor(row, row, y[:, :], ALU.add).then_inc(q["s_blk"], 1)
            dve.wait_ge(q["s_blk"], NB)
            layer_norm(nc, link, None, x1[:, :, :], mix[:, :, :], xn[:, :, :], stat[:, 0, :], stat[:, 1, :], stat[:, 2, :],
                       q["s_var"], q["s_std"], NB + 1)
            with dve.Fori(0, NB) as b:
                dve.wait_ge(q["s_tT"], b)
                nc.vector.tensor_copy(y[:, :], xn[:, bass.ds(b, 1), :].rearrange("p b d -> p (b d)")).then_inc(q["s_stage"], 1)
            dve.wait_ge(q["s_lg"], 1)
            link(nc.vector.tensor_copy(lg[:, :, :], psH[0][:, 0:NB * EXPERTS].rearrange("p (b e) -> p b e", e=EXPERTS)))
            exb = bc(ex[:, :], 1, NB)

            def first_best(src, best, number, hot):
                link(nc.vector.tensor_reduce(best, src, AX.X, ALU.max))
                link(nc.vector.tensor_tensor(t1[:, :, :], src, bc(best, 2, EXPERTS), ALU.is_equal))
                link(nc.vector.tensor_scalar(t1[:, :, :], t1[:, :, :], -100.0, 100.0, ALU.mult, ALU.add))
                link(nc.vector.tensor_tensor(t1[:, :, :], t1[:, :, :], exb, ALU.add))
                link(nc.vector.tensor_reduce(number, t1[:, :, :], AX.X, ALU.min))
                link(nc.vector.tensor_tensor(hot, exb, bc(number, 2, EXPERTS), ALU.is_equal))
            first_best(lg[:, :, :], gs[:, 0, :], gs[:, 1, :], G[:, :, :])
            link(nc.vector.scalar_tensor_tensor(l2[:, :, :], G[:, :, :], -BIG, lg[:, :, :], ALU.mult, ALU.add))
            first_best(l2[:, :, :], gs[:, 4, :], gs[:, 5, :], lg[:, :, :])
            nc.vector.tensor_tensor(gs[:, 2, :], gs[:, 4, :], gs[:, 0, :], ALU.subtract).then_inc(q["s_g"], 1)
            dve.wait_ge(q["s_g"], 2)
            link(nc.vector.tensor_scalar(gs[:, 6, :], gs[:, 3, :], 1.0, None, ALU.add))
            link(nc.vector.reciprocal(gs[:, 6, :], gs[:, 6, :]))
            link(nc.vector.tensor_tensor(gs[:, 7, :], gs[:, 3, :], gs[:, 6, :], ALU.mult))
            link(nc.vector.tensor_tensor(G[:, :, :], G[:, :, :], bc(gs[:, 6, :], 2, EXPERTS), ALU.mult))
            link(nc.vector.tensor_tensor(lg[:, :, :], lg[:, :, :], bc(gs[:, 7, :], 2, EXPERTS), ALU.mult))
            link(nc.vector.tensor_tensor(G[:, :, :], G[:, :, :], lg[:, :, :], ALU.add))
            with link.loop(NB, 1) as b:
                dve.wait_ge(q["s_gT"], b)
                nc.vector.tensor_copy(t1[:, 0, :], G[:, bass.ds(b, 1), :].rearrange("p b e -> p (b e)")).then_inc(q["s_stage"], 1)
                dve.wait_ge(q["s_gb"], b + 1)
                link(nc.vector.tensor_tensor(mix[:, bass.ds(b, 1), :].rearrange("p b d -> p (b d)"), psW[:, 0:D],
                                             xn[:, bass.ds(b, 1), :].rearrange("p b d -> p (b d)"), ALU.add))
                nc.vector.memset(y[:, 0:1], 0.0).then_inc(q["s_gbs"], 1)
            with dve.Fori(0, EXPERTS // 2) as g:
                for k in range(2 * CH):
                    n = g * (2 * CH) + k
                    for b in range(BC):
                        m = k * BC + b
                        blk = (k % CH) * BC + b
                        dve.wait_ge(q["s_es"], n * BC + b)
                        dve.wait_ge(q["s_e"], n * BC + b + 1)
                        nc.vector.scalar_tensor_tensor(mix[:, blk, :], psE[m % 2][:, 0:D], G[:, blk, bass.ds(g * 2 + k // CH, 1)],
                                                       mix[:, blk, :], ALU.mult, ALU.add).then_inc(q["s_es"], 1)
            dve.wait_ge(q["s_es"], EXPERTS * NB)
            layer_norm(nc, link, None, mix[:, :, :], xn[:, :, :], mix[:, :, :], stat[:, 0, :], stat[:, 1, :], stat[:, 2, :],
                       q["s_var"], q["s_std"], NB + 2)
            link(nc.vector.tensor_tensor(mix[:, :, :], mix[:, :, :], bc(gamma[:, :], 1, NB), ALU.mult))
            link(nc.vector.tensor_tensor(mix[:, :, :], mix[:, :, :], bc(beta[:, :], 1, NB), ALU.add))
            nc.vector.tensor_tensor(x1[:, :, :], x1[:, :, :], mix[:, :, :], ALU.add).then_inc(q["s_final"], 1)

        @block.tensor
        def _(pe):
            pe.wait_ge(q["s_wsum"], 2)
            pe.wait_ge(q["s_rows"], 48)

            def project(i, b, turn):
                pe.wait_ge(s_agg[i], turn)
                pe.wait_ge(q["s_aggTs"], b)
                nc.tensor.transpose(psT[:, 0, :], agg[i][:, 0:P], ident[:, :])
                nc.tensor.transpose(psT[:, 1, :], agg[i][:, P:D], ident[:, :]).then_inc(q["s_aggT"], 1)
                pe.wait_ge(q["s_mask"], b * (TYPES + 1) + 1)
                pe.wait_ge(q["s_blk"], b)
                nc.tensor.matmul(psY[:, 0:D], one_t[:, :], rows[:, 0, :], start=True, stop=False)
                nc.tensor.matmul(psW[:, :], one_t[:, :], rows[:, 1:3, :].rearrange("t a d -> t (a d)"), start=True, stop=True)
                for t in range(TYPES):
                    pe.wait_ge(q["s_mask"], b * (TYPES + 1) + t + 2)
                    nc.tensor.matmul(psY[:, 0:D], xm[t % 3][:, 0, :], WA[:, 0, t, :], start=False, stop=False)
                    nc.tensor.matmul(psY[:, 0:D], xm[t % 3][:, 1, :], WA[:, 1, t, :], start=False, stop=t == TYPES - 1).then_inc(q["s_mm"], 1)
            project(0, 0, 16)
            with pe.Fori(0, NB // 2) as b:
                project(1, b * 2 + 1, b * 16 + 16)
                project(0, b * 2 + 2, b * 16 + 32)
            with pe.Fori(0, NB) as b:
                pe.wait_ge(q["s_stage"], b + 1)
                pe.wait_ge(q["s_tTs"], b)
                nc.tensor.transpose(psT[:, 0, :], y[:, 0:P], ident[:, :])
                nc.tensor.transpose(psT[:, 1, :], y[:, P:D], ident[:, :]).then_inc(q["s_tT"], 1)
            pe.wait_ge(q["s_tTs"], NB)
            pe.wait_ge(q["s_small"], 96)
            for b in range(NB):
                o = psH[0][:, b * EXPERTS:(b + 1) * EXPERTS]
                for c in range(2):
                    nc.tensor.matmul(o, x2T[:, c, b * P:b * P + P], gw[:, c, :], start=c == 0, stop=False)
                mm = nc.tensor.matmul(o, ones1[:, :], gb[:, :], start=False, stop=True)
            mm.then_inc(q["s_lg"], 1)
            with pe.Fori(0, NB) as b:
                pe.wait_ge(q["s_stage"], b + NB + 1)
                pe.wait_ge(q["s_gTs"], b)
                nc.tensor.transpose(psY[0:EXPERTS, 0:P], t1[:, 0, :], ident[:, :]).then_inc(q["s_gT"], 1)
                pe.wait_ge(q["s_gTs"], b + 1)
                pe.wait_ge(q["s_gbs"], b)
                nc.tensor.matmul(psW[:, 0:D], GT[:, :], b2[:, :], start=True, stop=True).then_inc(q["s_gb"], 1)
            pe.wait_ge(q["s_gbs"], NB)
            with pe.Fori(0, EXPERTS // 2) as g:
                for k in range(2 * CH):
                    n = g * (2 * CH) + k
                    i, c = k // CH, k % CH
                    if c == 0:
                        pe.wait_ge(s_ww[i], g * 32 + 32)
                    for m in range(FC * 2):
                        f, half = m // 2, m % 2
                        pe.wait_ge(q["s_hs"], g * (2 * CH * FC * 2) + max(k * FC * 2 + m - 3, 0))
                        lo = c * BC * P + half * HALF
                        for kc in range(2):
                            mm = nc.tensor.matmul(psH[m % 4][:, 0:HALF], w1[i][:, kc, f * P:f * P + P], x2T[:, kc, lo:lo + HALF], start=kc == 0, stop=kc == 1)
                        mm.then_inc(q["s_h"], 1)
                    pe.wait_ge(q["s_hs"], n * (FC * 2) + FC * 2)
                    for b in range(BC):
                        m = k * BC + b
                        pe.wait_ge(q["s_es"], g * (2 * CH * BC) + max(m - 1, 0))
                        rows_h = h[k % 2][:, :, :, :].rearrange("p c a n -> p c (a n)")
                        for f in range(FC):
                            mm = nc.tensor.matmul(psE[m % 2][:, 0:D], rows_h[:, f, b * P:b * P + P], w2[i][:, f, :], start=f == 0, stop=f == FC - 1)
                        mm.then_inc(q["s_e"], 1)


_INS = ("x", "src", "dst", "edge_attr_5", "node_type_19",
        "L0_gnn_Wk", "L0_gnn_bk", "L0_gnn_Wq", "L0_gnn_bq", "L0_gnn_Wv", "L0_gnn_bv", "L0_gnn_Wa", "L0_gnn_ba",
        "L0_gnn_gamma", "L0_gnn_beta", "L0_gnn_w_time", "L0_gnn_b_time",
        "L0_mix_wq", "L0_mix_bq", "L0_mix_wk", "L0_mix_bk", "L0_mix_wv", "L0_mix_bv", "L0_mix_wo", "L0_mix_bo",
        "L0_ffn_gate_w", "L0_ffn_gate_b", "L0_ffn_w1", "L0_ffn_b1", "L0_ffn_w2", "L0_ffn_b2", "L0_ffn_gamma", "L0_ffn_beta")


def kernel(**inputs):
    import numpy as _np
    import concourse.bacc as _bacc
    from concourse import mybir as _mybir
    from concourse.bass_utils import run_bass_kernel_spmd as _run

    nc = _bacc.Bacc("TRN2", target_bir_lowering=False, num_devices=1)
    arrays, args = {}, {}
    for name in _INS:
        v = _np.ascontiguousarray(inputs[name])
        arrays[f"in_{name}_dram"] = v
        args[name] = nc.dram_tensor(f"in_{name}_dram", v.shape, _mybir.dt.from_np(v.dtype), kind="ExternalInput").ap()
    out = nc.dram_tensor("out_0_dram", (N, D), F32, kind="ExternalOutput").ap()
    build(nc, args, out)
    r = _run(nc, [arrays], core_ids=[0])
    return r.results[0]["out_0_dram"]
```

```python
from contextlib import ExitStack, contextmanager

import numpy as np

import concourse.bass as bass
from concourse import mybir

F32 = mybir.dt.float32
BF16 = mybir.dt.bfloat16
I32 = mybir.dt.int32
ALU = mybir.AluOpType
ACT = mybir.ActivationFunctionType
AX = mybir.AxisListType

P = 128
N = 3125
D = 256
NB = (N + P - 1) // P
NP = NB * P
LAST = N - (NB - 1) * P
E = 103125
ET = (E + P - 1) // P
EP = ET * P
ELAST = E - (P - 1) * ET
TYPES = 19
TD = 32
PROJ = 192
HEADS = 4
DK = 56
VW = HEADS * DK
QKV = 2 * PROJ + DK
S = 4
ITEM = S * P
GUARD = ITEM
DIR_ROWS = EP + GUARD
DIRS = 2
REC = 5
NI = E // ITEM * DIRS + NB * DIRS
BUFS = 4
NI += (5 - NI) % BUFS
SLOTS = NB * DIRS
PAYW = HEADS * (DK + 1)
ACCW = PAYW + TD
TABLE_ROWS = NP + P
BIG = 2.0 ** 100
PARTS = 3
MAGIC = 12582912.0
SCALE = 1.0 / float(np.sqrt(DK))
EPS = 1e-5
CHUNK = 13
EXPERTS = 16
FF = 512
MH = 8
MD = D // MH


class Chain:

    def __init__(self, eng, sem):
        self.eng, self.sem, self.n, self.term = eng, sem, 0, 0

    def __call__(self, ins):
        ins.then_inc(self.sem, 1)
        self.n += 1
        self.eng.wait_ge(self.sem, self.term + self.n)

    def post(self, ins):
        ins.then_inc(self.sem, 1)
        self.n += 1
        return self.n

    def until(self, n):
        if n:
            self.eng.wait_ge(self.sem, self.term + n)

    @contextmanager
    def loop(self, count, per):
        start = self.n
        with self.eng.Fori(0, count) as i:
            self.term = i * per
            yield i
            assert self.n - start == per, (self.n - start, per)
        self.n, self.term = start + per * count, 0


class Tick:

    def __init__(self, eng, sem, step, first, name):
        self.eng, self.sem, self.step = eng, sem, step
        self.reg = eng.alloc_register(name)
        eng.reg_mov(self.reg, first)

    def __call__(self, value=None):
        self.eng.wait_ge(self.sem, self.reg if value is None else value)
        self.eng.reg_add(self.reg, self.reg, self.step)


def bc(ap, axis, count):
    shape = list(ap.shape)
    shape.insert(axis, count)
    return ap.unsqueeze(axis).broadcast_to(shape)


def layer_norm(nc, link, act, src, sq, out, mean, var, std, s_var, s_std, turn):
    link(nc.vector.tensor_reduce(mean, src, AX.X, ALU.add))
    link(nc.vector.tensor_scalar(mean, mean, -1.0 / D, None, ALU.mult))
    link(nc.vector.tensor_tensor(out, src, bc(mean, 2, D), ALU.add))
    link(nc.vector.tensor_tensor(sq, out, out, ALU.mult))
    nc.vector.tensor_reduce(var, sq, AX.X, ALU.add).then_inc(s_var, 1)
    link.eng.wait_ge(s_std, turn)
    link(nc.vector.reciprocal(std, std))
    link(nc.vector.tensor_tensor(out, out, bc(std, 2, D), ALU.mult))


def build(nc, a, out):
    with ExitStack() as whole:
        def keep(name, shape, dt=F32):
            return whole.enter_context(nc.sbuf_tensor(name, shape, dt))

        rec_d = nc.dram_tensor("records", [DIRS * DIR_ROWS, REC], F32, kind="Internal").ap()
        kv_d = nc.dram_tensor("kv_table", [TABLE_ROWS, 2 * PROJ], F32, kind="Internal").ap()
        mix_d = nc.dram_tensor("mix_rows", [NP, D], F32, kind="Internal").ap()
        agg_d = nc.dram_tensor("agg_rows", [NP, D], F32, kind="Internal").ap()

        consts = keep("consts", [P, 4])
        ident = keep("ident", [P, P])
        identb = keep("identb", [P, P], BF16)
        iota = keep("iota", [P, P])
        types = keep("types", [P, NP])
        xn = keep("xn", [P, NB, D])
        with ExitStack() as edges:
            def hold(name, shape, dt=F32):
                return edges.enter_context(nc.sbuf_tensor(name, shape, dt))

            qtab = hold("qtab", [P, NB, DK])
            item_blk = hold("item_blk", [P, NI], I32)
            item_qblk = hold("item_qblk", [P, NI], I32)
            item_row = hold("item_row", [P, NI], I32)
            item_base = hold("item_base", [P, NI])
            prepare(nc, a, rec_d, kv_d, mix_d, consts, ident, identb, iota, qtab,
                    item_blk, item_qblk, item_row, item_base, types, xn)
            messages(nc, a, rec_d, kv_d, agg_d, consts, ident, identb, iota, qtab,
                     item_blk, item_qblk, item_row, item_base)
        finish(nc, a, agg_d, mix_d, consts, ident, types, xn, out)


def prepare(nc, a, rec_d, kv_d, mix_d, consts, ident, identb, iota, qtab,
            item_blk, item_qblk, item_row, item_base, types, xn):
    with ExitStack() as ctx:
        def sb(name, shape, dt=F32):
            return ctx.enter_context(nc.sbuf_tensor(name, shape, dt))

        def ps(name, shape, dt=F32):
            return ctx.enter_context(nc.psum_tensor(name, shape, dt))

        def sem(name):
            return ctx.enter_context(nc.semaphore(name))

        work = sb("work", [P, 2, ET])
        ends_i = work[:, :, :].bitcast(I32)
        ends = sb("ends", [P, 2, ET])
        logs = sb("logs", [P, 3, ET])
        key = sb("key", [P, ET])
        mask = sb("mask", [P, ET], I32)
        scan, rank = work[:, 0, :], work[:, 1, :]
        pos = sb("pos", [P, 2, ET], I32)
        KB = NB + 1
        tot = sb("tot", [P, DIRS, KB])
        base = sb("base", [P, KB])
        sums = sb("sums", [P, DIRS, KB])
        small = sb("small", [P, 8, SLOTS])
        small_i = sb("small_i", [P, SLOTS], I32)
        items = work[:, :, :].rearrange("p a t -> p (a t)")[:, 0:3 * NI].rearrange("p (a n) -> p a n", a=3)
        item_n = sb("item_n", [P, NI])
        item_ni = sb("item_ni", [P, NI], I32)
        before = sb("before", [P, P])
        ones = sb("ones", [P, P])
        stage = [sb(f"stage{i}", [P, CHUNK, REC]) for i in range(2)]
        spos = [sb(f"spos{i}", [P, CHUNK], I32) for i in range(2)]
        guard = sb("guard", [P, S, REC])

        stat = sb("stat", [P, 3, NB])
        xnT = sb("xnT", [P, 2, NP])
        xs = sb("xs", [P, D])
        WK = sb("WK", [P, 2, TYPES, QKV])
        wq_raw = sb("wq_raw", [P, TYPES, PROJ])
        types_i = xnT[:, 0, :].bitcast(I32)
        attr = wq_raw[:, :, :].rearrange("p a b -> p (a b)")
        bias = sb("bias", [TYPES, QKV])
        bq_raw = sb("bq_raw", [TYPES, PROJ])
        one_t = sb("one_t", [TYPES, P])
        pidx = sb("pidx", [P, 1])
        pidx_i = sb("pidx_i", [P, 1], I32)
        iota_i = sb("iota_i", [P, P], I32)
        xm = [sb(f"xm{i}", [P, 2, P]) for i in range(3)]
        kv_row = sb("kv_row", [P, 2 * PROJ])
        place = [0]

        def carve(shape, rows=P):
            size = int(np.prod(shape))
            lo, place[0] = place[0], place[0] + size
            v = WK[:, :, :, :].rearrange("p a b c -> p (a b c)")[0:rows, lo:lo + size]
            names = "abc"[:len(shape)]
            return v.rearrange(f"p ({' '.join(names)}) -> p {' '.join(names)}", **dict(zip(names, shape)))

        mw = carve([4, 2, D])
        mb = carve([2])
        mbr = carve([3, D], 1)
        fk = carve([2, 2 * D])
        kf = carve([D])
        vf = carve([D + 1])
        kvm = carve([2, P + 4])
        qT = carve([2, P])
        mo = carve([D])
        moT = carve([2, P])
        mrow = carve([D])
        rn = sb("rn", [P, MH])

        psT = ps("psT", [P, 4, P])[:, 0:2, :]
        psK = ps("psK", [P, 512])
        psC = ps("psC", [P, 2, 256])
        psM = ps("psM", [P, 2, D])
        psV = [ps(f"psV{i}", [P, 512]) for i in range(2)]
        psQ = ps("psQ", [P, 4, P])[:, 0:2, :]
        psO = ps("psO", [P, 2, 256])

        kv_zero = kv_row[:, :]

        s_clear = sem("s_clear")
        s_zero = sem("s_zero")
        s_x = sem("s_x")
        s_ends = sem("s_ends")
        s_attr = sem("s_attr")
        s_types = sem("s_types")
        s_w = sem("s_w")
        s_mw = sem("s_mw")
        s_wq = [sem(f"s_wq{i}") for i in range(2)]
        s_wqfree = sem("s_wqfree")
        s_iota = sem("s_iota")
        s_pool = sem("s_pool")
        s_dve = sem("s_dve")
        s_var = sem("s_var")
        s_std = sem("s_std")
        s_log = sem("s_log")
        s_tot = sem("s_tot")
        s_psC = sem("s_psC")
        s_pos = sem("s_pos")
        s_guard = sem("s_guard")
        s_gout = sem("s_gout")
        s_copied = sem("s_copied")
        s_scat = [sem(f"s_scat{i}") for i in range(2)]
        s_xs = sem("s_xs")
        s_psT = sem("s_psT")
        s_xT = sem("s_xT")
        s_tf = sem("s_tf")
        s_mask = sem("s_mask")
        s_mm = sem("s_mm")
        s_kvrow = sem("s_kvrow")
        s_kvout = sem("s_kvout")
        s_wsum = sem("s_wsum")
        s_kz = sem("s_kz")
        s_kzps = sem("s_kzps")
        s_kexp = sem("s_kexp")
        s_kf = sem("s_kf")
        s_vf = sem("s_vf")
        s_kvm = sem("s_kvm")
        s_qps = sem("s_qps")
        s_qz = sem("s_qz")
        s_qexp = sem("s_qexp")
        s_qT = sem("s_qT")
        s_ops = sem("s_ops")
        s_mo = sem("s_mo")
        s_moT = sem("s_moT")
        s_moTs = sem("s_moTs")
        s_mrow = sem("s_mrow")
        s_mout = sem("s_mout")
        s_mops = sem("s_mops")
        s_zt = sem("s_zt")

        block = ctx.enter_context(nc.Block())

        @block.sync
        def _(sp):
            sp.wait_ge(s_clear, 4)
            for n, end in enumerate(("src", "dst")):
                v = a[end]
                sp.dma_start(ends_i[0:P - 1, n, :], v[0:(P - 1) * ET].rearrange("(p t) -> p t", t=ET)).then_inc(s_ends, 16)
                sp.dma_start(ends_i[P - 1:P, n, 0:ELAST], v[(P - 1) * ET:E].rearrange("(o t) -> o t", o=1)).then_inc(s_ends, 16)
            sp.dma_start(xn[:, 0:NB - 1, :], a["x"][0:(NB - 1) * P, :].rearrange("(b p) d -> p b d", p=P)).then_inc(s_x, 16)
            sp.dma_start(xn[0:LAST, NB - 1, :], a["x"][(NB - 1) * P:N, :]).then_inc(s_x, 16)
            attr_d = a["edge_attr_5"]
            at = WK[:, :, :, :].rearrange("p a b c -> p (a b c)")[:, 0:ET * 5]
            sp.dma_start(at[0:P - 1, :], attr_d[0:(P - 1) * ET, :].rearrange("(p t) c -> p (t c)", t=ET)).then_inc(s_attr, 16)
            sp.dma_start(at[P - 1:P, 0:ELAST * 5], attr_d[(P - 1) * ET:E, :].rearrange("(o t) c -> o (t c)", o=1)).then_inc(s_attr, 16)
            sp.dma_start(types_i[:, 0:N], a["node_type_19"].rearrange("(o n) -> o n", o=1).broadcast_to([P, N])).then_inc(s_types, 16)
            sp.wait_ge(s_log, 1)
            for kc in range(2):
                sp.dma_start(WK[:, kc, :, 0:PROJ], a["L0_gnn_Wk"][:, kc * P:kc * P + P, :].rearrange("t i o -> i t o")).then_inc(s_w, 16)
                sp.dma_start(WK[:, kc, :, PROJ:2 * PROJ], a["L0_gnn_Wv"][:, kc * P:kc * P + P, :].rearrange("t i o -> i t o")).then_inc(s_w, 16)
            sp.dma_start(bias[:, 0:PROJ], a["L0_gnn_bk"]).then_inc(s_w, 16)
            sp.dma_start(bias[:, PROJ:2 * PROJ], a["L0_gnn_bv"]).then_inc(s_w, 16)
            sp.dma_start(bq_raw[:, :], a["L0_gnn_bq"]).then_inc(s_w, 16)
            for kc in range(2):
                if kc:
                    sp.wait_ge(s_wqfree, 1)
                sp.dma_start(wq_raw[:, :, :], a["L0_gnn_Wq"][:, kc * P:kc * P + P, :].rearrange("t i o -> i t o")).then_inc(s_wq[kc], 16)
            sp.wait_ge(s_guard, 2)
            sp.wait_ge(s_zero, 1)
            for d in range(DIRS):
                sp.dma_start(rec_d[d * DIR_ROWS + EP:(d + 1) * DIR_ROWS, :].rearrange("(p s) c -> p (s c)", p=P),
                             guard[:, :, :].rearrange("p s c -> p (s c)")).then_inc(s_gout, 16)
            sp.dma_start(kv_d[NP:TABLE_ROWS, :], kv_zero).then_inc(s_gout, 16)
            sp.wait_ge(s_gout, 48)
            sp.wait_ge(s_mm, NB * TYPES)
            for n, w in enumerate(("wq", "wk", "wv", "wo")):
                sp.dma_start(mw[:, n, :, :], a["L0_mix_" + w].rearrange("(c p) o -> p c o", p=P)).then_inc(s_mw, 16)
            sp.dma_start(mb[:, :], a["L0_mix_bq"].rearrange("(c p) -> p c", p=P), allow_slow_non_contiguous=True).then_inc(s_mw, 16)
            for n, w in enumerate(("bk", "bv", "bo")):
                sp.dma_start(mbr[:, n, :], a["L0_mix_" + w].rearrange("(o d) -> o d", o=1)).then_inc(s_mw, 16)

        @block.gpsimd
        def _(pool):
            nc.gpsimd.memset(ident[:, :], 0.0).then_inc(s_iota, 1)
            nc.gpsimd.memset(before[:, :], 1.0).then_inc(s_iota, 1)
            pool.wait_ge(s_iota, 2)
            nc.gpsimd.affine_select(out=ident[:, :], in_=ident[:, :], compare_op=ALU.not_equal, fill=1.0, base=0,
                                    pattern=[[-1, P]], channel_multiplier=1).then_inc(s_iota, 1)
            nc.gpsimd.affine_select(out=before[:, :], in_=before[:, :], compare_op=ALU.is_ge, fill=0.0, base=-1,
                                    pattern=[[1, P]], channel_multiplier=-1).then_inc(s_iota, 1)
            nc.gpsimd.iota(iota_i[:, :], pattern=[[1, P]], base=0, channel_multiplier=0).then_inc(s_iota, 1)
            nc.gpsimd.iota(pidx_i[:, :], pattern=[[0, 1]], base=0, channel_multiplier=1).then_inc(s_iota, 1)
            nc.gpsimd.iota(item_ni[:, :], pattern=[[1, NI]], base=0, channel_multiplier=0).then_inc(s_iota, 1)
            nc.gpsimd.memset(guard[:, :, :], 0.0).then_inc(s_guard, 1)
            pool.wait_ge(s_guard, 1)
            nc.gpsimd.memset(guard[:, :, 0:1], float(NP)).then_inc(s_guard, 1)
            chunks = ET // CHUNK
            pool.wait_ge(s_log, 1)
            ncopy = Tick(pool, s_copied, 6, 6, "copied")
            nscat = [Tick(pool, s_scat[u], 16 * CHUNK, 16 * CHUNK, f"scattered{u}") for u in range(2)]
            for d in range(DIRS):
                pool.wait_ge(s_pos, d + 1)
                centre, other = (1, 0) if d == 0 else (0, 1)
                cols = [(0, ends[:, centre, :]), (1, ends[:, other, :]), (2, logs[:, 1 + d, :]),
                        (3, logs[:, 2 - d, :]), (4, logs[:, 0, :])]

                def fill(u, c, first):
                    if not first:
                        nscat[u]()
                    for n, v in cols:
                        nc.gpsimd.tensor_copy(stage[u][:, :, n], v[:, bass.ds(c * CHUNK, CHUNK)]).then_inc(s_copied, 1)
                    nc.gpsimd.tensor_copy(spos[u][:, :], pos[:, d, bass.ds(c * CHUNK, CHUNK)]).then_inc(s_copied, 1)
                    ncopy()
                    for t in range(CHUNK):
                        pool.indirect_dma_start(
                            out=rec_d, out_offset=bass.IndirectOffsetOnAxis(ap=spos[u][:, t:t + 1], axis=0),
                            in_=stage[u][:, t, :], in_offset=None).then_inc(s_scat[u], 16)

                if d == 0:
                    fill(0, 0, True)
                    fill(1, 1, True)
                with pool.Fori(1 if d == 0 else 0, chunks // 2) as i:
                    for u in range(2):
                        fill(u, i * 2 + u, False)
            for u in range(2):
                nscat[u]()

        @block.scalar
        def _(act):
            act.wait_ge(s_attr, 32)
            at = WK[:, :, :, :].rearrange("p a b c -> p (a b c)")[:, 0:ET * 5].rearrange("p (t c) -> p c t", c=5)
            act.wait_ge(s_clear, 5)
            nc.scalar.activation(logs[:, :, :], at[:, 0:3, :], ACT.Ln, bias=1.0).then_inc(s_log, 1)
            act.wait_ge(s_var, 1)
            nc.scalar.activation(stat[:, 2, :], stat[:, 1, :], ACT.Sqrt, bias=consts[:, 0:1], scale=1.0 / D).then_inc(s_std, 1)
            turned = Tick(act, s_psT, 1, 1, "turned")
            with act.Fori(0, NB) as b:
                turned()
                nc.scalar.copy(xnT[:, :, bass.ds(b * P, P)], psT).then_inc(s_xT, 1)
            act.wait_ge(s_gout, 48)
            with act.Fori(0, NB) as b:
                act.wait_ge(s_mm, b * TYPES + TYPES)
                act.wait_ge(s_kvout, b * 16)
                lo = DK - TD
                nc.scalar.copy(kv_row[:, 0:lo], psK[:, 3 * DK:PROJ])
                kk = kv_row[:, lo:PROJ].rearrange("p (h d) -> p h d", h=3)
                kp = psK[:, 0:3 * DK].rearrange("p (h d) -> p h d", h=3)
                nc.scalar.copy(kk[:, :, 0:TD], kp[:, :, lo:DK])
                nc.scalar.copy(kk[:, :, TD:DK], kp[:, :, 0:lo])
                nc.scalar.copy(kv_row[:, PROJ:2 * PROJ], psK[:, PROJ:2 * PROJ])
                nc.scalar.copy(qtab[:, bass.ds(b, 1), 0:TD], psK[:, 2 * PROJ + lo:QKV].unsqueeze(1))
                nc.scalar.copy(qtab[:, bass.ds(b, 1), TD:DK], psK[:, 2 * PROJ:2 * PROJ + lo].unsqueeze(1)).then_inc(s_kvrow, 1)
                act.wait_ge(s_kvrow, b + 1)
                act.dma_start(kv_d[bass.ds(b * P, P), :], kv_row[:, :]).then_inc(s_kvout, 16)
            act.wait_ge(s_kvout, NB * 16)
            with act.Fori(0, NB) as b:
                act.wait_ge(s_kz, b + 1)
                nc.scalar.activation(fk[:, 1, 0:D], fk[:, 0, 0:D], ACT.Exp).then_inc(s_kexp, 1)
            with act.Fori(0, NB) as b:
                act.wait_ge(s_qz, b + 1)
                nc.scalar.activation(fk[:, 1, 0:D], fk[:, 0, 0:D], ACT.Exp).then_inc(s_qexp, 1)
                act.wait_ge(s_moT, b + 1)
                nc.scalar.copy(moT[:, :, :], psT).then_inc(s_moTs, 1)
                act.wait_ge(s_mops, b + 1)
                act.wait_ge(s_mout, b * 16)
                nc.scalar.copy(mrow[:, :], psO[:, 1, 0:D]).then_inc(s_mrow, 1)
                act.wait_ge(s_mrow, b + 1)
                act.dma_start(mix_d[bass.ds(b * P, P), :], mrow[:, :]).then_inc(s_mout, 16)
            act.wait_ge(s_mout, NB * 16)

        @block.vector
        def _(dve):
            link = Chain(dve, s_dve)
            at = WK[:, :, :, :].rearrange("p a b c -> p (a b c)")[:, 0:ET * 5]
            nc.vector.memset(at, 0.0).then_inc(s_clear, 1)
            nc.vector.memset(xn[:, NB - 1, :], 0.0).then_inc(s_clear, 1)
            nc.vector.memset(ends_i, NP).then_inc(s_clear, 1)
            nc.vector.memset(xnT[:, 0, :].bitcast(I32), -1).then_inc(s_clear, 1)
            for n, v in enumerate((EPS, MAGIC, -BIG, 1.0)):
                nc.vector.memset(consts[:, n:n + 1], v)
            nc.vector.memset(kv_zero, 0.0).then_inc(s_zero, 1)
            link(nc.vector.memset(ones[:, :], 1.0))
            nc.vector.memset(consts[:, 3:4], 1.0).then_inc(s_clear, 1)
            dve.wait_ge(s_iota, 7)
            nc.vector.tensor_copy(iota[:, :], iota_i[:, :])
            nc.vector.tensor_copy(pidx[:, :], pidx_i[:, :])
            nc.vector.tensor_copy(item_n[:, :], item_ni[:, :])
            link(nc.vector.tensor_copy(identb[:, :], ident[:, :]))
            dve.wait_ge(s_ends, 64)
            link(nc.vector.tensor_copy(ends[:, :, :], ends_i))

            for d in range(DIRS):
                centre = 1 - d
                link(nc.vector.tensor_copy(mask[:, :], ends[:, centre, :]))
                link(nc.vector.tensor_scalar(mask[:, :], mask[:, :], 7, None, ALU.arith_shift_right))
                link(nc.vector.tensor_copy(key[:, :], mask[:, :]))
                for k in range(KB):
                    link(nc.vector.tensor_scalar(mask[:, :], key[:, :], float(k), None, ALU.is_equal))
                    link(nc.vector.tensor_tensor_scan(scan, mask[:, :], mask[:, :], 0.0, ALU.add, ALU.max))
                    last = nc.vector.tensor_copy(tot[:, d, k:k + 1], scan[:, ET - 1:ET])
                    if k == KB - 1:
                        last.then_inc(s_tot, 1)
                    link(nc.vector.copy_predicated(rank, mask[:, :], scan) if k else
                         nc.vector.tensor_copy(rank, scan))
                dve.wait_ge(s_psC, d + 1)
                link(nc.vector.tensor_copy(sums[:, d, :], psC[:, 1, 0:KB]))
                first = small[:, 0, 0:KB]
                link(nc.vector.memset(first[:, 0:1], float(d * DIR_ROWS - 1)))
                for k in range(1, KB):
                    link(nc.vector.tensor_tensor(first[:, k:k + 1], first[:, k - 1:k], sums[:, d, k - 1:k], ALU.add))
                link(nc.vector.tensor_scalar(small[:, 1, d * NB:d * NB + NB], first[:, 0:NB], 1.0, None, ALU.add))
                link(nc.vector.tensor_tensor(base[:, :], first, psC[:, 0, 0:KB], ALU.add))
                for k in range(KB):
                    link(nc.vector.tensor_scalar(scan, key[:, :], float(k), base[:, k:k + 1], ALU.is_equal, ALU.mult))
                    link(nc.vector.tensor_tensor(rank, rank, scan, ALU.add))
                nc.vector.tensor_copy(pos[:, d, :], rank).then_inc(s_pos, 1)

            start = small[:, 1, :]
            link(nc.vector.tensor_copy(small[:, 2, :].rearrange("p (d k) -> p d k", d=DIRS), sums[:, :, 0:NB]))
            link(nc.vector.tensor_scalar(small[:, 2, :], small[:, 2, :], float(ITEM - 1), None, ALU.add))
            link(nc.vector.tensor_copy(small_i[:, :], small[:, 2, :]))
            link(nc.vector.tensor_scalar(small_i[:, :], small_i[:, :], int(np.log2(ITEM)), None, ALU.arith_shift_right))
            link(nc.vector.tensor_copy(small[:, 3, :], small_i[:, :]))
            link(nc.vector.tensor_tensor_scan(small[:, 4, :], small[:, 3, :], small[:, 3, :], 0.0, ALU.add, ALU.max))
            past = small[:, 4, :]
            link(nc.vector.tensor_tensor(small[:, 5, :], past, small[:, 3, :], ALU.subtract))
            link(nc.vector.tensor_scalar(small[:, 5, :], small[:, 5, :], -float(ITEM), None, ALU.mult))
            link(nc.vector.tensor_tensor(small[:, 5, :], small[:, 5, :], start, ALU.add))
            link(nc.vector.tensor_tensor(small[:, 6, 0:SLOTS - 1], small[:, 5, 1:SLOTS], small[:, 5, 0:SLOTS - 1], ALU.subtract))
            link(nc.vector.tensor_scalar(small[:, 7, 0:1], past[:, SLOTS - 1:SLOTS], -float(ITEM), float(DIRS * DIR_ROWS - GUARD), ALU.mult, ALU.add))
            link(nc.vector.tensor_tensor(small[:, 6, SLOTS - 1:SLOTS], small[:, 7, 0:1], small[:, 5, SLOTS - 1:SLOTS], ALU.subtract))
            link(nc.vector.tensor_scalar(items[:, 0, :], item_n[:, :], float(ITEM), small[:, 5, 0:1], ALU.mult, ALU.add))
            link(nc.vector.memset(items[:, 1, :], 0.0))
            for k in range(SLOTS):
                link(nc.vector.tensor_scalar(items[:, 2, :], item_n[:, :], past[:, k:k + 1], small[:, 6, k:k + 1], ALU.is_ge, ALU.mult))
                nc.vector.tensor_tensor(items[:, 0, :], items[:, 0, :], items[:, 2, :], ALU.add)
                link(nc.vector.scalar_tensor_tensor(items[:, 1, :], item_n[:, :], past[:, k:k + 1], items[:, 1, :], ALU.is_ge, ALU.add))
            link(nc.vector.tensor_scalar(items[:, 0, :], items[:, 0, :], float(DIRS * DIR_ROWS - GUARD), None, ALU.min))
            link(nc.vector.tensor_scalar(items[:, 1, :], items[:, 1, :], float(SLOTS - 1), None, ALU.min))
            link(nc.vector.tensor_scalar(items[:, 2, :], items[:, 1, :], float(NB), -float(NB), ALU.is_ge, ALU.mult))
            link(nc.vector.tensor_tensor(items[:, 2, :], items[:, 2, :], items[:, 1, :], ALU.add))
            nc.vector.tensor_copy(item_row[:, :], items[:, 0, :])
            nc.vector.tensor_copy(item_blk[:, :], items[:, 1, :])
            nc.vector.tensor_copy(item_qblk[:, :], items[:, 2, :])
            link(nc.vector.tensor_scalar(item_base[:, :], items[:, 2, :], float(P), None, ALU.mult))

            dve.wait_ge(s_types, 16)
            link(nc.vector.tensor_copy(types[:, :], types_i))
            dve.wait_ge(s_x, 32)
            layer_norm(nc, link, None, xn[:, :, :], xnT[:, :, :].rearrange("p c n -> p (c n)").rearrange("p (b d) -> p b d", d=D),
                       xn[:, :, :], stat[:, 0, :], stat[:, 1, :], stat[:, 2, :], s_var, s_std, 1)
            with dve.Fori(0, NB) as b:
                dve.wait_ge(s_psT, b)
                nc.vector.tensor_copy(xs[:, :], xn[:, bass.ds(b, 1), :].rearrange("p b d -> p (b d)")).then_inc(s_xs, 1)

            def head_sum(dst, src):
                link(nc.vector.tensor_tensor(dst, src[..., 0:DK], src[..., DK:2 * DK], ALU.add))
                link(nc.vector.tensor_tensor(dst, dst, src[..., 2 * DK:3 * DK], ALU.add))
                link(nc.vector.tensor_tensor(dst[..., 0:PROJ - 3 * DK], dst[..., 0:PROJ - 3 * DK], src[..., 3 * DK:PROJ], ALU.add))
            for kc in range(2):
                dve.wait_ge(s_wq[kc], 16)
                head_sum(WK[:, kc, :, 2 * PROJ:QKV], wq_raw[:, :, :])
                nc.vector.memset(rn[:, :], 0.0).then_inc(s_wqfree, 1)
            dve.wait_ge(s_w, 16 * 7)
            head_sum(bias[:, 2 * PROJ:QKV], bq_raw[:, :])
            nc.vector.memset(rn[:, :], 0.0).then_inc(s_wsum, 1)

            dve.wait_ge(s_xT, NB)
            with dve.Fori(0, NB) as b:
                cols = bass.ds(b * P, P)
                dve.wait_ge(s_mm, b * TYPES)
                nc.vector.tensor_scalar(one_t[:, :], types[0:TYPES, cols], pidx[0:TYPES, :], None, ALU.is_equal).then_inc(s_mask, 1)
                for t in range(TYPES):
                    dve.wait_ge(s_mm, b * TYPES + max(t - 2, 0))
                    nc.vector.scalar_tensor_tensor(xm[t % 3][:, :, :], bc(types[:, cols], 1, 2), float(t), xnT[:, :, cols],
                                                   ALU.is_equal, ALU.mult).then_inc(s_mask, 1)

            dve.wait_ge(s_mm, NB * TYPES)
            dve.wait_ge(s_mw, 16 * 8)
            nc.vector.memset(vf[:, D:D + 1], 1.0)
            link(nc.vector.memset(kvm[:, :, :], 0.0))
            with link.loop(NB, 1) as b:
                dve.wait_ge(s_kzps, b + 1)
                nc.vector.tensor_scalar(fk[:, 0, 0:D], psM[:, 0, :], 0.0, None, ALU.min).then_inc(s_kz, 1)
                dve.wait_ge(s_kf, b)
                nc.vector.tensor_copy(vf[:, 0:D], psM[:, 1, :])
                link(nc.vector.tensor_scalar(kf[:, :], psM[:, 0, :], 0.0, None, ALU.max))
                dve.wait_ge(s_kexp, b + 1)
                nc.vector.tensor_tensor(kf[:, :], kf[:, :], fk[:, 1, 0:D], ALU.add).then_inc(s_vf, 1)
            dve.wait_ge(s_kf, NB)
            for c in range(2):
                for h in range(4):
                    r = slice(h * MD, h * MD + MD)
                    nc.vector.tensor_copy(kvm[r, c, h * MD:h * MD + MD], psV[c][r, c * P + h * MD:c * P + h * MD + MD])
                    last = nc.vector.tensor_copy(kvm[r, c, P + h:P + h + 1], psV[c][r, D:D + 1])
            last.then_inc(s_kvm, 1)
            with link.loop(NB, 4) as b:
                dve.wait_ge(s_qps, b + 1)
                link(nc.vector.tensor_tensor(fk[:, 0, D:2 * D].rearrange("p (c n) -> p c n", c=2), psQ, bc(mb[:, :], 2, P), ALU.add))
                nc.vector.tensor_scalar(fk[:, 0, 0:D], fk[:, 0, D:2 * D], 0.0, None, ALU.min).then_inc(s_qz, 1)
                link(nc.vector.tensor_scalar(fk[:, 1, D:2 * D], fk[:, 0, D:2 * D], 0.0, None, ALU.max))
                dve.wait_ge(s_qexp, b + 1)
                dve.wait_ge(s_ops, b)
                nc.vector.tensor_tensor(qT[:, :, :].rearrange("p c n -> p (c n)"), fk[:, 1, D:2 * D], fk[:, 1, 0:D], ALU.add).then_inc(s_qT, 1)
                dve.wait_ge(s_ops, b + 1)
                link(nc.vector.tensor_scalar(rn[:, :], psM[:, 1, 0:MH], 1e-6, None, ALU.add))
                link(nc.vector.reciprocal(rn[:, :], rn[:, :]))
                dve.wait_ge(s_moT, b)
                nc.vector.tensor_tensor(mo[:, :].rearrange("p (h d) -> p h d", h=MH), psO[:, 0, 0:D].rearrange("p (h d) -> p h d", h=MH),
                                        bc(rn[:, :], 2, MD), ALU.mult).then_inc(s_mo, 1)

        @block.tensor
        def _(pe):
            for d in range(DIRS):
                pe.wait_ge(s_tot, d + 1)
                if d:
                    pe.wait_ge(s_pos, d)
                nc.tensor.matmul(psC[:, 0, 0:KB], before[:, :], tot[:, d, :], start=True, stop=True)
                nc.tensor.matmul(psC[:, 1, 0:KB], ones[:, :], tot[:, d, :], start=True, stop=True).then_inc(s_psC, 1)
            with pe.Fori(0, NB) as b:
                pe.wait_ge(s_xs, b + 1)
                pe.wait_ge(s_xT, b)
                nc.tensor.transpose(psT[:, 0, :], xs[:, 0:P], ident[:, :])
                nc.tensor.transpose(psT[:, 1, :], xs[:, P:D], ident[:, :]).then_inc(s_psT, 1)
            pe.wait_ge(s_wsum, 1)
            pe.wait_ge(s_wqfree, 2)
            with pe.Fori(0, NB) as b:
                pe.wait_ge(s_mask, b * (TYPES + 1) + 1)
                pe.wait_ge(s_kvrow, b)
                nc.tensor.matmul(psK[:, 0:QKV], one_t[:, :], bias[:, :], start=True, stop=False)
                for t in range(TYPES):
                    pe.wait_ge(s_mask, b * (TYPES + 1) + t + 2)
                    nc.tensor.matmul(psK[:, 0:QKV], xm[t % 3][:, 0, :], WK[:, 0, t, :], start=False, stop=False)
                    mm = nc.tensor.matmul(psK[:, 0:QKV], xm[t % 3][:, 1, :], WK[:, 1, t, :], start=False, stop=t == TYPES - 1)
                    mm.then_inc(s_mm, 1)
            pe.wait_ge(s_mw, 16 * 8)
            for b in range(NB):
                rows = P if b < NB - 1 else LAST
                cols = slice(b * P, b * P + P)
                if b:
                    pe.wait_ge(s_vf, b)
                for n in range(2):
                    for c in range(2):
                        nc.tensor.matmul(psM[:, n, :], xnT[:, c, cols], mw[:, 1 + n, c, :], start=c == 0, stop=False)
                    mm = nc.tensor.matmul(psM[:, n, :], ones[0:1, :], mbr[:, n, :], start=False, stop=True)
                mm.then_inc(s_kzps, 1)
                pe.wait_ge(s_vf, b + 1)
                for c in range(2):
                    mm = nc.tensor.matmul(psV[c][:, 0:D + 1], kf[0:rows, c * P:c * P + P], vf[0:rows, :], start=b == 0, stop=b == NB - 1)
                mm.then_inc(s_kf, 1)
            pe.wait_ge(s_kvm, 1)
            with pe.Fori(0, NB) as b:
                cols = bass.ds(b * P, P)
                for m in range(2):
                    for c in range(2):
                        mm = nc.tensor.matmul(psQ[:, m, :], mw[:, 0, c, m * P:m * P + P], xnT[:, c, cols], start=c == 0, stop=c == 1)
                mm.then_inc(s_qps, 1)
                pe.wait_ge(s_qT, b + 1)
                pe.wait_ge(s_mo, b)
                for c in range(2):
                    nc.tensor.matmul(psO[:, 0, c * P:c * P + P], qT[:, c, :], kvm[:, c, 0:P], start=True, stop=True)
                    mm = nc.tensor.matmul(psM[:, 1, c * 4:c * 4 + 4], qT[:, c, :], kvm[:, c, P:P + 4], start=True, stop=True)
                mm.then_inc(s_ops, 1)
                pe.wait_ge(s_mo, b + 1)
                pe.wait_ge(s_moTs, b)
                nc.tensor.transpose(psT[:, 0, :], mo[:, 0:P], ident[:, :])
                nc.tensor.transpose(psT[:, 1, :], mo[:, P:D], ident[:, :]).then_inc(s_moT, 1)
                pe.wait_ge(s_moTs, b + 1)
                pe.wait_ge(s_mrow, b)
                for c in range(2):
                    nc.tensor.matmul(psO[:, 1, 0:D], moT[:, c, :], mw[:, 3, c, :], start=c == 0, stop=False)
                nc.tensor.matmul(psO[:, 1, 0:D], ones[0:1, :], mbr[:, 2, :], start=False, stop=True).then_inc(s_mops, 1)


class Item:

    def __init__(self, c, i=None):
        self.c, self.i = c, i
        self.u = c % BUFS
        self.n = self.count()
        self.j = c // BUFS if i is None else i + c // BUFS

    def exists(self):
        return self.i is not None or 0 <= self.c < NI

    def count(self, plus=0, times=1, gap=0):
        const = (self.c + plus) * times - gap
        return const if self.i is None else self.i * (BUFS * times) + const


def each_item(eng, body):
    for n in range(BUFS):
        body(Item(n))
    with eng.Fori(0, NI // BUFS - 1) as i:
        for u in range(BUFS):
            body(Item(BUFS + u, i))
    for n in range(NI // BUFS * BUFS, NI):
        body(Item(n))


def each_step(eng, body, link=None, per=0, ahead=0):
    for s in range(-2 - ahead, 3):
        body(*(Item(s + k) for k in range(-2, 3 + ahead)))
    count = (NI - 5) // BUFS
    if ahead:
        count -= 1
    loop = link.loop(count, BUFS * per) if link else eng.Fori(0, count)
    with loop as i:
        for m in range(BUFS):
            body(*(Item(3 + m + k, i) for k in range(-2, 3 + ahead)))
    for s in range(3 + BUFS * count, NI + 2):
        body(*(Item(s + k) for k in range(-2, 3 + ahead)))


def wait(eng, sem, value):
    if not isinstance(value, int) or value > 0:
        eng.wait_ge(sem, value)


def messages(nc, a, rec_d, kv_d, agg_d, consts, ident, identb, iota, qtab,
             item_blk, item_qblk, item_row, item_base):
    with ExitStack() as ctx:
        def sb(name, shape, dt=F32):
            return ctx.enter_context(nc.sbuf_tensor(name, shape, dt))

        def ps(name, shape, dt=F32):
            return ctx.enter_context(nc.psum_tensor(name, shape, dt))

        def sem(name):
            return ctx.enter_context(nc.semaphore(name))

        def four(name, shape, dt=F32):
            return [sb(f"{name}{u}", shape, dt) for u in range(BUFS)]

        ROW = TD + 2 * PROJ + TD
        acc = sb("acc", [P, SLOTS, ACCW])
        mstate = sb("mstate", [P, SLOTS, HEADS])
        rec = four("rec", [P, S, REC])
        idx = four("idx", [P, S], I32)
        kv = four("kv", [P, S, ROW])
        ph = four("ph", [P, S, 3, TD])
        fr = four("fr", [P, S, 3, TD])
        oh = [sb(f"oh{u}", [P, S, P]) for u in range(2)]
        ohb = four("ohb", [P, S, P], BF16)
        oht = four("oht", [P, S, P], BF16)
        noht = four("noht", [P, S, P], BF16)
        eq = [sb(f"eq{u}", [P, S, DK]) for u in range(2)]
        pay = four("pay", [P, S, ACCW])
        att = four("att", [P, S, HEADS])
        mnew = four("mnew", [P, HEADS])
        dm = four("dm", [P, HEADS])
        alpha = four("alpha", [P, HEADS])
        qs = sb("qs", [P, S, DK])
        prod = sb("prod", [P, S, HEADS, DK])
        z = sb("z", [P, S, HEADS])
        zpos = sb("zpos", [P, S, HEADS])
        qparts = sb("qparts", [P, NB, PARTS, DK], BF16)
        qrest = sb("qrest", [P, NB, DK])
        mrest = sb("mrest", [P, HEADS])
        mparts = four("mparts", [P, PARTS, HEADS], BF16)
        top = sb("top", [P, HEADS])
        rest = sb("rest", [P, S, HEADS])
        parts = four("parts", [P, S, PARTS * HEADS], BF16)
        attT = sb("attT", [PARTS * HEADS, S, P], BF16)
        selc = sb("selc", [PARTS * HEADS, HEADS])
        sel = sb("sel", [PARTS * HEADS, HEADS, P], BF16)
        wt = sb("wt", [P, 2, TD])
        den = sb("den", [P, SLOTS, HEADS])

        psOT = ps("psOT", [P, 2 * S, P], BF16)[:, 0:S, :]
        psX = ps("psX", [PARTS * HEADS, 2 * S, P], BF16)[:, 0:S, :]
        psB = ps("psB", [P, HEADS, S, P])
        psG = ps("psG", [P, 512])
        psA = ps("psA", [P, 512])
        qg = psG[:, 0:S * DK].rearrange("p (s d) -> p s d", s=S)
        mg = psG[:, S * DK:S * (DK + HEADS)].rearrange("p (s h) -> p s h", s=S)

        s_wt = sem("s_wt")
        s_set = sem("s_set")
        s_dve = sem("s_dve2")
        s_rec = [sem(f"s_rec{u}") for u in range(BUFS)]
        s_kv = [sem(f"s_kv{u}") for u in range(BUFS)]
        s_idx = sem("s_idx")
        s_ph = sem("s_ph")
        s_whole = sem("s_whole")
        s_fr = sem("s_fr")
        s_sin = sem("s_sin")
        s_oh = sem("s_oh")
        s_oh32 = sem("s_oh32")
        s_ot = sem("s_ot")
        s_oht = sem("s_oht")
        s_qg = sem("s_qg")
        s_att = sem("s_att")
        s_x = sem("s_x2")
        s_attT = sem("s_attT")
        s_b = sem("s_b")
        s_part = sem("s_part")
        s_noht = sem("s_noht")
        s_dm = sem("s_dm")
        s_zpos = sem("s_zpos")
        s_m = sem("s_m")
        s_alpha = sem("s_alpha")
        s_mg = sem("s_mg")
        s_z = sem("s_z")
        s_w = sem("s_w2")
        s_pay = sem("s_pay")
        s_agg = sem("s_agg")
        s_acc = sem("s_acc")
        s_sum = sem("s_sum")
        s_out = sem("s_out2")

        block = ctx.enter_context(nc.Block())

        @block.sync
        def _(sp):
            sp.dma_start(wt[:, 0, :], a["L0_gnn_w_time"].rearrange("(o n) -> o n", o=1).broadcast_to([P, TD])).then_inc(s_wt, 16)
            sp.dma_start(wt[:, 1, :], a["L0_gnn_b_time"].rearrange("(o n) -> o n", o=1).broadcast_to([P, TD])).then_inc(s_wt, 16)

            def load(it):
                row = sp.value_load(item_row[0:1, bass.ds(it.n, 1)], min_val=0, max_val=DIRS * DIR_ROWS - ITEM)
                sp.lower_val(row * REC * 4)
                if it.i is not None:
                    sp.lower_val(it.count(-3))
                wait(sp, s_oh, it.count(-3))
                wait(sp, s_idx, it.count(-3))
                sp.dma_start(rec[it.u][:, :, :].rearrange("p s c -> p (s c)"),
                             rec_d[bass.ds(row, ITEM), :].rearrange("(p s) c -> p (s c)", p=P)).then_inc(s_rec[it.u], 16)

            each_item(sp, load)
            sp.wait_ge(s_sum, 2)
            sp.dma_start(agg_d.rearrange("(b p) d -> p b d", p=P), acc[:, 0:NB, 0:D]).then_inc(s_out, 16)
            sp.wait_ge(s_out, 16)

        @block.gpsimd
        def _(pool):
            have_rec = [Tick(pool, s_rec[u], 16, 16, f"have_rec{u}") for u in range(BUFS)]
            have_idx = Tick(pool, s_idx, 1, 1, "have_idx")
            kv_free = Tick(pool, s_pay, 1, 1, "kv_free")
            have_att = Tick(pool, s_att, 1, 1, "have_att")
            have_rest = Tick(pool, s_part, 4, 2, "have_rest")

            def step(old, last, it, nxt, far, ahead):
                if it.exists():
                    u = it.u
                    const = it.i is None
                    hi, mid, lo = (parts[u][:, :, k * HEADS:(k + 1) * HEADS] for k in range(PARTS))
                    have_att(it.c + 1 if const else None)
                    nc.gpsimd.tensor_copy(hi, att[u][:, :, :]).then_inc(s_part, 1)
                    pool.wait_ge(s_part, it.count(1, 4, 3))
                    nc.gpsimd.tensor_tensor(rest[:, :, :], att[u][:, :, :], hi, ALU.subtract).then_inc(s_part, 1)
                    have_rest(it.c * 4 + 2 if const else None)
                    nc.gpsimd.tensor_copy(mid, rest[:, :, :]).then_inc(s_part, 1)
                    pool.wait_ge(s_part, it.count(1, 4, 1))
                    nc.gpsimd.tensor_tensor(lo, rest[:, :, :], mid, ALU.subtract).then_inc(s_part, 1)
                if ahead.exists():
                    v = ahead.u
                    pool.wait_ge(s_rec[v], ahead.j * 16 + 16)
                    if ahead.i is None and ahead.c == 0:
                        pool.wait_ge(s_set, 1)
                    wait(pool, s_fr, ahead.count(-3))
                    nc.gpsimd.tensor_tensor(ph[v][:, :, :, :], bc(rec[v][:, :, 2:5], 3, TD),
                                            bc(bc(wt[:, 0, :], 1, 3), 1, S), ALU.mult).then_inc(s_ph, 1)
                    pool.wait_ge(s_ph, ahead.count(1, 2, 1))
                    nc.gpsimd.tensor_tensor(ph[v][:, :, :, :].rearrange("p s e d -> p (s e) d"), ph[v][:, :, :, :].rearrange("p s e d -> p (s e) d"),
                                            bc(wt[:, 1, :], 1, 3 * S), ALU.add).then_inc(s_ph, 1)
                if far.exists():
                    u = far.u
                    const = far.i is None
                    if not const or far.c >= BUFS:
                        kv_free(far.count(-3) if const else None)
                    have_rec[u](far.j * 16 + 16 if const else None)
                    nc.gpsimd.tensor_copy(idx[u][:, :], rec[u][:, :, 1]).then_inc(s_idx, 1)
                    have_idx(far.c + 1 if const else None)
                    for j in range(S):
                        pool.indirect_dma_start(out=kv[u][:, j, TD:TD + 2 * PROJ], out_offset=None, in_=kv_d,
                                                in_offset=bass.IndirectOffsetOnAxis(ap=idx[u][:, j:j + 1], axis=0)).then_inc(s_kv[u], 16)

            each_step(pool, step, ahead=1)

        @block.scalar
        def _(act):
            act.wait_ge(s_set, 1)

            def step(old, last, it, nxt, far):
                if old.exists():
                    u = old.u
                    act.wait_ge(s_z, old.n + 1)
                    nc.scalar.activation(zpos[:, :, :], z[:, :, :], ACT.Relu).then_inc(s_zpos, 1)
                    weights = pay[u][:, :, 0:PAYW].rearrange("p s (h d) -> p s h d", h=HEADS)[:, :, :, 0]
                    act.wait_ge(s_zpos, old.n + 1)
                    nc.scalar.activation(weights[:, :, 0:HEADS - 1], zpos[:, :, 1:HEADS], ACT.Exp, scale=-SCALE)
                    nc.scalar.activation(weights[:, :, HEADS - 1:HEADS], zpos[:, :, 0:1], ACT.Exp, scale=-SCALE).then_inc(s_w, 1)
                    act.wait_ge(s_dm, old.n + 1)
                    nc.scalar.activation(alpha[u][:, 0:HEADS - 1], dm[u][:, 1:HEADS], ACT.Exp, scale=SCALE)
                    nc.scalar.activation(alpha[u][:, HEADS - 1:HEADS], dm[u][:, 0:1], ACT.Exp, scale=SCALE).then_inc(s_alpha, 1)
                if nxt.exists():
                    u = nxt.u
                    act.wait_ge(s_ot, nxt.n + 1)
                    wait(act, s_mg, nxt.count(-3))
                    nc.scalar.copy(oht[u][:, :, :], psOT).then_inc(s_oht, 1)
                if far.exists():
                    act.wait_ge(s_ph, far.n * 2 + 2)
                    nc.scalar.activation(fr[far.u][:, :, :, :], ph[far.u][:, :, :, :], ACT.Identity, bias=consts[:, 1:2]).then_inc(s_whole, 1)
                if nxt.exists():
                    u = nxt.u
                    wait(act, s_b, nxt.count(-3))
                    nc.scalar.activation(noht[u][:, :, :], psOT, ACT.Identity, bias=consts[:, 2:3], scale=BIG).then_inc(s_noht, 1)
                if last.exists():
                    u = last.u
                    act.wait_ge(s_oh, last.n + 1)
                    wait(act, s_agg, last.count(-1))
                    nc.scalar.copy(oh[u % 2][:, :, :], ohb[u][:, :, :]).then_inc(s_oh32, 1)
                if nxt.exists():
                    u = nxt.u
                    act.wait_ge(s_fr, nxt.n + 1)
                    wait(act, s_pay, nxt.count(-3))
                    wait(act, s_agg, nxt.count(-3))
                    turn = -6.283185
                    kv_ends = kv[u][:, :, :]
                    nc.scalar.activation(kv_ends[:, :, 0:TD], fr[u][:, :, 0, :], ACT.Sin, scale=turn).then_inc(s_sin, 1)
                    nc.scalar.activation(kv_ends[:, :, ROW - TD:ROW], fr[u][:, :, 0, :], ACT.Sin, scale=turn).then_inc(s_sin, 1)
                    nc.scalar.activation(eq[u % 2][:, :, 0:TD], fr[u][:, :, 1, :], ACT.Sin, scale=turn).then_inc(s_sin, 1)
                    nc.scalar.activation(pay[u][:, :, PAYW:ACCW], fr[u][:, :, 2, :], ACT.Sin, scale=turn).then_inc(s_sin, 1)
                if it.exists():
                    act.wait_ge(s_x, it.n + 1)
                    wait(act, s_b, it.n)
                    nc.scalar.copy(attT[:, :, :], psX).then_inc(s_attT, 1)

            each_step(act, step)

        @block.vector
        def _(dve):
            link = Chain(dve, s_dve)
            for u in range(2):
                nc.vector.memset(eq[u][:, :, TD:DK], 0.0)
            nc.vector.memset(mstate[:, :, :], -BIG)
            nc.vector.memset(acc[:, :, :], 0.0)
            link(nc.vector.tensor_reduce(selc[:, :], ident[0:PARTS * HEADS, 0:PARTS * HEADS].rearrange("k (a h) -> k h a", a=PARTS), AX.X, ALU.add))
            nc.vector.tensor_copy(sel[:, :, :], bc(selc[:, :], 2, P))
            dve.wait_ge(s_wt, 32)
            turn = float(1 / (2 * np.pi))
            link(nc.vector.tensor_scalar(wt[:, 0, :], wt[:, 0, :], turn, None, ALU.mult))
            link(nc.vector.tensor_scalar(wt[:, 1, :], wt[:, 1, :], turn, 0.25, ALU.mult, ALU.add))
            link(nc.vector.tensor_copy(qparts[:, :, 0, :], qtab[:, :, :]))
            link(nc.vector.tensor_tensor(qrest[:, :, :], qtab[:, :, :], qparts[:, :, 0, :], ALU.subtract))
            link(nc.vector.tensor_copy(qparts[:, :, 1, :], qrest[:, :, :]))
            nc.vector.tensor_tensor(qparts[:, :, 2, :], qrest[:, :, :], qparts[:, :, 1, :], ALU.subtract).then_inc(s_set, 1)

            def step(old, last, it, nxt, far):
                link.until(link.n)
                if old.exists():
                    dve.wait_ge(s_mg, old.n + 1)
                    nc.vector.tensor_tensor(z[:, :, :], mg, att[old.u][:, :, :], ALU.subtract).then_inc(s_z, 1)
                if it.exists():
                    u = it.u
                    dve.wait_ge(s_qg, it.n + 1)
                    dve.wait_ge(s_sin, it.n * 4 + 4)
                    have_qs = link.post(nc.vector.tensor_tensor(qs[:, :, :], qg, eq[u % 2][:, :, :], ALU.add))
                if far.exists():
                    v = far.u
                    dve.wait_ge(s_rec[v], far.j * 16 + 16)
                    wait(dve, s_oh32, far.count(-3))
                    nc.vector.scalar_tensor_tensor(ohb[v][:, :, :], bc(iota[:, :], 1, S), item_base[:, bass.ds(far.n, 1)],
                                                   bc(rec[v][:, :, 0], 2, P), ALU.add, ALU.is_equal).then_inc(s_oh, 1)
                if it.exists():
                    dve.wait_ge(s_kv[u], it.j * 64 + 64)
                    link.until(have_qs)
                    have_prod = link.post(nc.vector.tensor_tensor(prod[:, :, :, :], kv[u][:, :, 0:VW].rearrange("p s (h d) -> p s h d", h=HEADS),
                                                                  bc(qs[:, :, :], 2, HEADS), ALU.mult))
                    link.until(have_prod)
                    nc.vector.tensor_reduce(att[u][:, :, :], prod[:, :, :, :], AX.X, ALU.add).then_inc(s_att, 1)
                if old.exists():
                    u = old.u
                    dve.wait_ge(s_w, old.n + 1)
                    rows = pay[u][:, :, 0:PAYW].rearrange("p s (h d) -> p s h d", h=HEADS)
                    nc.vector.tensor_tensor(rows[:, :, :, 1:DK + 1], kv[u][:, :, VW:2 * VW].rearrange("p s (h d) -> p s h d", h=HEADS),
                                            rows[:, :, :, 0:1].broadcast_to([P, S, HEADS, DK]), ALU.mult).then_inc(s_pay, 1)
                if last.exists():
                    u = last.u
                    slot = dve.value_load(item_blk[0:1, bass.ds(last.n, 1)], min_val=0, max_val=SLOTS - 1)
                    m = mstate[:, bass.ds(slot, 1), :].rearrange("p b h -> p (b h)")
                    hi, mid, lo = (mparts[u][:, k, :] for k in range(PARTS))
                    dve.wait_ge(s_b, last.n + 1)
                    have_top = link.post(nc.vector.tensor_reduce(top[:, :], psB[:, :, :, :].rearrange("p h s n -> p h (s n)"), AX.X, ALU.max))
                    link.until(have_top)
                    have_new = link.post(nc.vector.tensor_tensor(mnew[u][:, :], m, top[:, :], ALU.max))
                    link.until(have_new)
                    have_hi = link.post(nc.vector.tensor_copy(hi, mnew[u][:, :]))
                if far.exists():
                    dve.wait_ge(s_whole, far.n + 1)
                    nc.vector.scalar_tensor_tensor(fr[v][:, :, :, :], fr[v][:, :, :, :], -MAGIC, ph[v][:, :, :, :], ALU.add, ALU.subtract).then_inc(s_fr, 1)
                if last.exists():
                    link.until(have_hi)
                    have_rest = link.post(nc.vector.tensor_tensor(mrest[:, :], mnew[u][:, :], hi, ALU.subtract))
                    nc.vector.tensor_tensor(dm[u][:, :], m, mnew[u][:, :], ALU.subtract).then_inc(s_dm, 1)
                    link.until(have_rest)
                    have_mid = link.post(nc.vector.tensor_copy(mid, mrest[:, :]))
                if old.exists():
                    w = old.u
                    slot = dve.value_load(item_blk[0:1, bass.ds(old.n, 1)], min_val=0, max_val=SLOTS - 1)
                    row = acc[:, bass.ds(slot, 1), :].rearrange("p b w -> p (b w)")
                    heads = row[:, 0:PAYW].rearrange("p (h d) -> p h d", h=HEADS)
                    dve.wait_ge(s_alpha, old.n + 1)
                    wait(dve, s_acc, old.n)
                    have_scaled = link.post(nc.vector.tensor_tensor(heads, heads, bc(alpha[w][:, :], 2, DK + 1), ALU.mult))
                if last.exists():
                    link.until(have_mid)
                    nc.vector.tensor_tensor(lo, mrest[:, :], mid, ALU.subtract).then_inc(s_m, 1)
                    dve.wait_ge(s_dm, last.n + 1)
                    link.post(nc.vector.tensor_tensor(m, m, top[:, :], ALU.max))
                if old.exists():
                    link.until(have_scaled)
                    dve.wait_ge(s_agg, old.n + 1)
                    nc.vector.tensor_tensor(row, row, psA[:, 0:ACCW], ALU.add).then_inc(s_acc, 1)

            each_step(dve, step, link, 9)
            dve.wait_ge(s_acc, NI)
            heads = acc[:, :, 0:PAYW].rearrange("p b (h d) -> p b h d", h=HEADS)
            link(nc.vector.tensor_scalar(den[:, :, :], heads[:, :, :, 0], 1e-16, None, ALU.add))
            link(nc.vector.reciprocal(den[:, :, :], den[:, :, :]))
            link(nc.vector.tensor_tensor(heads[:, :, :, 1:DK + 1], heads[:, :, :, 1:DK + 1], bc(den[:, :, :], 3, DK), ALU.mult))
            link(nc.vector.tensor_tensor(heads[:, 0:NB, :, 1:DK + 1], heads[:, 0:NB, :, 1:DK + 1], heads[:, NB:SLOTS, :, 1:DK + 1], ALU.add))
            link(nc.vector.tensor_tensor(acc[:, 0:NB, PAYW:ACCW], acc[:, 0:NB, PAYW:ACCW], acc[:, NB:SLOTS, PAYW:ACCW], ALU.add))
            for h in range(HEADS):
                link(nc.vector.tensor_copy(acc[:, NB:SLOTS, h * DK:h * DK + DK], heads[:, 0:NB, h, 1:DK + 1]))
            link(nc.vector.tensor_copy(acc[:, NB:SLOTS, VW:D], acc[:, 0:NB, PAYW:ACCW]))
            nc.vector.tensor_copy(acc[:, 0:NB, 0:D], acc[:, NB:SLOTS, 0:D]).then_inc(s_sum, 2)

        @block.tensor
        def _(pe):
            def step(old, last, it, nxt, far):
                if last.exists():
                    u = last.u
                    pe.wait_ge(s_attT, last.n + 1)
                    pe.wait_ge(s_noht, last.n + 1)
                    wait(pe, s_m, last.n)
                    for h in range(HEADS):
                        nc.tensor.matmul(psB[:, h, :, :], sel[:, h, :], attT[:, :, :], start=True, stop=False)
                        mm = nc.tensor.matmul(psB[:, h, :, :], identb[:, :], noht[u][:, :, :], start=False, stop=True)
                    mm.then_inc(s_b, 1)
                if nxt.exists():
                    u = nxt.u
                    blk = pe.value_load(item_qblk[0:1, bass.ds(nxt.n, 1)], min_val=0, max_val=NB - 1)
                    q = qparts[:, bass.ds(blk, 1), :, :].rearrange("p b k d -> p (b k) d")
                    pe.wait_ge(s_oht, nxt.n + 1)
                    wait(pe, s_att, nxt.n)
                    for j in range(S):
                        for k in range(PARTS):
                            mm = nc.tensor.matmul(qg[:, j, :], oht[u][:, j, :], q[:, k, :], start=k == 0, stop=k == PARTS - 1)
                    mm.then_inc(s_qg, 1)
                if old.exists():
                    u = old.u
                    pe.wait_ge(s_pay, old.n + 1)
                    pe.wait_ge(s_oh32, old.n + 1)
                    wait(pe, s_acc, old.n)
                    for j in range(S):
                        mm = nc.tensor.matmul(psA[:, 0:ACCW], oh[u % 2][:, j, :], pay[u][:, j, :], start=j == 0, stop=j == S - 1)
                    mm.then_inc(s_agg, 1)
                if it.exists():
                    u = it.u
                    pe.wait_ge(s_part, it.n * 4 + 4)
                    wait(pe, s_attT, it.n)
                    for j in range(S):
                        mm = nc.tensor.transpose(psX[:, j, :], parts[u][:, j, :], identb[:, :])
                    mm.then_inc(s_x, 1)
                if last.exists():
                    u = last.u
                    pe.wait_ge(s_m, last.n + 1)
                    for j in range(S):
                        for k in range(PARTS):
                            mm = nc.tensor.matmul(mg[:, j, :], oht[u][:, j, :], mparts[u][:, k, :], start=k == 0, stop=k == PARTS - 1)
                    mm.then_inc(s_mg, 1)
                if far.exists():
                    u = far.u
                    pe.wait_ge(s_oh, far.n + 1)
                    wait(pe, s_noht, far.n)
                    for j in range(S):
                        mm = nc.tensor.transpose(psOT[:, j, :], ohb[u][:, j, :], identb[:, :])
                    mm.then_inc(s_ot, 1)

            pe.wait_ge(s_set, 1)
            each_step(pe, step)


def finish(nc, a, agg_d, mix_d, consts, ident, types, xn, out):
    with ExitStack() as ctx:
        def sb(name, shape, dt=F32):
            return ctx.enter_context(nc.sbuf_tensor(name, shape, dt))

        def ps(name, shape, dt=F32):
            return ctx.enter_context(nc.psum_tensor(name, shape, dt))

        def sem(name):
            return ctx.enter_context(nc.semaphore(name))

        BC = 5
        HALF = BC * P // 2
        CH = NB // BC
        FC = FF // P
        x1 = sb("x1", [P, NB, D])
        mix = sb("mix", [P, NB, D])
        WA = sb("WA", [P, 2, TYPES, D])
        raw = sb("raw", [P, TYPES, D])
        agg = [sb(f"agg{i}", [P, D]) for i in range(2)]
        aggT = sb("aggT", [P, 2, P])
        xm = [sb(f"fm{i}", [P, 2, P]) for i in range(3)]
        rows = sb("rows", [TYPES, 3, D])
        one_t = sb("one_t2", [TYPES, P])
        pidx = sb("pidx2", [P, 1])
        pidx_i = sb("pidx2_i", [P, 1], I32)
        y = sb("y", [P, D])
        bn = sb("bn", [P, 6])
        mv = sb("mv", [P, 2])
        std1 = sb("std1", [P, 1])
        stat = sb("stat3", [P, 3, NB])
        x2T = WA[:, :, :, :].rearrange("p a b c -> p (a b c)")[:, 0:2 * NP].rearrange("p (c n) -> p c n", c=2)
        gw = sb("gw", [P, 2, EXPERTS])
        gb = sb("gb", [1, EXPERTS])
        ones1 = sb("ones1", [1, P])
        lg = sb("lg", [P, NB, EXPERTS])
        l2 = sb("l2", [P, NB, EXPERTS])
        t1 = sb("t1", [P, NB, EXPERTS])
        G = sb("G", [P, NB, EXPERTS])
        ex_i = sb("ex_i", [P, EXPERTS], I32)
        ex = sb("ex", [P, EXPERTS])
        gs = sb("gs", [P, 8, NB])
        b1 = sb("b1", [P, EXPERTS, FC])
        b2 = sb("b2", [EXPERTS, D])
        GT = sb("GT", [EXPERTS, P])
        w1 = [sb(f"w1_{i}", [P, 2, FF]) for i in range(2)]
        w2 = [sb(f"w2_{i}", [P, FC, D]) for i in range(2)]
        h = [sb(f"h{i}", [P, FC, 2, HALF]) for i in range(2)]
        gamma = sb("gamma", [P, D])
        beta = sb("beta", [P, D])

        psT = ps("psT3", [P, 4, P])[:, 0:2, :]
        psY = ps("psY", [P, 512])
        psW = ps("psW", [P, 512])
        psH = [ps(f"psH{i}", [P, 512]) for i in range(3)] + [psW]
        psE = [ps(f"psE{i}", [P, 512]) for i in range(2)]

        names = ("s_x s_mixl s_wa s_rows s_wsum s_iota s_dve3 s_aggT s_aggTs s_mask s_mm s_var s_std s_stage s_blk "
                 "s_tT s_tTs s_lg s_lgs s_g s_gT s_gTs s_gb s_gbs s_small s_h s_hs s_e s_es s_final s_out s_ones s_bn").split()
        q = {n: sem(n + "_f") for n in names}
        s_agg = [sem(f"s_agg_f{i}") for i in range(2)]
        s_ww = [sem(f"s_ww_f{i}") for i in range(2)]
        s_raw = [sem(f"s_raw_f{i}") for i in range(2)]
        block = ctx.enter_context(nc.Block())

        @block.sync
        def _(sp):
            wa = a["L0_gnn_Wa"]
            for kc in range(2):
                sp.dma_start(WA[:, kc, :, :], wa[:, kc * P:kc * P + P, :].rearrange("t i o -> i t o")).then_inc(q["s_wa"], 16)
            sp.dma_start(raw[:, :, :], wa[:, D:D + P, :].rearrange("t i o -> i t o")).then_inc(s_raw[0], 16)
            for n, w in enumerate(("ba", "gamma", "beta")):
                sp.dma_start(rows[:, n, :], a["L0_gnn_" + w]).then_inc(q["s_rows"], 16)
            sp.wait_ge(q["s_ones"], 1)
            sp.dma_start(x1[:, 0:NB - 1, :], a["x"][0:(NB - 1) * P, :].rearrange("(b p) d -> p b d", p=P)).then_inc(q["s_x"], 16)
            sp.dma_start(x1[0:LAST, NB - 1, :], a["x"][(NB - 1) * P:N, :]).then_inc(q["s_x"], 16)
            sp.dma_start(mix[:, :, :], mix_d.rearrange("(b p) d -> p b d", p=P)).then_inc(q["s_mixl"], 16)
            sp.dma_start(gw[:, :, :], a["L0_ffn_gate_w"].rearrange("(c p) e -> p c e", p=P)).then_inc(q["s_small"], 16)
            sp.dma_start(gb[:, :], a["L0_ffn_gate_b"].rearrange("(o e) -> o e", o=1)).then_inc(q["s_small"], 16)
            sp.dma_start(b1[:, :, :], a["L0_ffn_b1"].rearrange("e (c p) -> p e c", p=P), allow_slow_non_contiguous=True).then_inc(q["s_small"], 16)
            sp.dma_start(b2[:, :], a["L0_ffn_b2"]).then_inc(q["s_small"], 16)
            sp.dma_start(gamma[:, :], a["L0_ffn_gamma"].rearrange("(o e) -> o e", o=1).broadcast_to([P, D])).then_inc(q["s_small"], 16)
            sp.dma_start(beta[:, :], a["L0_ffn_beta"].rearrange("(o e) -> o e", o=1).broadcast_to([P, D])).then_inc(q["s_small"], 16)
            sp.wait_ge(q["s_wsum"], 1)
            sp.dma_start(raw[:, :, :], wa[:, D + P:2 * D, :].rearrange("t i o -> i t o")).then_inc(s_raw[1], 16)

            def load_agg(i, b, used):
                sp.lower_val(b * P * D * 4)
                wait(sp, q["s_aggT"], used)
                sp.dma_start(agg[i][:, :], agg_d[bass.ds(b * P, P), :]).then_inc(s_agg[i], 16)
            load_agg(0, 0, 0)
            with sp.Fori(0, NB // 2) as b:
                load_agg(1, b * 2 + 1, b * 2)
                load_agg(0, b * 2 + 2, b * 2 + 1)

            def load_expert(i, e):
                sp.dma_start(w1[i][:, :, :], a["L0_ffn_w1"][bass.ds(e, 1), :, :].rearrange("o (c p) f -> p (o c) f", p=P)).then_inc(s_ww[i], 16)
                sp.dma_start(w2[i][:, :, :], a["L0_ffn_w2"][bass.ds(e, 1), :, :].rearrange("o (c p) f -> p (o c) f", p=P)).then_inc(s_ww[i], 16)
            load_expert(0, 0)
            load_expert(1, 1)
            with sp.Fori(0, EXPERTS // 2 - 1) as g:
                for i in range(2):
                    e = g * 2 + (2 + i)
                    sp.lower_val(e * D * FF * 4)
                    sp.wait_ge(q["s_e"], g * (2 * NB) + (1 + i) * NB)
                    load_expert(i, e)
            sp.wait_ge(q["s_final"], 1)
            sp.dma_start(out[0:(NB - 1) * P, :].rearrange("(b p) d -> p b d", p=P), x1[:, 0:NB - 1, :]).then_inc(q["s_out"], 16)
            sp.dma_start(out[(NB - 1) * P:N, :], x1[0:LAST, NB - 1, :]).then_inc(q["s_out"], 16)
            sp.wait_ge(q["s_out"], 32)

        @block.gpsimd
        def _(pool):
            nc.gpsimd.iota(pidx_i[:, :], pattern=[[0, 1]], base=0, channel_multiplier=1).then_inc(q["s_iota"], 1)
            nc.gpsimd.iota(ex_i[:, :], pattern=[[1, EXPERTS]], base=0, channel_multiplier=0).then_inc(q["s_iota"], 1)

        @block.scalar
        def _(act):
            with act.Fori(0, NB) as b:
                act.wait_ge(q["s_aggT"], b + 1)
                act.wait_ge(q["s_mask"], b * (TYPES + 1))
                nc.scalar.copy(aggT[:, :, :], psT).then_inc(q["s_aggTs"], 1)
                act.wait_ge(q["s_var"], b + 1)
                nc.scalar.activation(std1[:, :], mv[:, 1:2], ACT.Sqrt, bias=consts[:, 0:1]).then_inc(q["s_std"], 1)
            act.wait_ge(q["s_var"], NB + 1)
            nc.scalar.activation(stat[:, 2, :], stat[:, 1, :], ACT.Sqrt, bias=consts[:, 0:1], scale=1.0 / D).then_inc(q["s_std"], 1)
            turned = Tick(act, q["s_tT"], 1, 1, "turned2")
            with act.Fori(0, NB) as b:
                turned()
                nc.scalar.copy(x2T[:, :, bass.ds(b * P, P)], psT).then_inc(q["s_tTs"], 1)
            act.wait_ge(q["s_g"], 1)
            nc.scalar.activation(gs[:, 3, :], gs[:, 2, :], ACT.Exp).then_inc(q["s_g"], 1)
            with act.Fori(0, NB) as b:
                act.wait_ge(q["s_gT"], b + 1)
                nc.scalar.copy(GT[:, :], psY[0:EXPERTS, 0:P]).then_inc(q["s_gTs"], 1)
            hidden = Tick(act, q["s_h"], 1, 1, "hidden")
            with act.Fori(0, EXPERTS // 2) as g:
                for k in range(2 * CH):
                    n = g * (2 * CH) + k
                    for m in range(FC * 2):
                        hidden()
                        nc.scalar.activation(h[k % 2][:, m // 2, m % 2, :], psH[m % 4][:, 0:HALF], ACT.Relu,
                                             bias=b1[:, bass.ds(g * 2 + k // CH, 1), m // 2]).then_inc(q["s_hs"], 1)
            act.wait_ge(q["s_var"], NB + 2)
            nc.scalar.activation(stat[:, 2, :], stat[:, 1, :], ACT.Sqrt, bias=consts[:, 0:1], scale=1.0 / D).then_inc(q["s_std"], 1)

        @block.vector
        def _(dve):
            link = Chain(dve, q["s_dve3"])
            link(nc.vector.memset(ones1[:, :], 1.0))
            nc.vector.memset(x1[:, NB - 1, :], 0.0).then_inc(q["s_ones"], 1)
            dve.wait_ge(q["s_iota"], 2)
            nc.vector.tensor_copy(pidx[:, :], pidx_i[:, :])
            nc.vector.tensor_copy(ex[:, :], ex_i[:, :])
            dve.wait_ge(q["s_wa"], 32)
            for kc in range(2):
                dve.wait_ge(s_raw[kc], 16)
                nc.vector.tensor_tensor(WA[:, kc, :, :], WA[:, kc, :, :], raw[:, :, :], ALU.add).then_inc(q["s_wsum"], 1)
            dve.wait_ge(q["s_x"], 32)
            dve.wait_ge(q["s_mixl"], 16)
            link(nc.vector.tensor_tensor(x1[:, :, :], x1[:, :, :], mix[:, :, :], ALU.add))
            have_bn = Tick(dve, q["s_bn"], 1, 1, "have_bn")
            with link.loop(NB, 5) as b:
                cols = bass.ds(b * P, P)
                dve.wait_ge(q["s_mm"], b * TYPES)
                nc.vector.tensor_scalar(one_t[:, :], types[0:TYPES, cols], pidx[0:TYPES, :], None, ALU.is_equal).then_inc(q["s_mask"], 1)
                dve.wait_ge(q["s_aggTs"], b + 1)
                for t in range(TYPES):
                    dve.wait_ge(q["s_mm"], b * TYPES + max(t - 2, 0))
                    nc.vector.scalar_tensor_tensor(xm[t % 3][:, :, :], bc(types[:, cols], 1, 2), float(t), aggT[:, :, :],
                                                   ALU.is_equal, ALU.mult).then_inc(q["s_mask"], 1)
                dve.wait_ge(q["s_mm"], b * TYPES + TYPES)
                link(nc.vector.tensor_tensor(y[:, :], psY[:, 0:D], xn[:, bass.ds(b, 1), :].rearrange("p b d -> p (b d)"), ALU.add))
                nc.vector.bn_stats(bn[:, :], y[:, :]).then_inc(q["s_bn"], 1)
                have_bn()
                nc.vector.bn_aggr(mv[:, :], bn[:, :]).then_inc(q["s_var"], 1)
                dve.wait_ge(q["s_std"], b + 1)
                link(nc.vector.reciprocal(std1[:, :], std1[:, :]))
                link(nc.vector.tensor_scalar(y[:, :], y[:, :], mv[:, 0:1], std1[:, :], ALU.subtract, ALU.mult))
                link(nc.vector.tensor_tensor(y[:, :], y[:, :], psW[:, 0:D], ALU.mult))
                link(nc.vector.tensor_tensor(y[:, :], y[:, :], psW[:, D:2 * D], ALU.add))
                row = x1[:, bass.ds(b, 1), :].rearrange("p b d -> p (b d)")
                nc.vector.tensor_tensor(row, row, y[:, :], ALU.add).then_inc(q["s_blk"], 1)
            dve.wait_ge(q["s_blk"], NB)
            layer_norm(nc, link, None, x1[:, :, :], mix[:, :, :], xn[:, :, :], stat[:, 0, :], stat[:, 1, :], stat[:, 2, :],
                       q["s_var"], q["s_std"], NB + 1)
            with dve.Fori(0, NB) as b:
                dve.wait_ge(q["s_tT"], b)
                nc.vector.tensor_copy(y[:, :], xn[:, bass.ds(b, 1), :].rearrange("p b d -> p (b d)")).then_inc(q["s_stage"], 1)
            dve.wait_ge(q["s_lg"], 1)
            link(nc.vector.tensor_copy(lg[:, :, :], psH[0][:, 0:NB * EXPERTS].rearrange("p (b e) -> p b e", e=EXPERTS)))
            exb = bc(ex[:, :], 1, NB)

            def first_best(src, best, number, hot):
                link(nc.vector.tensor_reduce(best, src, AX.X, ALU.max))
                link(nc.vector.tensor_tensor(t1[:, :, :], src, bc(best, 2, EXPERTS), ALU.is_equal))
                link(nc.vector.tensor_scalar(t1[:, :, :], t1[:, :, :], -100.0, 100.0, ALU.mult, ALU.add))
                link(nc.vector.tensor_tensor(t1[:, :, :], t1[:, :, :], exb, ALU.add))
                link(nc.vector.tensor_reduce(number, t1[:, :, :], AX.X, ALU.min))
                link(nc.vector.tensor_tensor(hot, exb, bc(number, 2, EXPERTS), ALU.is_equal))
            first_best(lg[:, :, :], gs[:, 0, :], gs[:, 1, :], G[:, :, :])
            link(nc.vector.scalar_tensor_tensor(l2[:, :, :], G[:, :, :], -BIG, lg[:, :, :], ALU.mult, ALU.add))
            first_best(l2[:, :, :], gs[:, 4, :], gs[:, 5, :], lg[:, :, :])
            nc.vector.tensor_tensor(gs[:, 2, :], gs[:, 4, :], gs[:, 0, :], ALU.subtract).then_inc(q["s_g"], 1)
            dve.wait_ge(q["s_g"], 2)
            link(nc.vector.tensor_scalar(gs[:, 6, :], gs[:, 3, :], 1.0, None, ALU.add))
            link(nc.vector.reciprocal(gs[:, 6, :], gs[:, 6, :]))
            link(nc.vector.tensor_tensor(gs[:, 7, :], gs[:, 3, :], gs[:, 6, :], ALU.mult))
            link(nc.vector.tensor_tensor(G[:, :, :], G[:, :, :], bc(gs[:, 6, :], 2, EXPERTS), ALU.mult))
            link(nc.vector.tensor_tensor(lg[:, :, :], lg[:, :, :], bc(gs[:, 7, :], 2, EXPERTS), ALU.mult))
            link(nc.vector.tensor_tensor(G[:, :, :], G[:, :, :], lg[:, :, :], ALU.add))
            with link.loop(NB, 1) as b:
                dve.wait_ge(q["s_gT"], b)
                nc.vector.tensor_copy(t1[:, 0, :], G[:, bass.ds(b, 1), :].rearrange("p b e -> p (b e)")).then_inc(q["s_stage"], 1)
                dve.wait_ge(q["s_gb"], b + 1)
                link(nc.vector.tensor_tensor(mix[:, bass.ds(b, 1), :].rearrange("p b d -> p (b d)"), psW[:, 0:D],
                                             xn[:, bass.ds(b, 1), :].rearrange("p b d -> p (b d)"), ALU.add))
                nc.vector.memset(y[:, 0:1], 0.0).then_inc(q["s_gbs"], 1)
            with dve.Fori(0, EXPERTS // 2) as g:
                for k in range(2 * CH):
                    n = g * (2 * CH) + k
                    for b in range(BC):
                        m = k * BC + b
                        blk = (k % CH) * BC + b
                        dve.wait_ge(q["s_es"], n * BC + b)
                        dve.wait_ge(q["s_e"], n * BC + b + 1)
                        nc.vector.scalar_tensor_tensor(mix[:, blk, :], psE[m % 2][:, 0:D], G[:, blk, bass.ds(g * 2 + k // CH, 1)],
                                                       mix[:, blk, :], ALU.mult, ALU.add).then_inc(q["s_es"], 1)
            dve.wait_ge(q["s_es"], EXPERTS * NB)
            layer_norm(nc, link, None, mix[:, :, :], xn[:, :, :], mix[:, :, :], stat[:, 0, :], stat[:, 1, :], stat[:, 2, :],
                       q["s_var"], q["s_std"], NB + 2)
            link(nc.vector.tensor_tensor(mix[:, :, :], mix[:, :, :], bc(gamma[:, :], 1, NB), ALU.mult))
            link(nc.vector.tensor_tensor(mix[:, :, :], mix[:, :, :], bc(beta[:, :], 1, NB), ALU.add))
            nc.vector.tensor_tensor(x1[:, :, :], x1[:, :, :], mix[:, :, :], ALU.add).then_inc(q["s_final"], 1)

        @block.tensor
        def _(pe):
            pe.wait_ge(q["s_wsum"], 2)
            pe.wait_ge(q["s_rows"], 48)

            def project(i, b, turn):
                pe.wait_ge(s_agg[i], turn)
                pe.wait_ge(q["s_aggTs"], b)
                nc.tensor.transpose(psT[:, 0, :], agg[i][:, 0:P], ident[:, :])
                nc.tensor.transpose(psT[:, 1, :], agg[i][:, P:D], ident[:, :]).then_inc(q["s_aggT"], 1)
                pe.wait_ge(q["s_mask"], b * (TYPES + 1) + 1)
                pe.wait_ge(q["s_blk"], b)
                nc.tensor.matmul(psY[:, 0:D], one_t[:, :], rows[:, 0, :], start=True, stop=False)
                nc.tensor.matmul(psW[:, :], one_t[:, :], rows[:, 1:3, :].rearrange("t a d -> t (a d)"), start=True, stop=True)
                for t in range(TYPES):
                    pe.wait_ge(q["s_mask"], b * (TYPES + 1) + t + 2)
                    nc.tensor.matmul(psY[:, 0:D], xm[t % 3][:, 0, :], WA[:, 0, t, :], start=False, stop=False)
                    nc.tensor.matmul(psY[:, 0:D], xm[t % 3][:, 1, :], WA[:, 1, t, :], start=False, stop=t == TYPES - 1).then_inc(q["s_mm"], 1)
            project(0, 0, 16)
            with pe.Fori(0, NB // 2) as b:
                project(1, b * 2 + 1, b * 16 + 16)
                project(0, b * 2 + 2, b * 16 + 32)
            with pe.Fori(0, NB) as b:
                pe.wait_ge(q["s_stage"], b + 1)
                pe.wait_ge(q["s_tTs"], b)
                nc.tensor.transpose(psT[:, 0, :], y[:, 0:P], ident[:, :])
                nc.tensor.transpose(psT[:, 1, :], y[:, P:D], ident[:, :]).then_inc(q["s_tT"], 1)
            pe.wait_ge(q["s_tTs"], NB)
            pe.wait_ge(q["s_small"], 96)
            for b in range(NB):
                o = psH[0][:, b * EXPERTS:(b + 1) * EXPERTS]
                for c in range(2):
                    nc.tensor.matmul(o, x2T[:, c, b * P:b * P + P], gw[:, c, :], start=c == 0, stop=False)
                mm = nc.tensor.matmul(o, ones1[:, :], gb[:, :], start=False, stop=True)
            mm.then_inc(q["s_lg"], 1)
            with pe.Fori(0, NB) as b:
                pe.wait_ge(q["s_stage"], b + NB + 1)
                pe.wait_ge(q["s_gTs"], b)
                nc.tensor.transpose(psY[0:EXPERTS, 0:P], t1[:, 0, :], ident[:, :]).then_inc(q["s_gT"], 1)
                pe.wait_ge(q["s_gTs"], b + 1)
                pe.wait_ge(q["s_gbs"], b)
                nc.tensor.matmul(psW[:, 0:D], GT[:, :], b2[:, :], start=True, stop=True).then_inc(q["s_gb"], 1)
            pe.wait_ge(q["s_gbs"], NB)
            with pe.Fori(0, EXPERTS // 2) as g:
                for k in range(2 * CH):
                    n = g * (2 * CH) + k
                    i, c = k // CH, k % CH
                    if c == 0:
                        pe.wait_ge(s_ww[i], g * 32 + 32)
                    for m in range(FC * 2):
                        f, half = m // 2, m % 2
                        pe.wait_ge(q["s_hs"], g * (2 * CH * FC * 2) + max(k * FC * 2 + m - 3, 0))
                        lo = c * BC * P + half * HALF
                        for kc in range(2):
                            mm = nc.tensor.matmul(psH[m % 4][:, 0:HALF], w1[i][:, kc, f * P:f * P + P], x2T[:, kc, lo:lo + HALF], start=kc == 0, stop=kc == 1)
                        mm.then_inc(q["s_h"], 1)
                    pe.wait_ge(q["s_hs"], n * (FC * 2) + FC * 2)
                    for b in range(BC):
                        m = k * BC + b
                        pe.wait_ge(q["s_es"], g * (2 * CH * BC) + max(m - 1, 0))
                        rows_h = h[k % 2][:, :, :, :].rearrange("p c a n -> p c (a n)")
                        for f in range(FC):
                            mm = nc.tensor.matmul(psE[m % 2][:, 0:D], rows_h[:, f, b * P:b * P + P], w2[i][:, f, :], start=f == 0, stop=f == FC - 1)
                        mm.then_inc(q["s_e"], 1)


_INS = ("x", "src", "dst", "edge_attr_5", "node_type_19",
        "L0_gnn_Wk", "L0_gnn_bk", "L0_gnn_Wq", "L0_gnn_bq", "L0_gnn_Wv", "L0_gnn_bv", "L0_gnn_Wa", "L0_gnn_ba",
        "L0_gnn_gamma", "L0_gnn_beta", "L0_gnn_w_time", "L0_gnn_b_time",
        "L0_mix_wq", "L0_mix_bq", "L0_mix_wk", "L0_mix_bk", "L0_mix_wv", "L0_mix_bv", "L0_mix_wo", "L0_mix_bo",
        "L0_ffn_gate_w", "L0_ffn_gate_b", "L0_ffn_w1", "L0_ffn_b1", "L0_ffn_w2", "L0_ffn_b2", "L0_ffn_gamma", "L0_ffn_beta")


def kernel(**inputs):
    import numpy as _np
    import concourse.bacc as _bacc
    from concourse import mybir as _mybir
    from concourse.bass_utils import run_bass_kernel_spmd as _run

    nc = _bacc.Bacc("TRN2", target_bir_lowering=False, num_devices=1)
    arrays, args = {}, {}
    for name in _INS:
        v = _np.ascontiguousarray(inputs[name])
        arrays[f"in_{name}_dram"] = v
        args[name] = nc.dram_tensor(f"in_{name}_dram", v.shape, _mybir.dt.from_np(v.dtype), kind="ExternalInput").ap()
    out = nc.dram_tensor("out_0_dram", (N, D), F32, kind="ExternalOutput").ap()
    build(nc, args, out)
    r = _run(nc, [arrays], core_ids=[0])
    return r.results[0]["out_0_dram"]
```

```python
from contextlib import ExitStack, contextmanager

import numpy as np

import concourse.bass as bass
from concourse import mybir

F32 = mybir.dt.float32
BF16 = mybir.dt.bfloat16
I32 = mybir.dt.int32
ALU = mybir.AluOpType
ACT = mybir.ActivationFunctionType
AX = mybir.AxisListType

P = 128
N = 3125
D = 256
NB = (N + P - 1) // P
NP = NB * P
LAST = N - (NB - 1) * P
E = 103125
ET = (E + P - 1) // P
EP = ET * P
ELAST = E - (P - 1) * ET
TYPES = 19
TD = 32
PROJ = 192
HEADS = 4
DK = 56
VW = HEADS * DK
QKV = 2 * PROJ + DK
S = 4
ITEM = S * P
GUARD = ITEM
DIR_ROWS = EP + GUARD
DIRS = 2
REC = 5
NI = E // ITEM * DIRS + NB * DIRS
BUFS = 4
NI += (5 - NI) % BUFS
SLOTS = NB * DIRS
PAYW = HEADS * (DK + 1)
ACCW = PAYW + TD
TABLE_ROWS = NP + P
BIG = 2.0 ** 100
PARTS = 3
MAGIC = 12582912.0
SCALE = 1.0 / float(np.sqrt(DK))
EPS = 1e-5
CHUNK = 13
EXPERTS = 16
FF = 512
FC = FF // P
TOP = 2
NT = (TOP * NP + EXPERTS * (P - 1)) // P
NT += NT % 2
TT = (NP + TYPES * (P - 1)) // P
TT += TT % 2
MH = 8
MD = D // MH


class Chain:

    def __init__(self, eng, sem):
        self.eng, self.sem, self.n, self.term = eng, sem, 0, 0

    def __call__(self, ins):
        ins.then_inc(self.sem, 1)
        self.n += 1
        self.eng.wait_ge(self.sem, self.term + self.n)

    def post(self, ins):
        ins.then_inc(self.sem, 1)
        self.n += 1
        return self.n

    def until(self, n):
        if n:
            self.eng.wait_ge(self.sem, self.term + n)

    @contextmanager
    def loop(self, count, per):
        start = self.n
        with self.eng.Fori(0, count) as i:
            self.term = i * per
            yield i
            assert self.n - start == per, (self.n - start, per)
        self.n, self.term = start + per * count, 0


class Tick:

    def __init__(self, eng, sem, step, first, name):
        self.eng, self.sem, self.step = eng, sem, step
        self.reg = eng.alloc_register(name)
        eng.reg_mov(self.reg, first)

    def __call__(self, value=None):
        self.eng.wait_ge(self.sem, self.reg if value is None else value)
        self.eng.reg_add(self.reg, self.reg, self.step)


def bc(ap, axis, count):
    shape = list(ap.shape)
    shape.insert(axis, count)
    return ap.unsqueeze(axis).broadcast_to(shape)


def layer_norm(nc, link, act, src, sq, out, mean, var, std, s_var, s_std, turn):
    link(nc.vector.tensor_reduce(mean, src, AX.X, ALU.add))
    link(nc.vector.tensor_scalar(mean, mean, -1.0 / D, None, ALU.mult))
    link(nc.vector.tensor_tensor(out, src, bc(mean, 2, D), ALU.add))
    link(nc.vector.tensor_tensor(sq, out, out, ALU.mult))
    nc.vector.tensor_reduce(var, sq, AX.X, ALU.add).then_inc(s_var, 1)
    link.eng.wait_ge(s_std, turn)
    link(nc.vector.reciprocal(std, std))
    link(nc.vector.tensor_tensor(out, out, bc(std, 2, D), ALU.mult))


def build(nc, a, out):
    with ExitStack() as whole:
        def keep(name, shape, dt=F32):
            return whole.enter_context(nc.sbuf_tensor(name, shape, dt))

        rec_d = nc.dram_tensor("records", [DIRS * DIR_ROWS, REC], F32, kind="Internal").ap()
        kv_d = nc.dram_tensor("kv_table", [TABLE_ROWS, 2 * PROJ], F32, kind="Internal").ap()
        mix_d = nc.dram_tensor("mix_rows", [NP, D], F32, kind="Internal").ap()
        agg_d = nc.dram_tensor("agg_rows", [NP, D], F32, kind="Internal").ap()
        x1_d = nc.dram_tensor("residual_rows", [NP, D], F32, kind="Internal").ap()
        typed_d = nc.dram_tensor("typed_rows", [TT * P, D], F32, kind="Internal").ap()
        typed_out_d = nc.dram_tensor("typed_out_rows", [TT * P, D], F32, kind="Internal").ap()
        sent_d = nc.dram_tensor("sent_rows", [NT * P, D], F32, kind="Internal").ap()
        back_d = nc.dram_tensor("back_rows", [NT * P, D], F32, kind="Internal").ap()

        consts = keep("consts", [P, 4])
        ident = keep("ident", [P, P])
        identb = keep("identb", [P, P], BF16)
        iota = keep("iota", [P, P])
        types = keep("types", [P, NP])
        xn = keep("xn", [P, NB, D])
        with ExitStack() as edges:
            def hold(name, shape, dt=F32):
                return edges.enter_context(nc.sbuf_tensor(name, shape, dt))

            qtab = hold("qtab", [P, NB, DK])
            item_blk = hold("item_blk", [P, NI], I32)
            item_qblk = hold("item_qblk", [P, NI], I32)
            item_row = hold("item_row", [P, NI], I32)
            item_base = hold("item_base", [P, NI])
            prepare(nc, a, rec_d, kv_d, mix_d, typed_d, consts, ident, identb, iota, qtab,
                    item_blk, item_qblk, item_row, item_base, types, xn)
            messages(nc, a, rec_d, kv_d, agg_d, consts, ident, identb, iota, qtab,
                     item_blk, item_qblk, item_row, item_base)
        share = keep("share", [P, TOP, NB])
        place = keep("place", [P, TOP, NB], I32)
        tile_e = keep("tile_e", [P, NT])
        tile_ei = keep("tile_ei", [P, NT], I32)
        project(nc, a, agg_d, mix_d, x1_d, typed_d, typed_out_d, sent_d, consts, ident, iota, types, xn, share, place, tile_e, tile_ei)
        experts(nc, a, x1_d, sent_d, back_d, consts, ident, xn, share, place, tile_e, tile_ei, out)


def prepare(nc, a, rec_d, kv_d, mix_d, typed_d, consts, ident, identb, iota, qtab,
            item_blk, item_qblk, item_row, item_base, types, xn):
    with ExitStack() as ctx:
        def sb(name, shape, dt=F32):
            return ctx.enter_context(nc.sbuf_tensor(name, shape, dt))

        def ps(name, shape, dt=F32):
            return ctx.enter_context(nc.psum_tensor(name, shape, dt))

        def sem(name):
            return ctx.enter_context(nc.semaphore(name))

        work = sb("work", [P, 2, ET])
        ends_i = work[:, :, :].bitcast(I32)
        ends = sb("ends", [P, 2, ET])
        logs = sb("logs", [P, 3, ET])
        key = sb("key", [P, ET])
        mask = sb("mask", [P, ET], I32)
        scan, rank = work[:, 0, :], work[:, 1, :]
        pos = sb("pos", [P, 2, ET], I32)
        KB = NB + 1
        tot = sb("tot", [P, DIRS, KB])
        base = sb("base", [P, KB])
        sums = sb("sums", [P, DIRS, KB])
        small = sb("small", [P, 8, SLOTS])
        small_i = sb("small_i", [P, SLOTS], I32)
        items = work[:, :, :].rearrange("p a t -> p (a t)")[:, 0:3 * NI].rearrange("p (a n) -> p a n", a=3)
        item_n = sb("item_n", [P, NI])
        item_ni = sb("item_ni", [P, NI], I32)
        before = sb("before", [P, P])
        ones = sb("ones", [P, P])
        stage = [sb(f"stage{i}", [P, CHUNK, REC]) for i in range(2)]
        spos = [sb(f"spos{i}", [P, CHUNK], I32) for i in range(2)]
        guard = sb("guard", [P, S, REC])

        stat = sb("stat", [P, 3, NB])
        xnT = sb("xnT", [P, 2, NP])
        xs = sb("xs", [P, D])
        WK = sb("WK", [P, 2, TYPES, QKV])
        wq_raw = sb("wq_raw", [P, TYPES, PROJ])
        types_i = xnT[:, 0, :].bitcast(I32)
        attr = wq_raw[:, :, :].rearrange("p a b -> p (a b)")
        bias = sb("bias", [TYPES, QKV])
        bq_raw = sb("bq_raw", [TYPES, PROJ])
        one_t = sb("one_t", [TYPES, P])
        pidx = sb("pidx", [P, 1])
        pidx_i = sb("pidx_i", [P, 1], I32)
        iota_i = sb("iota_i", [P, P], I32)
        xm = [sb(f"xm{i}", [P, 2, P]) for i in range(3)]
        kv_row = sb("kv_row", [P, 2 * PROJ])
        place = [0]

        def carve(shape, rows=P):
            size = int(np.prod(shape))
            lo, place[0] = place[0], place[0] + size
            v = WK[:, :, :, :].rearrange("p a b c -> p (a b c)")[0:rows, lo:lo + size]
            names = "abc"[:len(shape)]
            return v.rearrange(f"p ({' '.join(names)}) -> p {' '.join(names)}", **dict(zip(names, shape)))

        mw = carve([4, 2, D])
        mb = carve([2])
        mbr = carve([3, D], 1)
        fk = carve([2, 2 * D])
        kf = carve([D])
        vf = carve([D + 1])
        kvm = carve([2, P + 4])
        qT = carve([2, P])
        mo = carve([D])
        moT = carve([2, P])
        mrow = carve([D])
        rn = sb("rn", [P, MH])

        psT = ps("psT", [P, 4, P])[:, 0:2, :]
        psK = ps("psK", [P, 512])
        psC = ps("psC", [P, 2, 256])
        psM = ps("psM", [P, 2, D])
        psV = [ps(f"psV{i}", [P, 512]) for i in range(2)]
        psQ = ps("psQ", [P, 4, P])[:, 0:2, :]
        psO = ps("psO", [P, 2, 256])

        kv_zero = kv_row[:, :]

        s_clear = sem("s_clear")
        s_zero = sem("s_zero")
        s_x = sem("s_x")
        s_ends = sem("s_ends")
        s_attr = sem("s_attr")
        s_types = sem("s_types")
        s_w = sem("s_w")
        s_mw = sem("s_mw")
        s_wq = [sem(f"s_wq{i}") for i in range(2)]
        s_wqfree = sem("s_wqfree")
        s_iota = sem("s_iota")
        s_dve = sem("s_dve")
        s_var = sem("s_var")
        s_std = sem("s_std")
        s_log = sem("s_log")
        s_tot = sem("s_tot")
        s_psC = sem("s_psC")
        s_pos = sem("s_pos")
        s_guard = sem("s_guard")
        s_gout = sem("s_gout")
        s_copied = sem("s_copied")
        s_scat = [sem(f"s_scat{i}") for i in range(2)]
        s_xs = sem("s_xs")
        s_psT = sem("s_psT")
        s_xT = sem("s_xT")
        s_mask = sem("s_mask")
        s_mm = sem("s_mm")
        s_kvrow = sem("s_kvrow")
        s_kvout = sem("s_kvout")
        s_wsum = sem("s_wsum")
        s_kz = sem("s_kz")
        s_kzps = sem("s_kzps")
        s_kexp = sem("s_kexp")
        s_kf = sem("s_kf")
        s_vf = sem("s_vf")
        s_kvm = sem("s_kvm")
        s_qps = sem("s_qps")
        s_qz = sem("s_qz")
        s_qexp = sem("s_qexp")
        s_qT = sem("s_qT")
        s_ops = sem("s_ops")
        s_mo = sem("s_mo")
        s_moT = sem("s_moT")
        s_moTs = sem("s_moTs")
        s_mrow = sem("s_mrow")
        s_mout = sem("s_mout")
        s_mops = sem("s_mops")

        block = ctx.enter_context(nc.Block())

        @block.sync
        def _(sp):
            sp.wait_ge(s_clear, 4)
            for n, end in enumerate(("src", "dst")):
                v = a[end]
                sp.dma_start(ends_i[0:P - 1, n, :], v[0:(P - 1) * ET].rearrange("(p t) -> p t", t=ET)).then_inc(s_ends, 16)
                sp.dma_start(ends_i[P - 1:P, n, 0:ELAST], v[(P - 1) * ET:E].rearrange("(o t) -> o t", o=1)).then_inc(s_ends, 16)
            sp.dma_start(xn[:, 0:NB - 1, :], a["x"][0:(NB - 1) * P, :].rearrange("(b p) d -> p b d", p=P)).then_inc(s_x, 16)
            sp.dma_start(xn[0:LAST, NB - 1, :], a["x"][(NB - 1) * P:N, :]).then_inc(s_x, 16)
            attr_d = a["edge_attr_5"]
            at = WK[:, :, :, :].rearrange("p a b c -> p (a b c)")[:, 0:ET * 5]
            sp.dma_start(at[0:P - 1, :], attr_d[0:(P - 1) * ET, :].rearrange("(p t) c -> p (t c)", t=ET)).then_inc(s_attr, 16)
            sp.dma_start(at[P - 1:P, 0:ELAST * 5], attr_d[(P - 1) * ET:E, :].rearrange("(o t) c -> o (t c)", o=1)).then_inc(s_attr, 16)
            sp.dma_start(types_i[:, 0:N], a["node_type_19"].rearrange("(o n) -> o n", o=1).broadcast_to([P, N])).then_inc(s_types, 16)
            sp.wait_ge(s_log, 1)
            for kc in range(2):
                sp.dma_start(WK[:, kc, :, 0:PROJ], a["L0_gnn_Wk"][:, kc * P:kc * P + P, :].rearrange("t i o -> i t o")).then_inc(s_w, 16)
                sp.dma_start(WK[:, kc, :, PROJ:2 * PROJ], a["L0_gnn_Wv"][:, kc * P:kc * P + P, :].rearrange("t i o -> i t o")).then_inc(s_w, 16)
            sp.dma_start(bias[:, 0:PROJ], a["L0_gnn_bk"]).then_inc(s_w, 16)
            sp.dma_start(bias[:, PROJ:2 * PROJ], a["L0_gnn_bv"]).then_inc(s_w, 16)
            sp.dma_start(bq_raw[:, :], a["L0_gnn_bq"]).then_inc(s_w, 16)
            for kc in range(2):
                if kc:
                    sp.wait_ge(s_wqfree, 1)
                sp.dma_start(wq_raw[:, :, :], a["L0_gnn_Wq"][:, kc * P:kc * P + P, :].rearrange("t i o -> i t o")).then_inc(s_wq[kc], 16)
            sp.wait_ge(s_guard, 2)
            sp.wait_ge(s_zero, 1)
            for d in range(DIRS):
                sp.dma_start(rec_d[d * DIR_ROWS + EP:(d + 1) * DIR_ROWS, :].rearrange("(p s) c -> p (s c)", p=P),
                             guard[:, :, :].rearrange("p s c -> p (s c)")).then_inc(s_gout, 16)
            sp.dma_start(kv_d[NP:TABLE_ROWS, :], kv_zero).then_inc(s_gout, 16)
            sp.dma_start(typed_d.rearrange("(t p) d -> p t d", p=P), bc(kv_zero[:, 0:D], 1, TT)).then_inc(s_gout, 16)
            sp.wait_ge(s_gout, 64)
            sp.wait_ge(s_mm, NB * TYPES)
            for n, w in enumerate(("wq", "wk", "wv", "wo")):
                sp.dma_start(mw[:, n, :, :], a["L0_mix_" + w].rearrange("(c p) o -> p c o", p=P)).then_inc(s_mw, 16)
            sp.dma_start(mb[:, :], a["L0_mix_bq"].rearrange("(c p) -> p c", p=P), allow_slow_non_contiguous=True).then_inc(s_mw, 16)
            for n, w in enumerate(("bk", "bv", "bo")):
                sp.dma_start(mbr[:, n, :], a["L0_mix_" + w].rearrange("(o d) -> o d", o=1)).then_inc(s_mw, 16)

        @block.gpsimd
        def _(pool):
            nc.gpsimd.memset(ident[:, :], 0.0).then_inc(s_iota, 1)
            nc.gpsimd.memset(before[:, :], 1.0).then_inc(s_iota, 1)
            pool.wait_ge(s_iota, 2)
            nc.gpsimd.affine_select(out=ident[:, :], in_=ident[:, :], compare_op=ALU.not_equal, fill=1.0, base=0,
                                    pattern=[[-1, P]], channel_multiplier=1).then_inc(s_iota, 1)
            nc.gpsimd.affine_select(out=before[:, :], in_=before[:, :], compare_op=ALU.is_ge, fill=0.0, base=-1,
                                    pattern=[[1, P]], channel_multiplier=-1).then_inc(s_iota, 1)
            nc.gpsimd.iota(iota_i[:, :], pattern=[[1, P]], base=0, channel_multiplier=0).then_inc(s_iota, 1)
            nc.gpsimd.iota(pidx_i[:, :], pattern=[[0, 1]], base=0, channel_multiplier=1).then_inc(s_iota, 1)
            nc.gpsimd.iota(item_ni[:, :], pattern=[[1, NI]], base=0, channel_multiplier=0).then_inc(s_iota, 1)
            nc.gpsimd.memset(guard[:, :, :], 0.0).then_inc(s_guard, 1)
            pool.wait_ge(s_guard, 1)
            nc.gpsimd.memset(guard[:, :, 0:1], float(NP)).then_inc(s_guard, 1)
            chunks = ET // CHUNK
            pool.wait_ge(s_log, 1)
            ncopy = Tick(pool, s_copied, 6, 6, "copied")
            nscat = [Tick(pool, s_scat[u], 16 * CHUNK, 16 * CHUNK, f"scattered{u}") for u in range(2)]
            for d in range(DIRS):
                pool.wait_ge(s_pos, d + 1)
                centre, other = (1, 0) if d == 0 else (0, 1)
                cols = [(0, ends[:, centre, :]), (1, ends[:, other, :]), (2, logs[:, 1 + d, :]),
                        (3, logs[:, 2 - d, :]), (4, logs[:, 0, :])]

                def fill(u, c, first):
                    if not first:
                        nscat[u]()
                    for n, v in cols:
                        nc.gpsimd.tensor_copy(stage[u][:, :, n], v[:, bass.ds(c * CHUNK, CHUNK)]).then_inc(s_copied, 1)
                    nc.gpsimd.tensor_copy(spos[u][:, :], pos[:, d, bass.ds(c * CHUNK, CHUNK)]).then_inc(s_copied, 1)
                    ncopy()
                    for t in range(CHUNK):
                        pool.indirect_dma_start(
                            out=rec_d, out_offset=bass.IndirectOffsetOnAxis(ap=spos[u][:, t:t + 1], axis=0),
                            in_=stage[u][:, t, :], in_offset=None).then_inc(s_scat[u], 16)

                if d == 0:
                    fill(0, 0, True)
                    fill(1, 1, True)
                with pool.Fori(1 if d == 0 else 0, chunks // 2) as i:
                    for u in range(2):
                        fill(u, i * 2 + u, False)
            for u in range(2):
                nscat[u]()

        @block.scalar
        def _(act):
            act.wait_ge(s_attr, 32)
            at = WK[:, :, :, :].rearrange("p a b c -> p (a b c)")[:, 0:ET * 5].rearrange("p (t c) -> p c t", c=5)
            act.wait_ge(s_clear, 5)
            nc.scalar.activation(logs[:, :, :], at[:, 0:3, :], ACT.Ln, bias=1.0).then_inc(s_log, 1)
            act.wait_ge(s_var, 1)
            nc.scalar.activation(stat[:, 2, :], stat[:, 1, :], ACT.Sqrt, bias=consts[:, 0:1], scale=1.0 / D).then_inc(s_std, 1)
            turned = Tick(act, s_psT, 1, 1, "turned")
            with act.Fori(0, NB) as b:
                turned()
                nc.scalar.copy(xnT[:, :, bass.ds(b * P, P)], psT).then_inc(s_xT, 1)
            act.wait_ge(s_gout, 64)
            with act.Fori(0, NB) as b:
                act.wait_ge(s_mm, b * TYPES + TYPES)
                act.wait_ge(s_kvout, b * 16)
                lo = DK - TD
                nc.scalar.copy(kv_row[:, 0:lo], psK[:, 3 * DK:PROJ])
                kk = kv_row[:, lo:PROJ].rearrange("p (h d) -> p h d", h=3)
                kp = psK[:, 0:3 * DK].rearrange("p (h d) -> p h d", h=3)
                nc.scalar.copy(kk[:, :, 0:TD], kp[:, :, lo:DK])
                nc.scalar.copy(kk[:, :, TD:DK], kp[:, :, 0:lo])
                nc.scalar.copy(kv_row[:, PROJ:2 * PROJ], psK[:, PROJ:2 * PROJ])
                nc.scalar.copy(qtab[:, bass.ds(b, 1), 0:TD], psK[:, 2 * PROJ + lo:QKV].unsqueeze(1))
                nc.scalar.copy(qtab[:, bass.ds(b, 1), TD:DK], psK[:, 2 * PROJ:2 * PROJ + lo].unsqueeze(1)).then_inc(s_kvrow, 1)
                act.wait_ge(s_kvrow, b + 1)
                act.dma_start(kv_d[bass.ds(b * P, P), :], kv_row[:, :]).then_inc(s_kvout, 16)
            act.wait_ge(s_kvout, NB * 16)
            with act.Fori(0, NB) as b:
                act.wait_ge(s_kz, b + 1)
                nc.scalar.activation(fk[:, 1, 0:D], fk[:, 0, 0:D], ACT.Exp).then_inc(s_kexp, 1)
            with act.Fori(0, NB) as b:
                act.wait_ge(s_qz, b + 1)
                nc.scalar.activation(fk[:, 1, 0:D], fk[:, 0, 0:D], ACT.Exp).then_inc(s_qexp, 1)
                act.wait_ge(s_moT, b + 1)
                nc.scalar.copy(moT[:, :, :], psT).then_inc(s_moTs, 1)
                act.wait_ge(s_mops, b + 1)
                act.wait_ge(s_mout, b * 16)
                nc.scalar.copy(mrow[:, :], psO[:, 1, 0:D]).then_inc(s_mrow, 1)
                act.wait_ge(s_mrow, b + 1)
                act.dma_start(mix_d[bass.ds(b * P, P), :], mrow[:, :]).then_inc(s_mout, 16)
            act.wait_ge(s_mout, NB * 16)

        @block.vector
        def _(dve):
            link = Chain(dve, s_dve)
            at = WK[:, :, :, :].rearrange("p a b c -> p (a b c)")[:, 0:ET * 5]
            nc.vector.memset(at, 0.0).then_inc(s_clear, 1)
            nc.vector.memset(xn[:, NB - 1, :], 0.0).then_inc(s_clear, 1)
            nc.vector.memset(ends_i, NP).then_inc(s_clear, 1)
            nc.vector.memset(xnT[:, 0, :].bitcast(I32), -1).then_inc(s_clear, 1)
            for n, v in enumerate((EPS, MAGIC, -BIG, 1.0)):
                nc.vector.memset(consts[:, n:n + 1], v)
            nc.vector.memset(kv_zero, 0.0).then_inc(s_zero, 1)
            link(nc.vector.memset(ones[:, :], 1.0))
            nc.vector.memset(consts[:, 3:4], 1.0).then_inc(s_clear, 1)
            dve.wait_ge(s_iota, 7)
            nc.vector.tensor_copy(iota[:, :], iota_i[:, :])
            nc.vector.tensor_copy(pidx[:, :], pidx_i[:, :])
            nc.vector.tensor_copy(item_n[:, :], item_ni[:, :])
            link(nc.vector.tensor_copy(identb[:, :], ident[:, :]))
            dve.wait_ge(s_ends, 64)
            link(nc.vector.tensor_copy(ends[:, :, :], ends_i))

            for d in range(DIRS):
                centre = 1 - d
                link(nc.vector.tensor_copy(mask[:, :], ends[:, centre, :]))
                link(nc.vector.tensor_scalar(mask[:, :], mask[:, :], 7, None, ALU.arith_shift_right))
                link(nc.vector.tensor_copy(key[:, :], mask[:, :]))
                for k in range(KB):
                    link(nc.vector.tensor_scalar(mask[:, :], key[:, :], float(k), None, ALU.is_equal))
                    link(nc.vector.tensor_tensor_scan(scan, mask[:, :], mask[:, :], 0.0, ALU.add, ALU.max))
                    last = nc.vector.tensor_copy(tot[:, d, k:k + 1], scan[:, ET - 1:ET])
                    if k == KB - 1:
                        last.then_inc(s_tot, 1)
                    link(nc.vector.copy_predicated(rank, mask[:, :], scan) if k else
                         nc.vector.tensor_copy(rank, scan))
                dve.wait_ge(s_psC, d + 1)
                link(nc.vector.tensor_copy(sums[:, d, :], psC[:, 1, 0:KB]))
                first = small[:, 0, 0:KB]
                link(nc.vector.memset(first[:, 0:1], float(d * DIR_ROWS - 1)))
                for k in range(1, KB):
                    link(nc.vector.tensor_tensor(first[:, k:k + 1], first[:, k - 1:k], sums[:, d, k - 1:k], ALU.add))
                link(nc.vector.tensor_scalar(small[:, 1, d * NB:d * NB + NB], first[:, 0:NB], 1.0, None, ALU.add))
                link(nc.vector.tensor_tensor(base[:, :], first, psC[:, 0, 0:KB], ALU.add))
                for k in range(KB):
                    link(nc.vector.tensor_scalar(scan, key[:, :], float(k), base[:, k:k + 1], ALU.is_equal, ALU.mult))
                    link(nc.vector.tensor_tensor(rank, rank, scan, ALU.add))
                nc.vector.tensor_copy(pos[:, d, :], rank).then_inc(s_pos, 1)

            start = small[:, 1, :]
            link(nc.vector.tensor_copy(small[:, 2, :].rearrange("p (d k) -> p d k", d=DIRS), sums[:, :, 0:NB]))
            link(nc.vector.tensor_scalar(small[:, 2, :], small[:, 2, :], float(ITEM - 1), None, ALU.add))
            link(nc.vector.tensor_copy(small_i[:, :], small[:, 2, :]))
            link(nc.vector.tensor_scalar(small_i[:, :], small_i[:, :], int(np.log2(ITEM)), None, ALU.arith_shift_right))
            link(nc.vector.tensor_copy(small[:, 3, :], small_i[:, :]))
            link(nc.vector.tensor_tensor_scan(small[:, 4, :], small[:, 3, :], small[:, 3, :], 0.0, ALU.add, ALU.max))
            past = small[:, 4, :]
            link(nc.vector.tensor_tensor(small[:, 5, :], past, small[:, 3, :], ALU.subtract))
            link(nc.vector.tensor_scalar(small[:, 5, :], small[:, 5, :], -float(ITEM), None, ALU.mult))
            link(nc.vector.tensor_tensor(small[:, 5, :], small[:, 5, :], start, ALU.add))
            link(nc.vector.tensor_tensor(small[:, 6, 0:SLOTS - 1], small[:, 5, 1:SLOTS], small[:, 5, 0:SLOTS - 1], ALU.subtract))
            link(nc.vector.tensor_scalar(small[:, 7, 0:1], past[:, SLOTS - 1:SLOTS], -float(ITEM), float(DIRS * DIR_ROWS - GUARD), ALU.mult, ALU.add))
            link(nc.vector.tensor_tensor(small[:, 6, SLOTS - 1:SLOTS], small[:, 7, 0:1], small[:, 5, SLOTS - 1:SLOTS], ALU.subtract))
            link(nc.vector.tensor_scalar(items[:, 0, :], item_n[:, :], float(ITEM), small[:, 5, 0:1], ALU.mult, ALU.add))
            link(nc.vector.memset(items[:, 1, :], 0.0))
            for k in range(SLOTS):
                link(nc.vector.tensor_scalar(items[:, 2, :], item_n[:, :], past[:, k:k + 1], small[:, 6, k:k + 1], ALU.is_ge, ALU.mult))
                nc.vector.tensor_tensor(items[:, 0, :], items[:, 0, :], items[:, 2, :], ALU.add)
                link(nc.vector.scalar_tensor_tensor(items[:, 1, :], item_n[:, :], past[:, k:k + 1], items[:, 1, :], ALU.is_ge, ALU.add))
            link(nc.vector.tensor_scalar(items[:, 0, :], items[:, 0, :], float(DIRS * DIR_ROWS - GUARD), None, ALU.min))
            link(nc.vector.tensor_scalar(items[:, 1, :], items[:, 1, :], float(SLOTS - 1), None, ALU.min))
            link(nc.vector.tensor_scalar(items[:, 2, :], items[:, 1, :], float(NB), -float(NB), ALU.is_ge, ALU.mult))
            link(nc.vector.tensor_tensor(items[:, 2, :], items[:, 2, :], items[:, 1, :], ALU.add))
            nc.vector.tensor_copy(item_row[:, :], items[:, 0, :])
            nc.vector.tensor_copy(item_blk[:, :], items[:, 1, :])
            nc.vector.tensor_copy(item_qblk[:, :], items[:, 2, :])
            link(nc.vector.tensor_scalar(item_base[:, :], items[:, 2, :], float(P), None, ALU.mult))

            dve.wait_ge(s_types, 16)
            link(nc.vector.tensor_copy(types[:, :], types_i))
            dve.wait_ge(s_x, 32)
            layer_norm(nc, link, None, xn[:, :, :], xnT[:, :, :].rearrange("p c n -> p (c n)").rearrange("p (b d) -> p b d", d=D),
                       xn[:, :, :], stat[:, 0, :], stat[:, 1, :], stat[:, 2, :], s_var, s_std, 1)
            with dve.Fori(0, NB) as b:
                dve.wait_ge(s_psT, b)
                nc.vector.tensor_copy(xs[:, :], xn[:, bass.ds(b, 1), :].rearrange("p b d -> p (b d)")).then_inc(s_xs, 1)

            def head_sum(dst, src):
                link(nc.vector.tensor_tensor(dst, src[..., 0:DK], src[..., DK:2 * DK], ALU.add))
                link(nc.vector.tensor_tensor(dst, dst, src[..., 2 * DK:3 * DK], ALU.add))
                link(nc.vector.tensor_tensor(dst[..., 0:PROJ - 3 * DK], dst[..., 0:PROJ - 3 * DK], src[..., 3 * DK:PROJ], ALU.add))
            for kc in range(2):
                dve.wait_ge(s_wq[kc], 16)
                head_sum(WK[:, kc, :, 2 * PROJ:QKV], wq_raw[:, :, :])
                nc.vector.memset(rn[:, :], 0.0).then_inc(s_wqfree, 1)
            dve.wait_ge(s_w, 16 * 7)
            head_sum(bias[:, 2 * PROJ:QKV], bq_raw[:, :])
            nc.vector.memset(rn[:, :], 0.0).then_inc(s_wsum, 1)

            dve.wait_ge(s_xT, NB)
            with dve.Fori(0, NB) as b:
                cols = bass.ds(b * P, P)
                dve.wait_ge(s_mm, b * TYPES)
                nc.vector.tensor_scalar(one_t[:, :], types[0:TYPES, cols], pidx[0:TYPES, :], None, ALU.is_equal).then_inc(s_mask, 1)
                for t in range(TYPES):
                    dve.wait_ge(s_mm, b * TYPES + max(t - 2, 0))
                    nc.vector.scalar_tensor_tensor(xm[t % 3][:, :, :], bc(types[:, cols], 1, 2), float(t), xnT[:, :, cols],
                                                   ALU.is_equal, ALU.mult).then_inc(s_mask, 1)

            dve.wait_ge(s_mm, NB * TYPES)
            dve.wait_ge(s_mw, 16 * 8)
            nc.vector.memset(vf[:, D:D + 1], 1.0)
            link(nc.vector.memset(kvm[:, :, :], 0.0))
            with link.loop(NB, 1) as b:
                dve.wait_ge(s_kzps, b + 1)
                nc.vector.tensor_scalar(fk[:, 0, 0:D], psM[:, 0, :], 0.0, None, ALU.min).then_inc(s_kz, 1)
                dve.wait_ge(s_kf, b)
                nc.vector.tensor_copy(vf[:, 0:D], psM[:, 1, :])
                link(nc.vector.tensor_scalar(kf[:, :], psM[:, 0, :], 0.0, None, ALU.max))
                dve.wait_ge(s_kexp, b + 1)
                nc.vector.tensor_tensor(kf[:, :], kf[:, :], fk[:, 1, 0:D], ALU.add).then_inc(s_vf, 1)
            dve.wait_ge(s_kf, NB)
            for c in range(2):
                for h in range(4):
                    r = slice(h * MD, h * MD + MD)
                    nc.vector.tensor_copy(kvm[r, c, h * MD:h * MD + MD], psV[c][r, c * P + h * MD:c * P + h * MD + MD])
                    last = nc.vector.tensor_copy(kvm[r, c, P + h:P + h + 1], psV[c][r, D:D + 1])
            last.then_inc(s_kvm, 1)
            with link.loop(NB, 4) as b:
                dve.wait_ge(s_qps, b + 1)
                link(nc.vector.tensor_tensor(fk[:, 0, D:2 * D].rearrange("p (c n) -> p c n", c=2), psQ, bc(mb[:, :], 2, P), ALU.add))
                nc.vector.tensor_scalar(fk[:, 0, 0:D], fk[:, 0, D:2 * D], 0.0, None, ALU.min).then_inc(s_qz, 1)
                link(nc.vector.tensor_scalar(fk[:, 1, D:2 * D], fk[:, 0, D:2 * D], 0.0, None, ALU.max))
                dve.wait_ge(s_qexp, b + 1)
                dve.wait_ge(s_ops, b)
                nc.vector.tensor_tensor(qT[:, :, :].rearrange("p c n -> p (c n)"), fk[:, 1, D:2 * D], fk[:, 1, 0:D], ALU.add).then_inc(s_qT, 1)
                dve.wait_ge(s_ops, b + 1)
                link(nc.vector.tensor_scalar(rn[:, :], psM[:, 1, 0:MH], 1e-6, None, ALU.add))
                link(nc.vector.reciprocal(rn[:, :], rn[:, :]))
                dve.wait_ge(s_moT, b)
                nc.vector.tensor_tensor(mo[:, :].rearrange("p (h d) -> p h d", h=MH), psO[:, 0, 0:D].rearrange("p (h d) -> p h d", h=MH),
                                        bc(rn[:, :], 2, MD), ALU.mult).then_inc(s_mo, 1)

        @block.tensor
        def _(pe):
            for d in range(DIRS):
                pe.wait_ge(s_tot, d + 1)
                if d:
                    pe.wait_ge(s_pos, d)
                nc.tensor.matmul(psC[:, 0, 0:KB], before[:, :], tot[:, d, :], start=True, stop=True)
                nc.tensor.matmul(psC[:, 1, 0:KB], ones[:, :], tot[:, d, :], start=True, stop=True).then_inc(s_psC, 1)
            with pe.Fori(0, NB) as b:
                pe.wait_ge(s_xs, b + 1)
                pe.wait_ge(s_xT, b)
                nc.tensor.transpose(psT[:, 0, :], xs[:, 0:P], ident[:, :])
                nc.tensor.transpose(psT[:, 1, :], xs[:, P:D], ident[:, :]).then_inc(s_psT, 1)
            pe.wait_ge(s_wsum, 1)
            pe.wait_ge(s_wqfree, 2)
            with pe.Fori(0, NB) as b:
                pe.wait_ge(s_mask, b * (TYPES + 1) + 1)
                pe.wait_ge(s_kvrow, b)
                nc.tensor.matmul(psK[:, 0:QKV], one_t[:, :], bias[:, :], start=True, stop=False)
                for t in range(TYPES):
                    pe.wait_ge(s_mask, b * (TYPES + 1) + t + 2)
                    nc.tensor.matmul(psK[:, 0:QKV], xm[t % 3][:, 0, :], WK[:, 0, t, :], start=False, stop=False)
                    mm = nc.tensor.matmul(psK[:, 0:QKV], xm[t % 3][:, 1, :], WK[:, 1, t, :], start=False, stop=t == TYPES - 1)
                    mm.then_inc(s_mm, 1)
            pe.wait_ge(s_mw, 16 * 8)
            for b in range(NB):
                rows = P if b < NB - 1 else LAST
                cols = slice(b * P, b * P + P)
                if b:
                    pe.wait_ge(s_vf, b)
                for n in range(2):
                    for c in range(2):
                        nc.tensor.matmul(psM[:, n, :], xnT[:, c, cols], mw[:, 1 + n, c, :], start=c == 0, stop=False)
                    mm = nc.tensor.matmul(psM[:, n, :], ones[0:1, :], mbr[:, n, :], start=False, stop=True)
                mm.then_inc(s_kzps, 1)
                pe.wait_ge(s_vf, b + 1)
                for c in range(2):
                    mm = nc.tensor.matmul(psV[c][:, 0:D + 1], kf[0:rows, c * P:c * P + P], vf[0:rows, :], start=b == 0, stop=b == NB - 1)
                mm.then_inc(s_kf, 1)
            pe.wait_ge(s_kvm, 1)
            with pe.Fori(0, NB) as b:
                cols = bass.ds(b * P, P)
                for m in range(2):
                    for c in range(2):
                        mm = nc.tensor.matmul(psQ[:, m, :], mw[:, 0, c, m * P:m * P + P], xnT[:, c, cols], start=c == 0, stop=c == 1)
                mm.then_inc(s_qps, 1)
                pe.wait_ge(s_qT, b + 1)
                pe.wait_ge(s_mo, b)
                for c in range(2):
                    nc.tensor.matmul(psO[:, 0, c * P:c * P + P], qT[:, c, :], kvm[:, c, 0:P], start=True, stop=True)
                    mm = nc.tensor.matmul(psM[:, 1, c * 4:c * 4 + 4], qT[:, c, :], kvm[:, c, P:P + 4], start=True, stop=True)
                mm.then_inc(s_ops, 1)
                pe.wait_ge(s_mo, b + 1)
                pe.wait_ge(s_moTs, b)
                nc.tensor.transpose(psT[:, 0, :], mo[:, 0:P], ident[:, :])
                nc.tensor.transpose(psT[:, 1, :], mo[:, P:D], ident[:, :]).then_inc(s_moT, 1)
                pe.wait_ge(s_moTs, b + 1)
                pe.wait_ge(s_mrow, b)
                for c in range(2):
                    nc.tensor.matmul(psO[:, 1, 0:D], moT[:, c, :], mw[:, 3, c, :], start=c == 0, stop=False)
                nc.tensor.matmul(psO[:, 1, 0:D], ones[0:1, :], mbr[:, 2, :], start=False, stop=True).then_inc(s_mops, 1)


class Item:

    def __init__(self, c, i=None):
        self.c, self.i = c, i
        self.u = c % BUFS
        self.n = self.count()
        self.j = c // BUFS if i is None else i + c // BUFS

    def exists(self):
        return self.i is not None or 0 <= self.c < NI

    def count(self, plus=0, times=1, gap=0):
        const = (self.c + plus) * times - gap
        return const if self.i is None else self.i * (BUFS * times) + const


def each_item(eng, body):
    for n in range(BUFS):
        body(Item(n))
    with eng.Fori(0, NI // BUFS - 1) as i:
        for u in range(BUFS):
            body(Item(BUFS + u, i))
    for n in range(NI // BUFS * BUFS, NI):
        body(Item(n))


def each_step(eng, body, link=None, per=0, ahead=0):
    for s in range(-2 - ahead, 3):
        body(*(Item(s + k) for k in range(-2, 3 + ahead)))
    count = (NI - 5) // BUFS
    if ahead:
        count -= 1
    loop = link.loop(count, BUFS * per) if link else eng.Fori(0, count)
    with loop as i:
        for m in range(BUFS):
            body(*(Item(3 + m + k, i) for k in range(-2, 3 + ahead)))
    for s in range(3 + BUFS * count, NI + 2):
        body(*(Item(s + k) for k in range(-2, 3 + ahead)))


def wait(eng, sem, value):
    if not isinstance(value, int) or value > 0:
        eng.wait_ge(sem, value)


def messages(nc, a, rec_d, kv_d, agg_d, consts, ident, identb, iota, qtab,
             item_blk, item_qblk, item_row, item_base):
    with ExitStack() as ctx:
        def sb(name, shape, dt=F32):
            return ctx.enter_context(nc.sbuf_tensor(name, shape, dt))

        def ps(name, shape, dt=F32):
            return ctx.enter_context(nc.psum_tensor(name, shape, dt))

        def sem(name):
            return ctx.enter_context(nc.semaphore(name))

        def four(name, shape, dt=F32):
            return [sb(f"{name}{u}", shape, dt) for u in range(BUFS)]

        ROW = TD + 2 * PROJ + TD
        acc = sb("acc", [P, SLOTS, ACCW])
        mstate = sb("mstate", [P, SLOTS, HEADS])
        rec = four("rec", [P, S, REC])
        idx = four("idx", [P, S], I32)
        kv = four("kv", [P, S, ROW])
        ph = four("ph", [P, S, 3, TD])
        fr = four("fr", [P, S, 3, TD])
        oh = [sb(f"oh{u}", [P, S, P]) for u in range(2)]
        ohb = four("ohb", [P, S, P], BF16)
        oht = four("oht", [P, S, P], BF16)
        noht = four("noht", [P, S, P], BF16)
        eq = [sb(f"eq{u}", [P, S, DK]) for u in range(2)]
        pay = four("pay", [P, S, ACCW])
        att = four("att", [P, S, HEADS])
        mnew = four("mnew", [P, HEADS])
        dm = four("dm", [P, HEADS])
        alpha = four("alpha", [P, HEADS])
        qs = sb("qs", [P, S, DK])
        prod = sb("prod", [P, S, HEADS, DK])
        z = sb("z", [P, S, HEADS])
        zpos = sb("zpos", [P, S, HEADS])
        qparts = sb("qparts", [P, NB, PARTS, DK], BF16)
        qrest = sb("qrest", [P, NB, DK])
        mrest = sb("mrest", [P, HEADS])
        mparts = four("mparts", [P, PARTS, HEADS], BF16)
        top = sb("top", [P, HEADS])
        rest = sb("rest", [P, S, HEADS])
        parts = four("parts", [P, S, PARTS * HEADS], BF16)
        attT = sb("attT", [PARTS * HEADS, S, P], BF16)
        selc = sb("selc", [PARTS * HEADS, HEADS])
        sel = sb("sel", [PARTS * HEADS, HEADS, P], BF16)
        wt = sb("wt", [P, 2, TD])
        den = sb("den", [P, SLOTS, HEADS])

        psOT = ps("psOT", [P, 2 * S, P], BF16)[:, 0:S, :]
        psX = ps("psX", [PARTS * HEADS, 2 * S, P], BF16)[:, 0:S, :]
        psB = ps("psB", [P, HEADS, S, P])
        psG = ps("psG", [P, 512])
        psA = ps("psA", [P, 512])
        qg = psG[:, 0:S * DK].rearrange("p (s d) -> p s d", s=S)
        mg = psA[:, ACCW:ACCW + S * HEADS].rearrange("p (s h) -> p s h", s=S)

        s_wt = sem("s_wt")
        s_set = sem("s_set")
        s_dve = sem("s_dve2")
        s_rec = [sem(f"s_rec{u}") for u in range(BUFS)]
        s_kv = [sem(f"s_kv{u}") for u in range(BUFS)]
        s_idx = sem("s_idx")
        s_ph = sem("s_ph")
        s_whole = sem("s_whole")
        s_fr = sem("s_fr")
        s_sin = sem("s_sin")
        s_oh = sem("s_oh")
        s_oh32 = sem("s_oh32")
        s_ot = sem("s_ot")
        s_oht = sem("s_oht")
        s_qg = sem("s_qg")
        s_att = sem("s_att")
        s_x = sem("s_x2")
        s_attT = sem("s_attT")
        s_b = sem("s_b")
        s_part = sem("s_part")
        s_noht = sem("s_noht")
        s_dm = sem("s_dm")
        s_zpos = sem("s_zpos")
        s_m = sem("s_m")
        s_alpha = sem("s_alpha")
        s_mg = sem("s_mg")
        s_z = sem("s_z")
        s_w = sem("s_w2")
        s_pay = sem("s_pay")
        s_agg = sem("s_agg")
        s_acc = sem("s_acc")
        s_sum = sem("s_sum")
        s_out = sem("s_out2")

        block = ctx.enter_context(nc.Block())

        @block.sync
        def _(sp):
            sp.dma_start(wt[:, 0, :], a["L0_gnn_w_time"].rearrange("(o n) -> o n", o=1).broadcast_to([P, TD])).then_inc(s_wt, 16)
            sp.dma_start(wt[:, 1, :], a["L0_gnn_b_time"].rearrange("(o n) -> o n", o=1).broadcast_to([P, TD])).then_inc(s_wt, 16)

            def load(it):
                row = sp.value_load(item_row[0:1, bass.ds(it.n, 1)], min_val=0, max_val=DIRS * DIR_ROWS - ITEM)
                sp.lower_val(row * REC * 4)
                if it.i is not None:
                    sp.lower_val(it.count(-3))
                wait(sp, s_oh, it.count(-3))
                wait(sp, s_idx, it.count(-3))
                sp.dma_start(rec[it.u][:, :, :].rearrange("p s c -> p (s c)"),
                             rec_d[bass.ds(row, ITEM), :].rearrange("(p s) c -> p (s c)", p=P)).then_inc(s_rec[it.u], 16)

            each_item(sp, load)
            sp.wait_ge(s_sum, 2)
            sp.dma_start(agg_d.rearrange("(b p) d -> p b d", p=P), acc[:, 0:NB, 0:D]).then_inc(s_out, 16)
            sp.wait_ge(s_out, 16)

        @block.gpsimd
        def _(pool):
            have_rec = [Tick(pool, s_rec[u], 16, 16, f"have_rec{u}") for u in range(BUFS)]
            have_idx = Tick(pool, s_idx, 1, 1, "have_idx")
            kv_free = Tick(pool, s_pay, 1, 1, "kv_free")
            have_att = Tick(pool, s_att, 1, 1, "have_att")
            have_rest = Tick(pool, s_part, 4, 2, "have_rest")

            def step(old, last, it, nxt, far, ahead):
                if it.exists():
                    u = it.u
                    const = it.i is None
                    hi, mid, lo = (parts[u][:, :, k * HEADS:(k + 1) * HEADS] for k in range(PARTS))
                    have_att(it.c + 1 if const else None)
                    nc.gpsimd.tensor_copy(hi, att[u][:, :, :]).then_inc(s_part, 1)
                    pool.wait_ge(s_part, it.count(1, 4, 3))
                    nc.gpsimd.tensor_tensor(rest[:, :, :], att[u][:, :, :], hi, ALU.subtract).then_inc(s_part, 1)
                    have_rest(it.c * 4 + 2 if const else None)
                    nc.gpsimd.tensor_copy(mid, rest[:, :, :]).then_inc(s_part, 1)
                    pool.wait_ge(s_part, it.count(1, 4, 1))
                    nc.gpsimd.tensor_tensor(lo, rest[:, :, :], mid, ALU.subtract).then_inc(s_part, 1)
                if ahead.exists():
                    v = ahead.u
                    pool.wait_ge(s_rec[v], ahead.j * 16 + 16)
                    if ahead.i is None and ahead.c == 0:
                        pool.wait_ge(s_set, 1)
                    wait(pool, s_fr, ahead.count(-3))
                    nc.gpsimd.tensor_tensor(ph[v][:, :, :, :], bc(rec[v][:, :, 2:5], 3, TD),
                                            bc(bc(wt[:, 0, :], 1, 3), 1, S), ALU.mult).then_inc(s_ph, 1)
                    pool.wait_ge(s_ph, ahead.count(1, 2, 1))
                    nc.gpsimd.tensor_tensor(ph[v][:, :, :, :].rearrange("p s e d -> p (s e) d"), ph[v][:, :, :, :].rearrange("p s e d -> p (s e) d"),
                                            bc(wt[:, 1, :], 1, 3 * S), ALU.add).then_inc(s_ph, 1)
                if far.exists():
                    u = far.u
                    const = far.i is None
                    if not const or far.c >= BUFS:
                        kv_free(far.count(-3) if const else None)
                    have_rec[u](far.j * 16 + 16 if const else None)
                    nc.gpsimd.tensor_copy(idx[u][:, :], rec[u][:, :, 1]).then_inc(s_idx, 1)
                    have_idx(far.c + 1 if const else None)
                    for j in range(S):
                        pool.indirect_dma_start(out=kv[u][:, j, TD:TD + 2 * PROJ], out_offset=None, in_=kv_d,
                                                in_offset=bass.IndirectOffsetOnAxis(ap=idx[u][:, j:j + 1], axis=0)).then_inc(s_kv[u], 16)

            each_step(pool, step, ahead=1)

        @block.scalar
        def _(act):
            act.wait_ge(s_set, 1)

            def step(old, last, it, nxt, far):
                if old.exists():
                    u = old.u
                    act.wait_ge(s_z, old.n + 1)
                    nc.scalar.activation(zpos[:, :, :], z[:, :, :], ACT.Relu).then_inc(s_zpos, 1)
                    weights = pay[u][:, :, 0:PAYW].rearrange("p s (h d) -> p s h d", h=HEADS)[:, :, :, 0]
                    act.wait_ge(s_zpos, old.n + 1)
                    nc.scalar.activation(weights[:, :, 0:HEADS - 1], zpos[:, :, 1:HEADS], ACT.Exp, scale=-SCALE)
                    nc.scalar.activation(weights[:, :, HEADS - 1:HEADS], zpos[:, :, 0:1], ACT.Exp, scale=-SCALE).then_inc(s_w, 1)
                    act.wait_ge(s_dm, old.n + 1)
                    nc.scalar.activation(alpha[u][:, 0:HEADS - 1], dm[u][:, 1:HEADS], ACT.Exp, scale=SCALE)
                    nc.scalar.activation(alpha[u][:, HEADS - 1:HEADS], dm[u][:, 0:1], ACT.Exp, scale=SCALE).then_inc(s_alpha, 1)
                if nxt.exists():
                    u = nxt.u
                    act.wait_ge(s_ot, nxt.n + 1)
                    wait(act, s_mg, nxt.count(-3))
                    nc.scalar.copy(oht[u][:, :, :], psOT).then_inc(s_oht, 1)
                if far.exists():
                    act.wait_ge(s_ph, far.n * 2 + 2)
                    nc.scalar.activation(fr[far.u][:, :, :, :], ph[far.u][:, :, :, :], ACT.Identity, bias=consts[:, 1:2]).then_inc(s_whole, 1)
                if nxt.exists():
                    u = nxt.u
                    wait(act, s_b, nxt.count(-3))
                    nc.scalar.activation(noht[u][:, :, :], psOT, ACT.Identity, bias=consts[:, 2:3], scale=BIG).then_inc(s_noht, 1)
                if last.exists():
                    u = last.u
                    act.wait_ge(s_oh, last.n + 1)
                    wait(act, s_agg, last.count(-1))
                    nc.scalar.copy(oh[u % 2][:, :, :], ohb[u][:, :, :]).then_inc(s_oh32, 1)
                if nxt.exists():
                    u = nxt.u
                    act.wait_ge(s_fr, nxt.n + 1)
                    wait(act, s_pay, nxt.count(-3))
                    wait(act, s_agg, nxt.count(-3))
                    turn = -6.283185
                    kv_ends = kv[u][:, :, :]
                    nc.scalar.activation(kv_ends[:, :, 0:TD], fr[u][:, :, 0, :], ACT.Sin, scale=turn).then_inc(s_sin, 1)
                    nc.scalar.activation(kv_ends[:, :, ROW - TD:ROW], fr[u][:, :, 0, :], ACT.Sin, scale=turn).then_inc(s_sin, 1)
                    nc.scalar.activation(eq[u % 2][:, :, 0:TD], fr[u][:, :, 1, :], ACT.Sin, scale=turn).then_inc(s_sin, 1)
                    nc.scalar.activation(pay[u][:, :, PAYW:ACCW], fr[u][:, :, 2, :], ACT.Sin, scale=turn).then_inc(s_sin, 1)
                if it.exists():
                    act.wait_ge(s_x, it.n + 1)
                    wait(act, s_b, it.n)
                    nc.scalar.copy(attT[:, :, :], psX).then_inc(s_attT, 1)

            each_step(act, step)

        @block.vector
        def _(dve):
            link = Chain(dve, s_dve)
            for u in range(2):
                nc.vector.memset(eq[u][:, :, TD:DK], 0.0)
            nc.vector.memset(mstate[:, :, :], -BIG)
            nc.vector.memset(acc[:, :, :], 0.0)
            link(nc.vector.tensor_reduce(selc[:, :], ident[0:PARTS * HEADS, 0:PARTS * HEADS].rearrange("k (a h) -> k h a", a=PARTS), AX.X, ALU.add))
            nc.vector.tensor_copy(sel[:, :, :], bc(selc[:, :], 2, P))
            dve.wait_ge(s_wt, 32)
            turn = float(1 / (2 * np.pi))
            link(nc.vector.tensor_scalar(wt[:, 0, :], wt[:, 0, :], turn, None, ALU.mult))
            link(nc.vector.tensor_scalar(wt[:, 1, :], wt[:, 1, :], turn, 0.25, ALU.mult, ALU.add))
            link(nc.vector.tensor_copy(qparts[:, :, 0, :], qtab[:, :, :]))
            link(nc.vector.tensor_tensor(qrest[:, :, :], qtab[:, :, :], qparts[:, :, 0, :], ALU.subtract))
            link(nc.vector.tensor_copy(qparts[:, :, 1, :], qrest[:, :, :]))
            nc.vector.tensor_tensor(qparts[:, :, 2, :], qrest[:, :, :], qparts[:, :, 1, :], ALU.subtract).then_inc(s_set, 1)

            def step(old, last, it, nxt, far):
                link.until(link.n)
                if it.exists():
                    u = it.u
                    dve.wait_ge(s_qg, it.n + 1)
                    dve.wait_ge(s_sin, it.n * 4 + 4)
                    have_qs = link.post(nc.vector.tensor_tensor(qs[:, :, :], qg, eq[u % 2][:, :, :], ALU.add))
                if far.exists():
                    v = far.u
                    dve.wait_ge(s_rec[v], far.j * 16 + 16)
                    wait(dve, s_oh32, far.count(-3))
                    nc.vector.scalar_tensor_tensor(ohb[v][:, :, :], bc(iota[:, :], 1, S), item_base[:, bass.ds(far.n, 1)],
                                                   bc(rec[v][:, :, 0], 2, P), ALU.add, ALU.is_equal).then_inc(s_oh, 1)
                if old.exists():
                    dve.wait_ge(s_mg, old.n + 1)
                    nc.vector.tensor_tensor(z[:, :, :], mg, att[old.u][:, :, :], ALU.subtract).then_inc(s_z, 1)
                if it.exists():
                    dve.wait_ge(s_kv[u], it.j * 64 + 64)
                    link.until(have_qs)
                    have_prod = link.post(nc.vector.tensor_tensor(prod[:, :, :, :], kv[u][:, :, 0:VW].rearrange("p s (h d) -> p s h d", h=HEADS),
                                                                  bc(qs[:, :, :], 2, HEADS), ALU.mult))
                    link.until(have_prod)
                    nc.vector.tensor_reduce(att[u][:, :, :], prod[:, :, :, :], AX.X, ALU.add).then_inc(s_att, 1)
                if old.exists():
                    u = old.u
                    dve.wait_ge(s_w, old.n + 1)
                    rows = pay[u][:, :, 0:PAYW].rearrange("p s (h d) -> p s h d", h=HEADS)
                    nc.vector.tensor_tensor(rows[:, :, :, 1:DK + 1], kv[u][:, :, VW:2 * VW].rearrange("p s (h d) -> p s h d", h=HEADS),
                                            rows[:, :, :, 0:1].broadcast_to([P, S, HEADS, DK]), ALU.mult).then_inc(s_pay, 1)
                if last.exists():
                    u = last.u
                    hi, mid, lo = (mparts[u][:, k, :] for k in range(PARTS))
                    dve.wait_ge(s_b, last.n + 1)
                    have_top = link.post(nc.vector.tensor_reduce(top[:, :], psB[:, :, :, :].rearrange("p h s n -> p h (s n)"), AX.X, ALU.max))
                    slot_last = dve.value_load(item_blk[0:1, bass.ds(last.n, 1)], min_val=0, max_val=SLOTS - 1)
                    m = mstate[:, bass.ds(slot_last, 1), :].rearrange("p b h -> p (b h)")
                if old.exists():
                    slot_old = dve.value_load(item_blk[0:1, bass.ds(old.n, 1)], min_val=0, max_val=SLOTS - 1)
                if far.exists():
                    dve.wait_ge(s_whole, far.n + 1)
                    nc.vector.scalar_tensor_tensor(fr[v][:, :, :, :], fr[v][:, :, :, :], -MAGIC, ph[v][:, :, :, :], ALU.add, ALU.subtract).then_inc(s_fr, 1)
                if last.exists():
                    link.until(have_top)
                    have_new = link.post(nc.vector.tensor_tensor(mnew[u][:, :], m, top[:, :], ALU.max))
                if old.exists():
                    row = acc[:, bass.ds(slot_old, 1), :].rearrange("p b w -> p (b w)")
                    heads = row[:, 0:PAYW].rearrange("p (h d) -> p h d", h=HEADS)
                    dve.wait_ge(s_alpha, old.n + 1)
                    wait(dve, s_acc, old.n)
                    have_scaled = link.post(nc.vector.tensor_tensor(heads, heads, bc(alpha[old.u][:, :], 2, DK + 1), ALU.mult))
                if last.exists():
                    link.until(have_new)
                    have_hi = link.post(nc.vector.tensor_copy(hi, mnew[u][:, :]))
                    nc.vector.tensor_tensor(dm[u][:, :], m, mnew[u][:, :], ALU.subtract).then_inc(s_dm, 1)
                    link.until(have_hi)
                    have_rest = link.post(nc.vector.tensor_tensor(mrest[:, :], mnew[u][:, :], hi, ALU.subtract))
                    dve.wait_ge(s_dm, last.n + 1)
                    link.post(nc.vector.tensor_tensor(m, m, top[:, :], ALU.max))
                    link.until(have_rest)
                    have_mid = link.post(nc.vector.tensor_copy(mid, mrest[:, :]))
                if old.exists():
                    link.until(have_scaled)
                    dve.wait_ge(s_agg, old.n + 1)
                    nc.vector.tensor_tensor(row, row, psA[:, 0:ACCW], ALU.add).then_inc(s_acc, 1)
                if last.exists():
                    link.until(have_mid)
                    nc.vector.tensor_tensor(lo, mrest[:, :], mid, ALU.subtract).then_inc(s_m, 1)

            each_step(dve, step, link, 9)
            dve.wait_ge(s_acc, NI)
            heads = acc[:, :, 0:PAYW].rearrange("p b (h d) -> p b h d", h=HEADS)
            link(nc.vector.tensor_scalar(den[:, :, :], heads[:, :, :, 0], 1e-16, None, ALU.add))
            link(nc.vector.reciprocal(den[:, :, :], den[:, :, :]))
            link(nc.vector.tensor_tensor(heads[:, :, :, 1:DK + 1], heads[:, :, :, 1:DK + 1], bc(den[:, :, :], 3, DK), ALU.mult))
            link(nc.vector.tensor_tensor(heads[:, 0:NB, :, 1:DK + 1], heads[:, 0:NB, :, 1:DK + 1], heads[:, NB:SLOTS, :, 1:DK + 1], ALU.add))
            link(nc.vector.tensor_tensor(acc[:, 0:NB, PAYW:ACCW], acc[:, 0:NB, PAYW:ACCW], acc[:, NB:SLOTS, PAYW:ACCW], ALU.add))
            for h in range(HEADS):
                link(nc.vector.tensor_copy(acc[:, NB:SLOTS, h * DK:h * DK + DK], heads[:, 0:NB, h, 1:DK + 1]))
            link(nc.vector.tensor_copy(acc[:, NB:SLOTS, VW:D], acc[:, 0:NB, PAYW:ACCW]))
            nc.vector.tensor_copy(acc[:, 0:NB, 0:D], acc[:, NB:SLOTS, 0:D]).then_inc(s_sum, 2)

        @block.tensor
        def _(pe):
            def step(old, last, it, nxt, far):
                if last.exists():
                    u = last.u
                    pe.wait_ge(s_attT, last.n + 1)
                    pe.wait_ge(s_noht, last.n + 1)
                    wait(pe, s_m, last.n)
                    for h in range(HEADS):
                        nc.tensor.matmul(psB[:, h, :, :], sel[:, h, :], attT[:, :, :], start=True, stop=False)
                        mm = nc.tensor.matmul(psB[:, h, :, :], identb[:, :], noht[u][:, :, :], start=False, stop=True)
                    mm.then_inc(s_b, 1)
                if nxt.exists():
                    u = nxt.u
                    blk = pe.value_load(item_qblk[0:1, bass.ds(nxt.n, 1)], min_val=0, max_val=NB - 1)
                    q = qparts[:, bass.ds(blk, 1), :, :].rearrange("p b k d -> p (b k) d")
                    pe.wait_ge(s_oht, nxt.n + 1)
                    wait(pe, s_att, nxt.n)
                    for j in range(S):
                        for k in range(PARTS):
                            mm = nc.tensor.matmul(qg[:, j, :], oht[u][:, j, :], q[:, k, :], start=k == 0, stop=k == PARTS - 1)
                    mm.then_inc(s_qg, 1)
                if old.exists():
                    u = old.u
                    pe.wait_ge(s_pay, old.n + 1)
                    pe.wait_ge(s_oh32, old.n + 1)
                    wait(pe, s_acc, old.n)
                    for j in range(S):
                        mm = nc.tensor.matmul(psA[:, 0:ACCW], oh[u % 2][:, j, :], pay[u][:, j, :], start=j == 0, stop=j == S - 1)
                    mm.then_inc(s_agg, 1)
                if it.exists():
                    u = it.u
                    pe.wait_ge(s_part, it.n * 4 + 4)
                    wait(pe, s_attT, it.n)
                    for j in range(S):
                        mm = nc.tensor.transpose(psX[:, j, :], parts[u][:, j, :], identb[:, :])
                    mm.then_inc(s_x, 1)
                if far.exists():
                    u = far.u
                    pe.wait_ge(s_oh, far.n + 1)
                    wait(pe, s_noht, far.n)
                    for j in range(S):
                        mm = nc.tensor.transpose(psOT[:, j, :], ohb[u][:, j, :], identb[:, :])
                    mm.then_inc(s_ot, 1)
                if last.exists():
                    u = last.u
                    pe.wait_ge(s_m, last.n + 1)
                    wait(pe, s_acc, last.n)
                    for j in range(S):
                        for k in range(PARTS):
                            mm = nc.tensor.matmul(mg[:, j, :], oht[u][:, j, :], mparts[u][:, k, :], start=k == 0, stop=k == PARTS - 1)
                    mm.then_inc(s_mg, 1)

            pe.wait_ge(s_set, 1)
            each_step(pe, step)


def each_tile(eng, count, body):
    for t in range(2):
        body(t, t, 0)
    with eng.Fori(0, count // 2 - 2) as g:
        for i in range(2):
            body(g * 2 + (2 + i), i, g + 1)
    for i in range(2):
        body(count - 2 + i, i, count // 2 - 1)


def places(nc, link, hot, total, run, within, tiles, own, past, numbers, place, tile_k, tile_ki):
    groups, kinds = total.shape[1], total.shape[2]
    count, first, end = tiles
    cur, reach, n = total, 1, 0
    while reach < groups:
        nc.vector.tensor_copy(run[n][:, 0:reach, :], cur[:, 0:reach, :])
        link(nc.vector.tensor_tensor(run[n][:, reach:, :], cur[:, reach:, :], cur[:, 0:groups - reach, :], ALU.add))
        cur, reach, n = run[n], reach * 2, 1 - n
    link(nc.vector.tensor_scalar(count, cur[:, groups - 1, :], (P - 1) / 2, 1.0 / P, ALU.add, ALU.mult))
    link(nc.vector.tensor_scalar(count, count, MAGIC, None, ALU.add))
    link(nc.vector.tensor_scalar(count, count, -MAGIC, None, ALU.add))
    link(nc.vector.tensor_copy(end, count))
    for e in range(1, kinds):
        link(nc.vector.tensor_tensor(end[:, e:e + 1], end[:, e:e + 1], end[:, e - 1:e], ALU.add))
    link(nc.vector.tensor_tensor(first, end, count, ALU.subtract))
    link(nc.vector.tensor_scalar(first, first, float(P), None, ALU.mult))
    link(nc.vector.tensor_tensor(cur, cur, total, ALU.subtract))
    link(nc.vector.tensor_tensor(cur, cur, bc(first, 1, groups), ALU.add))
    part = groups // len(within)
    for c, w in enumerate(within):
        half = cur[:, c * part:(c + 1) * part, :]
        link(nc.vector.tensor_tensor(half, half, w.rearrange("p (b e) -> p b e", e=kinds), ALU.add))
    link(nc.vector.tensor_tensor(cur, cur, hot, ALU.mult))
    link(nc.vector.tensor_reduce(own, cur, AX.X, ALU.add))
    link(nc.vector.tensor_copy(place, own))
    link(nc.vector.tensor_tensor(past, bc(numbers, 2, kinds), bc(end, 1, numbers.shape[1]), ALU.is_ge))
    link(nc.vector.tensor_reduce(tile_k, past, AX.X, ALU.add))
    link(nc.vector.tensor_scalar(tile_k, tile_k, float(kinds - 1), None, ALU.min))
    link(nc.vector.tensor_copy(tile_ki, tile_k))


def project(nc, a, agg_d, mix_d, x1_d, typed_d, typed_out_d, sent_d, consts, ident, iota, types, xn, share, place, tile_e, tile_ei):
    with ExitStack() as ctx:
        def sb(name, shape, dt=F32):
            return ctx.enter_context(nc.sbuf_tensor(name, shape, dt))

        def ps(name, shape, dt=F32):
            return ctx.enter_context(nc.psum_tensor(name, shape, dt))

        def sem(name):
            return ctx.enter_context(nc.semaphore(name))

        x1 = sb("x1", [P, NB, D])
        mix = sb("mix", [P, NB, D])
        WA = sb("WA", [P, 2, TYPES, D])
        raw = sb("raw", [P, TYPES, D])
        agg = sb("agg", [P, NB, D])
        typ = sb("typ", [P, NB])
        typ_i = sb("typ_i", [P, NB], I32)
        which = [sb(f"which_t{i}", [TYPES, P]) for i in range(2)]
        number = sb("number_t", [TYPES, P])
        row = [sb(f"row_t{i}", [P, D]) for i in range(2)]
        rowT = [sb(f"rowT_t{i}", [P, 2, P]) for i in range(2)]
        ty = [sb(f"ty{i}", [P, D]) for i in range(2)]
        tplace = sb("tplace", [P, NB], I32)
        tile_t = sb("tile_t", [P, TT])
        tile_ti = sb("tile_ti", [P, TT], I32)
        rows = sb("rows", [TYPES, 3, D])
        one_t = raw[:, :, :].rearrange("p t d -> p (t d)")[0:TYPES, 0:NP]
        pidx = sb("pidx2", [P, 1])
        pidx_i = sb("pidx2_i", [P, 1], I32)
        y = sb("y", [P, D])
        stat = sb("stat3", [P, 3, NB])
        x2T = WA[:, :, :, :].rearrange("p a b c -> p (a b c)")[:, 0:2 * NP].rearrange("p (c n) -> p c n", c=2)
        gw = sb("gw", [P, 2, EXPERTS])
        gb = sb("gb", [1, EXPERTS])
        ones1 = sb("ones1", [1, P])
        lg = sb("lg", [P, NB, EXPERTS])
        l2 = sb("l2", [P, NB, EXPERTS])
        t1 = sb("t1", [P, NB, EXPERTS])
        ex_i = sb("ex_i", [P, EXPERTS], I32)
        ex = sb("ex", [P, EXPERTS])
        gs = sb("gs", [P, 8, NB])
        hot = sb("hot", [P, TOP, NB, EXPERTS])
        before = sb("before2", [P, P])
        ones = sb("ones2", [P, P])
        counts = sb("counts", [P, 3, TOP * NB, EXPERTS])
        total, run = counts[:, 0, :, :], [counts[:, 1, :, :], counts[:, 2, :, :]]
        tiles = [sb(f"tiles{i}", [P, max(EXPERTS, TYPES)]) for i in range(3)]
        own = sb("own", [P, TOP * NB])
        past = counts[:, :, :, :].rearrange("p a n e -> p (a n e)")
        zero = sb("zero", [P, D])

        def by_type(ap):
            return ap.rearrange("p n e -> p (n e)")[:, 0:NB * TYPES].rearrange("p (b t) -> p b t", t=TYPES)

        hot_t = by_type(hot[:, :, :, :].rearrange("p c b e -> p (c b) e"))

        psT = ps("psT3", [P, 4, P])[:, 0:2, :]
        psY = [ps(f"psY{i}", [P, 512]) for i in range(2)]
        psL = ps("psL", [P, 512])
        psP = [ps(f"psP{i}", [P, 512]) for i in range(2)]
        psN = [ps(f"psN{i}", [P, 512]) for i in range(2)]

        names = ("s_x s_mixl s_wa s_rows s_wsum s_iota s_dve3 s_mm s_var s_std s_stage s_tT s_tTs s_lg "
                 "s_g s_small s_ps s_x1 s_agg s_typ s_hot s_pst s_place s_turned s_rowT s_which s_ycopy s_back "
                 "s_norm s_gb s_one s_out s_ones").split()
        q = {n: sem(n + "_f") for n in names}
        s_row = [sem(f"s_row_f{i}") for i in range(2)]
        s_store = [sem(f"s_store_f{i}") for i in range(2)]
        s_raw = [sem(f"s_raw_f{i}") for i in range(2)]
        block = ctx.enter_context(nc.Block())

        @block.sync
        def _(sp):
            wa = a["L0_gnn_Wa"]
            sp.wait_ge(q["s_ones"], 1)
            node_type = a["node_type_19"]
            sp.dma_start(typ_i[:, 0:NB - 1], node_type[0:(NB - 1) * P].rearrange("(b p) -> p b", p=P), allow_slow_non_contiguous=True).then_inc(q["s_typ"], 16)
            sp.dma_start(typ_i[0:LAST, NB - 1:NB], node_type[(NB - 1) * P:N].rearrange("(p o) -> p o", o=1)).then_inc(q["s_typ"], 16)
            sp.dma_start(agg[:, :, :], agg_d.rearrange("(b p) d -> p b d", p=P)).then_inc(q["s_agg"], 16)
            for kc in range(2):
                sp.dma_start(WA[:, kc, :, :], wa[:, kc * P:kc * P + P, :].rearrange("t i o -> i t o")).then_inc(q["s_wa"], 16)
            sp.dma_start(raw[:, :, :], wa[:, D:D + P, :].rearrange("t i o -> i t o")).then_inc(s_raw[0], 16)
            for n, w in enumerate(("ba", "gamma", "beta")):
                sp.dma_start(rows[:, n, :], a["L0_gnn_" + w]).then_inc(q["s_rows"], 16)
            sp.dma_start(x1[:, 0:NB - 1, :], a["x"][0:(NB - 1) * P, :].rearrange("(b p) d -> p b d", p=P)).then_inc(q["s_x"], 16)
            sp.dma_start(x1[0:LAST, NB - 1, :], a["x"][(NB - 1) * P:N, :]).then_inc(q["s_x"], 16)
            sp.dma_start(mix[:, :, :], mix_d.rearrange("(b p) d -> p b d", p=P)).then_inc(q["s_mixl"], 16)
            sp.dma_start(gw[:, :, :], a["L0_ffn_gate_w"].rearrange("(c p) e -> p c e", p=P)).then_inc(q["s_small"], 16)
            sp.dma_start(gb[:, :], a["L0_ffn_gate_b"].rearrange("(o e) -> o e", o=1)).then_inc(q["s_small"], 16)
            sp.dma_start(sent_d.rearrange("(t p) d -> p t d", p=P), bc(zero[:, :], 1, NT)).then_inc(q["s_out"], 16)
            sp.wait_ge(q["s_wsum"], 1)
            sp.dma_start(raw[:, :, :], wa[:, D + P:2 * D, :].rearrange("t i o -> i t o")).then_inc(s_raw[1], 16)

            sp.wait_ge(q["s_back"], 16 * NB)

            def load(t, i, turn):
                sp.lower_val(t * P * D * 4)
                wait(sp, q["s_turned"], t - 1)
                sp.dma_start(row[i][:, :], typed_d[bass.ds(t * P, P), :]).then_inc(s_row[i], 16)

            each_tile(sp, TT, load)
            sp.wait_ge(q["s_x1"], 1)
            sp.dma_start(x1_d.rearrange("(b p) d -> p b d", p=P), x1[:, :, :]).then_inc(q["s_out"], 16)
            sp.wait_ge(q["s_out"], 32)

        @block.gpsimd
        def _(pool):
            nc.gpsimd.iota(pidx_i[:, :], pattern=[[0, 1]], base=0, channel_multiplier=1).then_inc(q["s_iota"], 1)
            nc.gpsimd.iota(ex_i[:, :], pattern=[[1, EXPERTS]], base=0, channel_multiplier=0).then_inc(q["s_iota"], 1)
            pool.wait_ge(q["s_place"], 1)
            pool.wait_ge(q["s_agg"], 16)
            for b in range(NB):
                pool.indirect_dma_start(out=typed_d, out_offset=bass.IndirectOffsetOnAxis(ap=tplace[:, b:b + 1], axis=0),
                                        in_=agg[:, b, :], in_offset=None).then_inc(q["s_back"], 16)
            pool.wait_ge(q["s_back"], 16 * NB)
            for i in range(2):
                pool.wait_ge(s_store[i], 16 * (TT // 2))
            for b in range(NB):
                pool.indirect_dma_start(out=agg[:, b, :], out_offset=None, in_=typed_out_d,
                                        in_offset=bass.IndirectOffsetOnAxis(ap=tplace[:, b:b + 1], axis=0)).then_inc(q["s_back"], 16)

        @block.scalar
        def _(act):
            def store(t, i, turn):
                act.wait_ge(q["s_ycopy"], t + 1)
                act.dma_start(typed_out_d[bass.ds(t * P, P), :], ty[i][:, :]).then_inc(s_store[i], 16)

            each_tile(act, TT, store)
            act.wait_ge(q["s_var"], 1)
            nc.scalar.activation(stat[:, 2, :], stat[:, 1, :], ACT.Sqrt, bias=consts[:, 0:1], scale=1.0 / D).then_inc(q["s_std"], 1)
            act.wait_ge(q["s_var"], 2)
            nc.scalar.activation(stat[:, 2, :], stat[:, 1, :], ACT.Sqrt, bias=consts[:, 0:1], scale=1.0 / D).then_inc(q["s_std"], 1)
            turned = Tick(act, q["s_tT"], 1, 1, "turned2")
            with act.Fori(0, NB) as b:
                turned()
                nc.scalar.copy(x2T[:, :, bass.ds(b * P, P)], psT).then_inc(q["s_tTs"], 1)
            act.wait_ge(q["s_g"], 1)
            nc.scalar.activation(gs[:, 3, :], gs[:, 2, :], ACT.Exp).then_inc(q["s_g"], 1)

        @block.vector
        def _(dve):
            link = Chain(dve, q["s_dve3"])
            link(nc.vector.memset(ones1[:, :], 1.0))
            nc.vector.memset(ones[:, :], 1.0)
            nc.vector.memset(zero[:, :], 0.0)
            nc.vector.memset(typ_i[:, :], 0)
            nc.vector.memset(x1[:, NB - 1, :], 0.0).then_inc(q["s_ones"], 1)
            dve.wait_ge(q["s_iota"], 2)
            link(nc.vector.tensor_copy(pidx[:, :], pidx_i[:, :]))
            nc.vector.tensor_scalar(before[:, :], iota[:, :], pidx[:, :], None, ALU.is_gt)
            nc.vector.tensor_copy(ex[:, :], ex_i[:, :])
            nc.vector.tensor_copy(number[:, :], bc(pidx[0:TYPES, 0], 1, P))
            dve.wait_ge(q["s_typ"], 32)
            link(nc.vector.tensor_copy(typ[:, :], typ_i[:, :]))
            nc.vector.tensor_tensor(hot_t, bc(typ[:, :], 2, TYPES), bc(iota[:, 0:TYPES], 1, NB), ALU.is_equal).then_inc(q["s_hot"], 1)
            dve.wait_ge(q["s_pst"], 1)
            link(nc.vector.tensor_copy(by_type(total), psN[0][:, 0:NB * TYPES].rearrange("p (b t) -> p b t", t=TYPES)))
            places(nc, link, hot_t, by_type(total), [by_type(r) for r in run], [psP[0][:, 0:NB * TYPES]],
                   [t[:, 0:TYPES] for t in tiles], own[:, 0:NB], past[:, 0:TT * TYPES].rearrange("p (n t) -> p n t", t=TYPES),
                   iota[:, 0:TT], tplace[:, :], tile_t[:, :], tile_ti[:, :])
            nc.vector.memset(y[:, 0:1], 0.0).then_inc(q["s_place"], 1)
            dve.wait_ge(q["s_wa"], 32)
            for kc in range(2):
                dve.wait_ge(s_raw[kc], 16)
                nc.vector.tensor_tensor(WA[:, kc, :, :], WA[:, kc, :, :], raw[:, :, :], ALU.add).then_inc(q["s_wsum"], 1)
            dve.wait_ge(q["s_x"], 32)
            dve.wait_ge(q["s_mixl"], 16)
            link(nc.vector.tensor_tensor(x1[:, :, :], x1[:, :, :], mix[:, :, :], ALU.add))
            stored = [Tick(dve, s_store[i], 16, 16, f"stored_t{i}") for i in range(2)]

            def prepare_tile(t, i):
                nc.vector.tensor_scalar(which[i][:, :], number[:, :], tile_t[0:TYPES, bass.ds(t, 1)], None, ALU.is_equal).then_inc(q["s_which"], 1)
                dve.wait_ge(q["s_turned"], t + 1)
                nc.vector.tensor_scalar(rowT[i][:, :, :], psT, 0.0, None, ALU.add).then_inc(q["s_rowT"], 1)

            def step(t, i, turn):
                if not isinstance(t, int) or t + 1 < TT:
                    prepare_tile(t + 1, 1 - i)
                dve.wait_ge(q["s_mm"], t + 1)
                if not isinstance(t, int) or t >= 2:
                    stored[i](16 * turn if isinstance(t, int) else None)
                nc.vector.tensor_scalar(ty[i][:, :], psY[i][:, 0:D], 0.0, None, ALU.add).then_inc(q["s_ycopy"], 1)

            prepare_tile(0, 0)
            each_tile(dve, TT, step)
            nc.vector.tensor_scalar(one_t, types[0:TYPES, :], pidx[0:TYPES, :], None, ALU.is_equal).then_inc(q["s_one"], 1)
            dve.wait_ge(q["s_back"], 32 * NB)
            link(nc.vector.tensor_tensor(agg[:, :, :], agg[:, :, :], xn[:, :, :], ALU.add))
            layer_norm(nc, link, None, agg[:, :, :], mix[:, :, :], agg[:, :, :], stat[:, 0, :], stat[:, 1, :], stat[:, 2, :],
                       q["s_var"], q["s_std"], 1)
            for b in range(NB):
                dve.wait_ge(q["s_gb"], b + 1)
                link(nc.vector.tensor_tensor(agg[:, b, :], agg[:, b, :], psY[b % 2][:, 0:D], ALU.mult))
                nc.vector.tensor_tensor(agg[:, b, :], agg[:, b, :], psY[b % 2][:, D:2 * D], ALU.add).then_inc(q["s_norm"], 1)
            dve.wait_ge(q["s_norm"], NB)
            link(nc.vector.tensor_tensor(x1[:, :, :], x1[:, :, :], agg[:, :, :], ALU.add))
            nc.vector.memset(y[:, 0:1], 0.0).then_inc(q["s_x1"], 1)
            layer_norm(nc, link, None, x1[:, :, :], mix[:, :, :], xn[:, :, :], stat[:, 0, :], stat[:, 1, :], stat[:, 2, :],
                       q["s_var"], q["s_std"], 2)
            with dve.Fori(0, NB) as b:
                dve.wait_ge(q["s_tT"], b)
                nc.vector.tensor_copy(y[:, :], xn[:, bass.ds(b, 1), :].rearrange("p b d -> p (b d)")).then_inc(q["s_stage"], 1)
            dve.wait_ge(q["s_lg"], 1)
            link(nc.vector.tensor_copy(lg[:, :, :], psL[:, 0:NB * EXPERTS].rearrange("p (b e) -> p b e", e=EXPERTS)))
            exb = bc(ex[:, :], 1, NB)

            def first_best(src, best, number, hot):
                link(nc.vector.tensor_reduce(best, src, AX.X, ALU.max))
                link(nc.vector.tensor_tensor(t1[:, :, :], src, bc(best, 2, EXPERTS), ALU.is_equal))
                link(nc.vector.tensor_scalar(t1[:, :, :], t1[:, :, :], -100.0, 100.0, ALU.mult, ALU.add))
                link(nc.vector.tensor_tensor(t1[:, :, :], t1[:, :, :], exb, ALU.add))
                link(nc.vector.tensor_reduce(number, t1[:, :, :], AX.X, ALU.min))
                link(nc.vector.tensor_tensor(hot, exb, bc(number, 2, EXPERTS), ALU.is_equal))
            first_best(lg[:, :, :], gs[:, 0, :], gs[:, 1, :], hot[:, 0, :, :])
            link(nc.vector.scalar_tensor_tensor(l2[:, :, :], hot[:, 0, :, :], -BIG, lg[:, :, :], ALU.mult, ALU.add))
            first_best(l2[:, :, :], gs[:, 4, :], gs[:, 5, :], hot[:, 1, :, :])
            nc.vector.tensor_tensor(gs[:, 2, :], gs[:, 4, :], gs[:, 0, :], ALU.subtract).then_inc(q["s_g"], 1)
            dve.wait_ge(q["s_g"], 2)
            link(nc.vector.tensor_scalar(gs[:, 6, :], gs[:, 3, :], 1.0, None, ALU.add))
            link(nc.vector.reciprocal(share[:, 0, :], gs[:, 6, :]))
            link(nc.vector.tensor_tensor(share[:, 1, :], gs[:, 3, :], share[:, 0, :], ALU.mult))
            dve.wait_ge(q["s_ps"], 1)
            for c in range(TOP):
                link(nc.vector.tensor_copy(total[:, c * NB:(c + 1) * NB, :], psN[c][:, 0:NB * EXPERTS].rearrange("p (b e) -> p b e", e=EXPERTS)))
            places(nc, link, hot[:, :, :, :].rearrange("p c b e -> p (c b) e"), total, run,
                   [psP[c][:, 0:NB * EXPERTS] for c in range(TOP)], [t[:, 0:EXPERTS] for t in tiles], own[:, :], past[:, 0:NT * EXPERTS].rearrange("p (n e) -> p n e", e=EXPERTS),
                   iota[:, 0:NT], place[:, :, :].rearrange("p c b -> p (c b)"), tile_e[:, :], tile_ei[:, :])

        @block.tensor
        def _(pe):
            pe.wait_ge(q["s_hot"], 1)
            nc.tensor.matmul(psP[0][:, 0:NB * TYPES], before[:, :], hot_t.rearrange("p b t -> p (b t)"), start=True, stop=True)
            nc.tensor.matmul(psN[0][:, 0:NB * TYPES], ones[:, :], hot_t.rearrange("p b t -> p (b t)"), start=True, stop=True).then_inc(q["s_pst"], 1)
            pe.wait_ge(q["s_wsum"], 2)
            pe.wait_ge(q["s_rows"], 48)

            def turn_rows(t, i, turn):
                pe.wait_ge(s_row[i], turn * 16 + 16)
                wait(pe, q["s_rowT"], t)
                nc.tensor.transpose(psT[:, 0, :], row[i][:, 0:P], ident[:, :])
                nc.tensor.transpose(psT[:, 1, :], row[i][:, P:D], ident[:, :]).then_inc(q["s_turned"], 1)

            def step(t, i, turn):
                if not isinstance(t, int) or t + 1 < TT:
                    turn_rows(t + 1, 1 - i, turn + i)
                kind = pe.value_load(tile_ti[0:1, bass.ds(t, 1)], min_val=0, max_val=TYPES - 1)
                pe.wait_ge(q["s_which"], t + 1)
                wait(pe, q["s_ycopy"], t - 1)
                nc.tensor.matmul(psY[i][:, 0:D], which[i][:, :], rows[:, 0, :], start=True, stop=False)
                pe.wait_ge(q["s_rowT"], t + 1)
                for c in range(2):
                    mm = nc.tensor.matmul(psY[i][:, 0:D], rowT[i][:, c, :], WA[:, c, bass.ds(kind, 1), :].rearrange("p t d -> p (t d)"), start=False, stop=c == 1)
                mm.then_inc(q["s_mm"], 1)

            turn_rows(0, 0, 0)
            each_tile(pe, TT, step)
            pe.wait_ge(q["s_one"], 1)
            pe.wait_ge(q["s_ycopy"], TT)
            for b in range(NB):
                wait(pe, q["s_norm"], b - 1)
                nc.tensor.matmul(psY[b % 2][:, :], one_t[:, b * P:b * P + P], rows[:, 1:3, :].rearrange("t a d -> t (a d)"), start=True, stop=True).then_inc(q["s_gb"], 1)
            with pe.Fori(0, NB) as b:
                pe.wait_ge(q["s_stage"], b + 1)
                pe.wait_ge(q["s_tTs"], b)
                nc.tensor.transpose(psT[:, 0, :], y[:, 0:P], ident[:, :])
                nc.tensor.transpose(psT[:, 1, :], y[:, P:D], ident[:, :]).then_inc(q["s_tT"], 1)
            pe.wait_ge(q["s_tTs"], NB)
            pe.wait_ge(q["s_small"], 32)
            for b in range(NB):
                o = psL[:, b * EXPERTS:(b + 1) * EXPERTS]
                for c in range(2):
                    nc.tensor.matmul(o, x2T[:, c, b * P:b * P + P], gw[:, c, :], start=c == 0, stop=False)
                mm = nc.tensor.matmul(o, ones1[:, :], gb[:, :], start=False, stop=True)
            mm.then_inc(q["s_lg"], 1)
            pe.wait_ge(q["s_g"], 1)
            for c in range(TOP):
                rows_c = hot[:, c, :, :].rearrange("p b e -> p (b e)")
                nc.tensor.matmul(psP[c][:, 0:NB * EXPERTS], before[:, :], rows_c, start=True, stop=True)
                mm = nc.tensor.matmul(psN[c][:, 0:NB * EXPERTS], ones[:, :], rows_c, start=True, stop=True)
            mm.then_inc(q["s_ps"], 1)


def experts(nc, a, x1_d, sent_d, back_d, consts, ident, xn, share, place, tile_e, tile_ei, out):
    with ExitStack() as ctx:
        def sb(name, shape, dt=F32):
            return ctx.enter_context(nc.sbuf_tensor(name, shape, dt))

        def ps(name, shape, dt=F32):
            return ctx.enter_context(nc.psum_tensor(name, shape, dt))

        def sem(name):
            return ctx.enter_context(nc.semaphore(name + "_e"))

        def two(name, shape):
            return [sb(f"{name}{i}", shape) for i in range(2)]

        W1 = sb("W1", [P, EXPERTS, 2, FF])
        W2 = sb("W2", [P, EXPERTS, FC, D])
        b1 = sb("b1", [EXPERTS, FF])
        b2 = sb("b2", [EXPERTS, D])
        number = sb("number", [P, P])
        number_i = sb("number_i", [P, P], I32)
        which = two("which", [EXPERTS, P])
        row = two("row", [P, D])
        rowT = two("rowT", [P, 2, P])
        h = two("h", [P, FC, P])
        hT = two("hT", [P, FC, P])
        y = two("y", [P, D])
        stat = sb("stat4", [P, 3, NB])
        gamma = sb("gamma", [P, D])
        beta = sb("beta", [P, D])
        back = W1[:, :, :, :].rearrange("p e c f -> p (e c f)")[:, 0:TOP * NB * D].rearrange("p (c b d) -> p c b d", c=TOP, b=NB)
        late = W2[:, :, :, :].rearrange("p e c f -> p (e c f)")[:, 0:2 * NB * D].rearrange("p (c b d) -> p c b d", c=2, b=NB)
        x1, sq = late[:, 0, :, :], late[:, 1, :, :]

        psT = ps("psT4", [P, 4, P])[:, 0:2, :]
        psH = [ps(f"psH{i}", [P, FC, P]) for i in range(2)]
        psHT = [ps(f"psHT{i}", [P, FC, P]) for i in range(2)]
        psY = [ps(f"psY4{i}", [P, 512]) for i in range(2)]

        s_w = sem("s_w")
        s_number = sem("s_number")
        s_sent = sem("s_sent")
        s_row = [sem(f"s_row{i}") for i in range(2)]
        s_turned = sem("s_turned")
        s_rowT = sem("s_rowT")
        s_which = sem("s_which")
        s_h = sem("s_h")
        s_relu = sem("s_relu")
        s_ht = sem("s_ht")
        s_hT = sem("s_hT")
        s_y = sem("s_y")
        s_ycopy = sem("s_ycopy")
        s_store = [sem(f"s_store{i}") for i in range(2)]
        s_back = [sem(f"s_back{c}") for c in range(TOP)]
        s_x1 = sem("s_x1")
        s_dve = sem("s_dve")
        s_var = sem("s_var")
        s_std = sem("s_std")
        s_final = sem("s_final")
        s_out = sem("s_out")
        block = ctx.enter_context(nc.Block())

        @block.sync
        def _(sp):
            sp.dma_start(b1[:, :], a["L0_ffn_b1"]).then_inc(s_w, 16)
            sp.dma_start(b2[:, :], a["L0_ffn_b2"]).then_inc(s_w, 16)
            sp.dma_start(gamma[:, :], a["L0_ffn_gamma"].rearrange("(o e) -> o e", o=1).broadcast_to([P, D])).then_inc(s_w, 16)
            sp.dma_start(beta[:, :], a["L0_ffn_beta"].rearrange("(o e) -> o e", o=1).broadcast_to([P, D])).then_inc(s_w, 16)
            for e in range(EXPERTS):
                sp.dma_start(W1[:, e, :, :], a["L0_ffn_w1"][e, :, :].rearrange("(c p) f -> p c f", p=P)).then_inc(s_w, 16)
                sp.dma_start(W2[:, e, :, :], a["L0_ffn_w2"][e, :, :].rearrange("(c p) f -> p c f", p=P)).then_inc(s_w, 16)
            sp.wait_ge(s_sent, 16 * TOP * NB)

            def load(t, i, turn):
                sp.lower_val(t * P * D * 4)
                wait(sp, s_turned, t - 1)
                sp.dma_start(row[i][:, :], sent_d[bass.ds(t * P, P), :]).then_inc(s_row[i], 16)

            each_tile(sp, NT, load)
            sp.wait_ge(s_y, NT)
            sp.dma_start(x1, x1_d.rearrange("(b p) d -> p b d", p=P)).then_inc(s_x1, 16)
            sp.wait_ge(s_x1, 16)
            sp.wait_ge(s_final, 1)
            sp.dma_start(out[0:(NB - 1) * P, :].rearrange("(b p) d -> p b d", p=P), x1[:, 0:NB - 1, :]).then_inc(s_out, 16)
            sp.dma_start(out[(NB - 1) * P:N, :], x1[0:LAST, NB - 1, :]).then_inc(s_out, 16)
            sp.wait_ge(s_out, 32)

        @block.gpsimd
        def _(pool):
            nc.gpsimd.iota(number_i[:, :], pattern=[[0, P]], base=0, channel_multiplier=1).then_inc(s_number, 1)
            for c in range(TOP):
                for b in range(NB):
                    pool.indirect_dma_start(out=sent_d, out_offset=bass.IndirectOffsetOnAxis(ap=place[:, c, b:b + 1], axis=0),
                                            in_=xn[:, b, :], in_offset=None).then_inc(s_sent, 16)
            pool.wait_ge(s_y, NT)
            for i in range(2):
                pool.wait_ge(s_store[i], 16 * (NT // 2))
            for c in range(TOP):
                for b in range(NB):
                    pool.indirect_dma_start(out=back[:, c, b, :], out_offset=None, in_=back_d,
                                            in_offset=bass.IndirectOffsetOnAxis(ap=place[:, c, b:b + 1], axis=0)).then_inc(s_back[c], 16)

        @block.scalar
        def _(act):
            def relu(i, t):
                act.wait_ge(s_h, t + 1)
                wait(act, s_ht, t - 1)
                nc.scalar.activation(h[i][:, :, :], psH[i][:, :, :], ACT.Relu).then_inc(s_relu, 1)

            def turn(i, t):
                act.wait_ge(s_ht, t + 1)
                wait(act, s_y, t - 1)
                nc.scalar.copy(hT[i][:, :, :], psHT[i][:, :, :]).then_inc(s_hT, 1)

            def store(i, t):
                act.wait_ge(s_ycopy, t + 1)
                act.dma_start(back_d[bass.ds(t * P, P), :], y[i][:, :]).then_inc(s_store[i], 16)

            def step(t, i):
                turn(i, t)
                relu(1 - i, t + 1)
                store(i, t)

            relu(0, 0)
            step(0, 0)
            step(1, 1)
            with act.Fori(0, NT // 2 - 2) as g:
                for i in range(2):
                    step(g * 2 + (2 + i), i)
            step(NT - 2, 0)
            turn(1, NT - 1)
            store(1, NT - 1)
            act.wait_ge(s_var, 1)
            nc.scalar.activation(stat[:, 2, :], stat[:, 1, :], ACT.Sqrt, bias=consts[:, 0:1], scale=1.0 / D).then_inc(s_std, 1)

        @block.vector
        def _(dve):
            link = Chain(dve, s_dve)
            dve.wait_ge(s_number, 1)
            link(nc.vector.tensor_copy(number[:, :], number_i[:, :]))
            stored = [Tick(dve, s_store[i], 16, 16, f"stored{i}") for i in range(2)]

            def prepare_tile(i, t):
                nc.vector.tensor_scalar(which[i][:, :], number[0:EXPERTS, :], tile_e[0:EXPERTS, bass.ds(t, 1)], None, ALU.is_equal).then_inc(s_which, 1)
                dve.wait_ge(s_turned, t + 1)
                nc.vector.tensor_scalar(rowT[i][:, :, :], psT, 0.0, None, ALU.add).then_inc(s_rowT, 1)

            def take(i, t, const):
                dve.wait_ge(s_y, t + 1)
                if not const or t >= 2:
                    stored[i](16 * (t // 2) if const else None)
                nc.vector.tensor_scalar(y[i][:, :], psY[i][:, 0:D], 0.0, None, ALU.add).then_inc(s_ycopy, 1)

            prepare_tile(0, 0)
            prepare_tile(1, 1)
            for t in range(2):
                take(t, t, True)
                prepare_tile(t, t + 2)
            with dve.Fori(0, NT // 2 - 2) as g:
                for i in range(2):
                    take(i, g * 2 + (2 + i), False)
                    prepare_tile(i, g * 2 + (4 + i))
            for i in range(2):
                take(i, NT - 2 + i, True)
            for c in range(TOP):
                dve.wait_ge(s_back[c], 16 * NB)
                for b in range(NB):
                    last = link.post(nc.vector.scalar_tensor_tensor(xn[:, b, :], back[:, c, b, :], share[:, c, b:b + 1], xn[:, b, :], ALU.mult, ALU.add))
                link.until(last)
            layer_norm(nc, link, None, xn[:, :, :], sq, xn[:, :, :], stat[:, 0, :], stat[:, 1, :], stat[:, 2, :], s_var, s_std, 1)
            link(nc.vector.tensor_tensor(xn[:, :, :], xn[:, :, :], bc(gamma[:, :], 1, NB), ALU.mult))
            link(nc.vector.tensor_tensor(xn[:, :, :], xn[:, :, :], bc(beta[:, :], 1, NB), ALU.add))
            dve.wait_ge(s_x1, 16)
            nc.vector.tensor_tensor(x1, x1, xn[:, :, :], ALU.add).then_inc(s_final, 1)

        @block.tensor
        def _(pe):
            def turn_rows(i, t, turn):
                pe.wait_ge(s_row[i], turn * 16 + 16)
                wait(pe, s_rowT, t)
                nc.tensor.transpose(psT[:, 0, :], row[i][:, 0:P], ident[:, :])
                nc.tensor.transpose(psT[:, 1, :], row[i][:, P:D], ident[:, :]).then_inc(s_turned, 1)

            def expert(t):
                return pe.value_load(tile_ei[0:1, bass.ds(t, 1)], min_val=0, max_val=EXPERTS - 1)

            def first_layer(i, t):
                e = expert(t)
                out_h = psH[i][:, :, :].rearrange("p c n -> p (c n)")
                pe.wait_ge(s_which, t + 1)
                wait(pe, s_relu, t - 1)
                nc.tensor.matmul(out_h, which[i][:, :], b1[:, :], start=True, stop=False)
                pe.wait_ge(s_rowT, t + 1)
                for c in range(2):
                    mm = nc.tensor.matmul(out_h, rowT[i][:, c, :], W1[:, bass.ds(e, 1), c, :].rearrange("p e f -> p (e f)"), start=False, stop=c == 1)
                mm.then_inc(s_h, 1)

            def turn_hidden(i, t):
                pe.wait_ge(s_relu, t + 1)
                wait(pe, s_hT, t - 1)
                for f in range(FC):
                    mm = nc.tensor.transpose(psHT[i][:, f, :], h[i][:, f, :], ident[:, :])
                mm.then_inc(s_ht, 1)

            def second_layer(i, t):
                e = expert(t)
                wait(pe, s_ycopy, t - 1)
                nc.tensor.matmul(psY[i][:, 0:D], which[i][:, :], b2[:, :], start=True, stop=False)
                pe.wait_ge(s_hT, t + 1)
                for f in range(FC):
                    mm = nc.tensor.matmul(psY[i][:, 0:D], hT[i][:, f, :], W2[:, bass.ds(e, 1), f, :].rearrange("p e d -> p (e d)"), start=False, stop=f == FC - 1)
                mm.then_inc(s_y, 1)

            def step(t, i, turn):
                turn_hidden(i, t)
                first_layer(1 - i, t + 1)
                second_layer(i, t)
                if turn is not None:
                    turn_rows(i, t + 2, turn)

            pe.wait_ge(s_w, 16 * (4 + 2 * EXPERTS))
            turn_rows(0, 0, 0)
            turn_rows(1, 1, 0)
            first_layer(0, 0)
            step(0, 0, 1)
            step(1, 1, 1)
            with pe.Fori(0, NT // 2 - 2) as g:
                for i in range(2):
                    step(g * 2 + (2 + i), i, g + 2)
            step(NT - 2, 0, None)
            turn_hidden(1, NT - 1)
            second_layer(1, NT - 1)


_INS = ("x", "src", "dst", "edge_attr_5", "node_type_19",
        "L0_gnn_Wk", "L0_gnn_bk", "L0_gnn_Wq", "L0_gnn_bq", "L0_gnn_Wv", "L0_gnn_bv", "L0_gnn_Wa", "L0_gnn_ba",
        "L0_gnn_gamma", "L0_gnn_beta", "L0_gnn_w_time", "L0_gnn_b_time",
        "L0_mix_wq", "L0_mix_bq", "L0_mix_wk", "L0_mix_bk", "L0_mix_wv", "L0_mix_bv", "L0_mix_wo", "L0_mix_bo",
        "L0_ffn_gate_w", "L0_ffn_gate_b", "L0_ffn_w1", "L0_ffn_b1", "L0_ffn_w2", "L0_ffn_b2", "L0_ffn_gamma", "L0_ffn_beta")


def kernel(**inputs):
    import numpy as _np
    import concourse.bacc as _bacc
    from concourse import mybir as _mybir
    from concourse.bass_utils import run_bass_kernel_spmd as _run

    nc = _bacc.Bacc("TRN2", target_bir_lowering=False, num_devices=1)
    arrays, args = {}, {}
    for name in _INS:
        v = _np.ascontiguousarray(inputs[name])
        arrays[f"in_{name}_dram"] = v
        args[name] = nc.dram_tensor(f"in_{name}_dram", v.shape, _mybir.dt.from_np(v.dtype), kind="ExternalInput").ap()
    out = nc.dram_tensor("out_0_dram", (N, D), F32, kind="ExternalOutput").ap()
    build(nc, args, out)
    r = _run(nc, [arrays], core_ids=[0])
    return r.results[0]["out_0_dram"]
```
